# Optimizing a Trainium2 kernel written in Bass

```python
import numpy as np
import jax
import jax.numpy as jnp

def _softmax(x, axis=-1):
    return jax.nn.softmax(x, axis=axis)

def _gelu(x):
    return jax.nn.gelu(x, approximate=True)

def _silu(x):
    return jax.nn.silu(x)

def _sigmoid(x):
    return jax.nn.sigmoid(x)

def _layernorm(x, axis=-1, eps=1e-05):
    m = jnp.mean(x, axis=axis, keepdims=True)
    v = jnp.var(x, axis=axis, keepdims=True)
    return (x - m) / jnp.sqrt(v + eps)

def _scatter_add(tgt, idx, src, axis=0):
    return tgt.at[idx].add(src)

def _segment_sum(src, seg, n):
    return jax.ops.segment_sum(src, seg, n)
kernel_name = 'mk_early_fusion_d2_tok_img1024_r4_c6eaac'

def setup_inputs(seed: int=0):
    np.random.seed(seed)
    _w = jnp.asarray

    def _rec_inputs():
        import jax
        import jax.numpy as jnp
        _rk = jax.random.key(seed)
        x = -0.00150118 + 0.499729 * jax.random.normal(jax.random.fold_in(_rk, 1), (4, 256, 64, 2), jnp.float32)
        txt = 0.00326275 + 2.8086 * jax.random.normal(jax.random.fold_in(_rk, 2), (4, 512, 256), jnp.float32)
        return (x, txt)
    x, txt = _rec_inputs()

    def _L0_tok_setup():
        import jax, jax.numpy as jnp
        import numpy as np
        import math
        H = 256
        N = 64
        CH = 1
        SEQ_L = 256
        key = jax.random.key(seed)
        k1, k2, k3, k4 = jax.random.split(key, 4)
        log_dt = jax.random.uniform(k1, (H,), dtype=jnp.float32, minval=math.log(0.001), maxval=math.log(0.1))
        inv_A_real = jnp.log(0.5 * jnp.ones((H, N), jnp.float32)) + 0.1 * jax.random.normal(k2, (H, N), dtype=jnp.float32)
        A_imag = jnp.broadcast_to(math.pi * jnp.arange(N, dtype=jnp.float32), (H, N)).copy()
        B_ri = jax.random.normal(k3, (H, N, 2), dtype=jnp.float32) * 0.5
        C_ri = jax.random.normal(k4, (CH, H, N, 2), dtype=jnp.float32) * 0.5
        return {'log_dt': log_dt, 'inv_A_real': inv_A_real, 'A_imag': A_imag, 'B_ri': B_ri, 'C_ri': C_ri, 'L': SEQ_L}
    _L0_tok_all = _L0_tok_setup()
    _L0_tok_in = {k: v for k, v in _L0_tok_all.items() if k in ('log_dt', 'inv_A_real', 'A_imag', 'B_ri')}
    del _L0_tok_all

    def _L0_attn_setup():
        import jax, jax.numpy as jnp
        import numpy as np
        import math
        from jax import lax
        B, T, HID, H, J = (4, 512, 256, 8, 2)
        EPS = 1e-06
        LN_EPS = 1e-05

        def _alibi_slopes(n):

            def pow2(m):
                start = 2 ** (-2 ** (-(math.log2(m) - 3)))
                return [start * start ** i for i in range(m)]
            if math.log2(n).is_integer():
                return np.array(pow2(n), dtype=np.float32)
            c = 2 ** int(math.floor(math.log2(n)))
            s = pow2(c) + _alibi_slopes(2 * c).tolist()[:n - c]
            return np.array(s, dtype=np.float32)

        def _deltanet(x, Wq, Wk, Wv, Wbeta, bbeta, Wmix, bmix, Wgate, bgate, Wout, bout, ln_g, ln_b):
            b, t, hid = x.shape
            h = Wgate.shape[0]
            j = Wbeta.shape[0] // h
            d = hid // h
            r = jnp.asarray(np.exp(-_alibi_slopes(h)))[None, :, None]
            q = (jax.nn.elu(x @ Wq.T) + 1.0).reshape(b, t, h, d)
            k = (jax.nn.elu(x @ Wk.T) + 1.0).reshape(b, t, h, d)
            v = (x @ Wv.T).reshape(b, t, h, d)
            beta = (x @ Wbeta.T + bbeta).reshape(b, t, h, j)
            mix = (x @ Wmix.T + bmix).reshape(b, t, h, j)
            gate = jax.nn.sigmoid(x @ Wgate.T + bgate)

            def step(carry, inp):
                S, z = carry
                q_t, k_t, v_t, beta_t, mix_t, g_t = inp
                beta_eff = jnp.minimum(jax.nn.sigmoid(beta_t) * r, 0.9999)
                outer = jnp.einsum('bhd,bhe->bhde', k_t, v_t).astype(jnp.float32)[:, :, None]
                S = S * beta_eff[..., None, None] + g_t[:, :, None, None, None] * outer
                z = z * beta_eff[..., None] + g_t[:, :, None, None] * k_t[:, :, None, :]
                num = jnp.einsum('bhd,bhjde->bhje', q_t, S)
                denom = jnp.einsum('bhd,bhjd->bhj', q_t, z) + EPS
                w = jax.nn.softmax(mix_t, axis=-1)[..., None]
                y_t = jnp.sum(num / denom[..., None] * w, axis=2)
                return ((S, z), y_t)
            S0 = jnp.zeros((b, h, j, d, d), jnp.float32)
            z0 = jnp.zeros((b, h, j, d), jnp.float32)
            tm = lambda a: jnp.swapaxes(a, 0, 1)
            _, yT = lax.scan(step, (S0, z0), (tm(q), tm(k), tm(v), tm(beta), tm(mix), tm(gate)))
            y = jnp.swapaxes(yT, 0, 1).reshape(b, t, hid).astype(x.dtype)
            out = y @ Wout.T + bout
            hres = x + out
            mu = jnp.mean(hres, axis=-1, keepdims=True)
            var = jnp.mean(jnp.square(hres - mu), axis=-1, keepdims=True)
            return (hres - mu) / jnp.sqrt(var + LN_EPS) * ln_g + ln_b
        key = jax.random.key(seed)
        ks = jax.random.split(key, 9)
        sc = 0.02
        return {'x': jax.random.normal(ks[0], (B, T, HID), jnp.float32), 'Wq': jax.random.normal(ks[1], (HID, HID), jnp.float32) * sc, 'Wk': jax.random.normal(ks[2], (HID, HID), jnp.float32) * sc, 'Wv': jax.random.normal(ks[3], (HID, HID), jnp.float32) * sc, 'Wbeta': jax.random.normal(ks[4], (H * J, HID), jnp.float32) * sc, 'bbeta': jnp.full((H * J,), 2.1972, jnp.float32), 'Wmix': jax.random.normal(ks[5], (H * J, HID), jnp.float32) * sc, 'bmix': jnp.zeros((H * J,), jnp.float32), 'Wgate': jax.random.normal(ks[6], (H, HID), jnp.float32) * sc, 'bgate': jnp.zeros((H,), jnp.float32), 'Wout': jax.random.normal(ks[7], (HID, HID), jnp.float32) * sc, 'bout': jnp.zeros((HID,), jnp.float32), 'ln_g': jnp.ones((HID,), jnp.float32), 'ln_b': jnp.zeros((HID,), jnp.float32)}
    _L0_attn_all = _L0_attn_setup()
    _L0_attn_in = {k: v for k, v in _L0_attn_all.items() if k in ('Wq', 'Wk', 'Wv', 'Wbeta', 'bbeta', 'Wmix', 'bmix', 'Wgate', 'bgate', 'Wout', 'bout', 'ln_g', 'ln_b')}
    del _L0_attn_all

    def _L0_ffn_setup():
        import jax, jax.numpy as jnp
        import numpy as np
        D_MODEL = 256
        N_HEADS = 16
        HEAD_DIM = D_MODEL // N_HEADS
        FFN_DIM = 1024
        N_EXPERTS = 8
        TOP_K = 2
        BATCH = 4
        SEQ = 256

        def _layernorm(x, w, b, eps=1e-05):
            mu = jnp.mean(x, axis=-1, keepdims=True)
            var = jnp.mean(jnp.square(x - mu), axis=-1, keepdims=True)
            return (x - mu) * jax.lax.rsqrt(var + eps) * w + b

        def _causal_attention(nx, Wqkv, bqkv, Wo, bo):
            B, S, D = nx.shape
            qkv = nx @ Wqkv + bqkv
            q, k, v = jnp.split(qkv, 3, axis=-1)
            q = q.reshape(B, S, N_HEADS, HEAD_DIM)
            k = k.reshape(B, S, N_HEADS, HEAD_DIM)
            v = v.reshape(B, S, N_HEADS, HEAD_DIM)
            scores = jnp.einsum('bqhd,bkhd->bhqk', q, k) / jnp.sqrt(jnp.float32(HEAD_DIM))
            causal = jnp.tril(jnp.ones((S, S), bool))
            scores = jnp.where(causal, scores, jnp.finfo(scores.dtype).min)
            attn = jax.nn.softmax(scores, axis=-1)
            out = jnp.einsum('bhqk,bkhd->bqhd', attn, v).reshape(B, S, D)
            return out @ Wo + bo

        def _moe_ffn(nx, gate_W, fc1_w, fc1_b, fc2_w, fc2_b):
            gate_logits = nx @ gate_W
            topk_vals, topk_idx = jax.lax.top_k(gate_logits, TOP_K)
            gate_w = jax.nn.softmax(topk_vals, axis=-1)
            dense_gates = jnp.sum(jax.nn.one_hot(topk_idx, N_EXPERTS, dtype=nx.dtype) * gate_w[..., None], axis=-2)
            moe_out = jnp.zeros_like(nx)
            for e in range(N_EXPERTS):
                h = jax.nn.gelu(jnp.einsum('bsd,fd->bsf', nx, fc1_w[e]) + fc1_b[e], approximate=False)
                y = jnp.einsum('bsf,df->bsd', h, fc2_w[e]) + fc2_b[e]
                moe_out = moe_out + y * dense_gates[..., e:e + 1]
            return moe_out
        key = jax.random.key(seed)
        ks = jax.random.split(key, 12)
        s = lambda k, shape, scale: jax.random.normal(k, shape, dtype=jnp.float32) * scale
        inp = {'x': s(ks[0], (BATCH, SEQ, D_MODEL), 1.0), 'ln1_w': jnp.ones((D_MODEL,), jnp.float32), 'ln1_b': jnp.zeros((D_MODEL,), jnp.float32), 'ln2_w': jnp.ones((D_MODEL,), jnp.float32), 'ln2_b': jnp.zeros((D_MODEL,), jnp.float32), 'Wqkv': s(ks[1], (D_MODEL, 3 * D_MODEL), 0.02), 'bqkv': jnp.zeros((3 * D_MODEL,), jnp.float32), 'Wo': s(ks[2], (D_MODEL, D_MODEL), 0.02), 'bo': jnp.zeros((D_MODEL,), jnp.float32), 'gate_W': s(ks[3], (D_MODEL, N_EXPERTS), 0.02), 'fc1_w': s(ks[4], (N_EXPERTS, FFN_DIM, D_MODEL), (2.0 / D_MODEL) ** 0.5), 'fc1_b': jnp.zeros((N_EXPERTS, FFN_DIM), jnp.float32), 'fc2_w': s(ks[5], (N_EXPERTS, D_MODEL, FFN_DIM), (1.0 / FFN_DIM) ** 0.5), 'fc2_b': jnp.zeros((N_EXPERTS, D_MODEL), jnp.float32)}
        return inp
    _L0_ffn_all = _L0_ffn_setup()
    _L0_ffn_in = {k: v for k, v in _L0_ffn_all.items() if k in ('ln1_w', 'ln1_b', 'ln2_w', 'ln2_b', 'Wqkv', 'bqkv', 'Wo', 'bo', 'gate_W', 'fc1_w', 'fc1_b', 'fc2_w', 'fc2_b')}
    del _L0_ffn_all

    def _L1_attn_setup():
        import jax, jax.numpy as jnp
        import numpy as np

        def _ln(x, g, b):
            m = x.mean(-1, keepdims=True)
            v = x.var(-1, keepdims=True)
            return (x - m) * jax.lax.rsqrt(v + 1e-05) * g + b

        def _shift(x):
            return jnp.pad(x, ((0, 0), (1, 0), (0, 0)))[:, :-1]
        key = jax.random.key(seed)
        ks = jax.random.split(key, 20)
        B, S, D, E, F = (2, 512, 256, 8, 512)
        s = 0.02
        return dict(x=jax.random.normal(ks[0], (B, S, D), jnp.float32), ln1_g=jnp.ones((D,), jnp.float32), ln1_b=jnp.zeros((D,), jnp.float32), ln2_g=jnp.ones((D,), jnp.float32), ln2_b=jnp.zeros((D,), jnp.float32), tm_mu_k=jax.random.uniform(ks[1], (D,), jnp.float32), tm_mu_v=jax.random.uniform(ks[2], (D,), jnp.float32), tm_mu_r=jax.random.uniform(ks[3], (D,), jnp.float32), time_decay=jax.random.normal(ks[4], (D,), jnp.float32) * 0.1, time_first=jax.random.normal(ks[5], (D,), jnp.float32) * 0.1, Wk=jax.random.normal(ks[6], (D, D), jnp.float32) * s, Wv=jax.random.normal(ks[7], (D, D), jnp.float32) * s, Wr=jax.random.normal(ks[8], (D, D), jnp.float32) * s, Wo=jax.random.normal(ks[9], (D, D), jnp.float32) * s, router_w=jax.random.normal(ks[10], (D, E), jnp.float32) * s, cm_mu_k=jax.random.uniform(ks[11], (E, D), jnp.float32), cm_mu_r=jax.random.uniform(ks[12], (E, D), jnp.float32), eWk=jax.random.normal(ks[13], (E, D, F), jnp.float32) * s, eWv=jax.random.normal(ks[14], (E, F, D), jnp.float32) * s, eWr=jax.random.normal(ks[15], (E, D, D), jnp.float32) * s)
    _L1_attn_all = _L1_attn_setup()
    _L1_attn_in = {k: v for k, v in _L1_attn_all.items() if k in ('ln1_g', 'ln1_b', 'ln2_g', 'ln2_b', 'tm_mu_k', 'tm_mu_v', 'tm_mu_r', 'time_decay', 'time_first', 'Wk', 'Wv', 'Wr', 'Wo', 'router_w', 'cm_mu_k', 'cm_mu_r', 'eWk', 'eWv', 'eWr')}
    del _L1_attn_all

    def _L1_ffn_setup():
        import jax, jax.numpy as jnp
        import numpy as np
        E = 32
        H = 256
        I = 128
        G = 8
        TKG = 4
        TOPK = 8
        NSH = 2
        SCALE = 2.5
        key = jax.random.key(seed)
        ks = jax.random.split(key, 10)
        s = 0.02
        return {'hidden_states': jax.random.normal(ks[0], (2, 256, H), jnp.float32), 'gate_w': jax.random.normal(ks[1], (E, H), jnp.float32) * s, 'gate_bias': jax.random.normal(ks[2], (E,), jnp.float32) * s, 'w_gate': jax.random.normal(ks[3], (E, I, H), jnp.float32) * s, 'w_up': jax.random.normal(ks[4], (E, I, H), jnp.float32) * s, 'w_down': jax.random.normal(ks[5], (E, H, I), jnp.float32) * s, 'sh_gate': jax.random.normal(ks[6], (I * NSH, H), jnp.float32) * s, 'sh_up': jax.random.normal(ks[7], (I * NSH, H), jnp.float32) * s, 'sh_down': jax.random.normal(ks[8], (H, I * NSH), jnp.float32) * s}
    _L1_ffn_all = _L1_ffn_setup()
    _L1_ffn_in = {k: v for k, v in _L1_ffn_all.items() if k in ('gate_w', 'gate_bias', 'w_gate', 'w_up', 'w_down', 'sh_gate', 'sh_up', 'sh_down')}
    del _L1_ffn_all
    return {'x': x, 'txt': txt, 'L0_tok_log_dt': _L0_tok_in['log_dt'], 'L0_tok_inv_A_real': _L0_tok_in['inv_A_real'], 'L0_tok_A_imag': _L0_tok_in['A_imag'], 'L0_tok_B_ri': _L0_tok_in['B_ri'], 'L0_attn_Wq': _L0_attn_in['Wq'], 'L0_attn_Wk': _L0_attn_in['Wk'], 'L0_attn_Wv': _L0_attn_in['Wv'], 'L0_attn_Wbeta': _L0_attn_in['Wbeta'], 'L0_attn_bbeta': _L0_attn_in['bbeta'], 'L0_attn_Wmix': _L0_attn_in['Wmix'], 'L0_attn_bmix': _L0_attn_in['bmix'], 'L0_attn_Wgate': _L0_attn_in['Wgate'], 'L0_attn_bgate': _L0_attn_in['bgate'], 'L0_attn_Wout': _L0_attn_in['Wout'], 'L0_attn_bout': _L0_attn_in['bout'], 'L0_attn_ln_g': _L0_attn_in['ln_g'], 'L0_attn_ln_b': _L0_attn_in['ln_b'], 'L0_ffn_ln1_w': _L0_ffn_in['ln1_w'], 'L0_ffn_ln1_b': _L0_ffn_in['ln1_b'], 'L0_ffn_ln2_w': _L0_ffn_in['ln2_w'], 'L0_ffn_ln2_b': _L0_ffn_in['ln2_b'], 'L0_ffn_Wqkv': _L0_ffn_in['Wqkv'], 'L0_ffn_bqkv': _L0_ffn_in['bqkv'], 'L0_ffn_Wo': _L0_ffn_in['Wo'], 'L0_ffn_bo': _L0_ffn_in['bo'], 'L0_ffn_gate_W': _L0_ffn_in['gate_W'], 'L0_ffn_fc1_w': _L0_ffn_in['fc1_w'], 'L0_ffn_fc1_b': _L0_ffn_in['fc1_b'], 'L0_ffn_fc2_w': _L0_ffn_in['fc2_w'], 'L0_ffn_fc2_b': _L0_ffn_in['fc2_b'], 'L1_attn_ln1_g': _L1_attn_in['ln1_g'], 'L1_attn_ln1_b': _L1_attn_in['ln1_b'], 'L1_attn_ln2_g': _L1_attn_in['ln2_g'], 'L1_attn_ln2_b': _L1_attn_in['ln2_b'], 'L1_attn_tm_mu_k': _L1_attn_in['tm_mu_k'], 'L1_attn_tm_mu_v': _L1_attn_in['tm_mu_v'], 'L1_attn_tm_mu_r': _L1_attn_in['tm_mu_r'], 'L1_attn_time_decay': _L1_attn_in['time_decay'], 'L1_attn_time_first': _L1_attn_in['time_first'], 'L1_attn_Wk': _L1_attn_in['Wk'], 'L1_attn_Wv': _L1_attn_in['Wv'], 'L1_attn_Wr': _L1_attn_in['Wr'], 'L1_attn_Wo': _L1_attn_in['Wo'], 'L1_attn_router_w': _L1_attn_in['router_w'], 'L1_attn_cm_mu_k': _L1_attn_in['cm_mu_k'], 'L1_attn_cm_mu_r': _L1_attn_in['cm_mu_r'], 'L1_attn_eWk': _L1_attn_in['eWk'], 'L1_attn_eWv': _L1_attn_in['eWv'], 'L1_attn_eWr': _L1_attn_in['eWr'], 'L1_ffn_gate_w': _L1_ffn_in['gate_w'], 'L1_ffn_gate_bias': _L1_ffn_in['gate_bias'], 'L1_ffn_w_gate': _L1_ffn_in['w_gate'], 'L1_ffn_w_up': _L1_ffn_in['w_up'], 'L1_ffn_w_down': _L1_ffn_in['w_down'], 'L1_ffn_sh_gate': _L1_ffn_in['sh_gate'], 'L1_ffn_sh_up': _L1_ffn_in['sh_up'], 'L1_ffn_sh_down': _L1_ffn_in['sh_down']}

def reference(x, txt, L0_tok_log_dt, L0_tok_inv_A_real, L0_tok_A_imag, L0_tok_B_ri, L0_attn_Wq, L0_attn_Wk, L0_attn_Wv, L0_attn_Wbeta, L0_attn_bbeta, L0_attn_Wmix, L0_attn_bmix, L0_attn_Wgate, L0_attn_bgate, L0_attn_Wout, L0_attn_bout, L0_attn_ln_g, L0_attn_ln_b, L0_ffn_ln1_w, L0_ffn_ln1_b, L0_ffn_ln2_w, L0_ffn_ln2_b, L0_ffn_Wqkv, L0_ffn_bqkv, L0_ffn_Wo, L0_ffn_bo, L0_ffn_gate_W, L0_ffn_fc1_w, L0_ffn_fc1_b, L0_ffn_fc2_w, L0_ffn_fc2_b, L1_attn_ln1_g, L1_attn_ln1_b, L1_attn_ln2_g, L1_attn_ln2_b, L1_attn_tm_mu_k, L1_attn_tm_mu_v, L1_attn_tm_mu_r, L1_attn_time_decay, L1_attn_time_first, L1_attn_Wk, L1_attn_Wv, L1_attn_Wr, L1_attn_Wo, L1_attn_router_w, L1_attn_cm_mu_k, L1_attn_cm_mu_r, L1_attn_eWk, L1_attn_eWv, L1_attn_eWr, L1_ffn_gate_w, L1_ffn_gate_bias, L1_ffn_w_gate, L1_ffn_w_up, L1_ffn_w_down, L1_ffn_sh_gate, L1_ffn_sh_up, L1_ffn_sh_down):
    import jax
    import jax.numpy as jnp

    def _L0_tok_ref(log_dt, inv_A_real, A_imag, B_ri, C_ri, L):
        import jax, jax.numpy as jnp
        import numpy as np
        import math
        H = 256
        N = 64
        CH = 1
        SEQ_L = 256
        dt = jnp.exp(log_dt)
        A = -jnp.exp(inv_A_real) + 1j * A_imag
        B = B_ri[..., 0] + 1j * B_ri[..., 1]
        C = C_ri[..., 0] + 1j * C_ri[..., 1]
        dtA = A * dt[:, None]
        dA = (1.0 + dtA / 2) / (1.0 - dtA / 2)
        C_term = C * B[None]
        log_dA = jnp.log(dA)
        V = jnp.exp(log_dA[:, :, None] * jnp.arange(L))
        K = 2.0 * jnp.einsum('chn,hnl->chl', C_term, V).real
        return K.astype(jnp.float32)

    def _L0_attn_ref(x, Wq, Wk, Wv, Wbeta, bbeta, Wmix, bmix, Wgate, bgate, Wout, bout, ln_g, ln_b):
        import jax, jax.numpy as jnp
        import numpy as np
        import math
        from jax import lax
        B, T, HID, H, J = (4, 512, 256, 8, 2)
        EPS = 1e-06
        LN_EPS = 1e-05

        def _alibi_slopes(n):

            def pow2(m):
                start = 2 ** (-2 ** (-(math.log2(m) - 3)))
                return [start * start ** i for i in range(m)]
            if math.log2(n).is_integer():
                return np.array(pow2(n), dtype=np.float32)
            c = 2 ** int(math.floor(math.log2(n)))
            s = pow2(c) + _alibi_slopes(2 * c).tolist()[:n - c]
            return np.array(s, dtype=np.float32)

        def _deltanet(x, Wq, Wk, Wv, Wbeta, bbeta, Wmix, bmix, Wgate, bgate, Wout, bout, ln_g, ln_b):
            b, t, hid = x.shape
            h = Wgate.shape[0]
            j = Wbeta.shape[0] // h
            d = hid // h
            r = jnp.asarray(np.exp(-_alibi_slopes(h)))[None, :, None]
            q = (jax.nn.elu(x @ Wq.T) + 1.0).reshape(b, t, h, d)
            k = (jax.nn.elu(x @ Wk.T) + 1.0).reshape(b, t, h, d)
            v = (x @ Wv.T).reshape(b, t, h, d)
            beta = (x @ Wbeta.T + bbeta).reshape(b, t, h, j)
            mix = (x @ Wmix.T + bmix).reshape(b, t, h, j)
            gate = jax.nn.sigmoid(x @ Wgate.T + bgate)

            def step(carry, inp):
                S, z = carry
                q_t, k_t, v_t, beta_t, mix_t, g_t = inp
                beta_eff = jnp.minimum(jax.nn.sigmoid(beta_t) * r, 0.9999)
                outer = jnp.einsum('bhd,bhe->bhde', k_t, v_t).astype(jnp.float32)[:, :, None]
                S = S * beta_eff[..., None, None] + g_t[:, :, None, None, None] * outer
                z = z * beta_eff[..., None] + g_t[:, :, None, None] * k_t[:, :, None, :]
                num = jnp.einsum('bhd,bhjde->bhje', q_t, S)
                denom = jnp.einsum('bhd,bhjd->bhj', q_t, z) + EPS
                w = jax.nn.softmax(mix_t, axis=-1)[..., None]
                y_t = jnp.sum(num / denom[..., None] * w, axis=2)
                return ((S, z), y_t)
            S0 = jnp.zeros((b, h, j, d, d), jnp.float32)
            z0 = jnp.zeros((b, h, j, d), jnp.float32)
            tm = lambda a: jnp.swapaxes(a, 0, 1)
            _, yT = lax.scan(step, (S0, z0), (tm(q), tm(k), tm(v), tm(beta), tm(mix), tm(gate)))
            y = jnp.swapaxes(yT, 0, 1).reshape(b, t, hid).astype(x.dtype)
            out = y @ Wout.T + bout
            hres = x + out
            mu = jnp.mean(hres, axis=-1, keepdims=True)
            var = jnp.mean(jnp.square(hres - mu), axis=-1, keepdims=True)
            return (hres - mu) / jnp.sqrt(var + LN_EPS) * ln_g + ln_b
        return _deltanet(x, Wq, Wk, Wv, Wbeta, bbeta, Wmix, bmix, Wgate, bgate, Wout, bout, ln_g, ln_b)

    def _L0_ffn_ref(x, ln1_w, ln1_b, ln2_w, ln2_b, Wqkv, bqkv, Wo, bo, gate_W, fc1_w, fc1_b, fc2_w, fc2_b):
        import jax, jax.numpy as jnp
        import numpy as np
        D_MODEL = 256
        N_HEADS = 16
        HEAD_DIM = D_MODEL // N_HEADS
        FFN_DIM = 1024
        N_EXPERTS = 8
        TOP_K = 2
        BATCH = 4
        SEQ = 256

        def _layernorm(x, w, b, eps=1e-05):
            mu = jnp.mean(x, axis=-1, keepdims=True)
            var = jnp.mean(jnp.square(x - mu), axis=-1, keepdims=True)
            return (x - mu) * jax.lax.rsqrt(var + eps) * w + b

        def _causal_attention(nx, Wqkv, bqkv, Wo, bo):
            B, S, D = nx.shape
            qkv = nx @ Wqkv + bqkv
            q, k, v = jnp.split(qkv, 3, axis=-1)
            q = q.reshape(B, S, N_HEADS, HEAD_DIM)
            k = k.reshape(B, S, N_HEADS, HEAD_DIM)
            v = v.reshape(B, S, N_HEADS, HEAD_DIM)
            scores = jnp.einsum('bqhd,bkhd->bhqk', q, k) / jnp.sqrt(jnp.float32(HEAD_DIM))
            causal = jnp.tril(jnp.ones((S, S), bool))
            scores = jnp.where(causal, scores, jnp.finfo(scores.dtype).min)
            attn = jax.nn.softmax(scores, axis=-1)
            out = jnp.einsum('bhqk,bkhd->bqhd', attn, v).reshape(B, S, D)
            return out @ Wo + bo

        def _moe_ffn(nx, gate_W, fc1_w, fc1_b, fc2_w, fc2_b):
            gate_logits = nx @ gate_W
            topk_vals, topk_idx = jax.lax.top_k(gate_logits, TOP_K)
            gate_w = jax.nn.softmax(topk_vals, axis=-1)
            dense_gates = jnp.sum(jax.nn.one_hot(topk_idx, N_EXPERTS, dtype=nx.dtype) * gate_w[..., None], axis=-2)
            moe_out = jnp.zeros_like(nx)
            for e in range(N_EXPERTS):
                h = jax.nn.gelu(jnp.einsum('bsd,fd->bsf', nx, fc1_w[e]) + fc1_b[e], approximate=False)
                y = jnp.einsum('bsf,df->bsd', h, fc2_w[e]) + fc2_b[e]
                moe_out = moe_out + y * dense_gates[..., e:e + 1]
            return moe_out
        nx = _layernorm(x, ln1_w, ln1_b)
        attn_out = _causal_attention(nx, Wqkv, bqkv, Wo, bo)
        x = x + attn_out
        nx2 = _layernorm(x, ln2_w, ln2_b)
        moe_out = _moe_ffn(nx2, gate_W, fc1_w, fc1_b, fc2_w, fc2_b)
        return x + moe_out

    def _L1_attn_ref(x, ln1_g, ln1_b, ln2_g, ln2_b, tm_mu_k, tm_mu_v, tm_mu_r, time_decay, time_first, Wk, Wv, Wr, Wo, router_w, cm_mu_k, cm_mu_r, eWk, eWv, eWr):
        import jax, jax.numpy as jnp
        import numpy as np

        def _ln(x, g, b):
            m = x.mean(-1, keepdims=True)
            v = x.var(-1, keepdims=True)
            return (x - m) * jax.lax.rsqrt(v + 1e-05) * g + b

        def _shift(x):
            return jnp.pad(x, ((0, 0), (1, 0), (0, 0)))[:, :-1]
        TOP_K = 2
        E = router_w.shape[1]
        B, S, D = x.shape
        xn = _ln(x, ln1_g, ln1_b)
        xx = _shift(xn)
        xk = xn * tm_mu_k + xx * (1.0 - tm_mu_k)
        xv = xn * tm_mu_v + xx * (1.0 - tm_mu_v)
        xr = xn * tm_mu_r + xx * (1.0 - tm_mu_r)
        k = xk @ Wk
        v = xv @ Wv
        r = jax.nn.sigmoid(xr @ Wr)
        w = -jnp.exp(time_decay)
        u = time_first

        def step(carry, kv_t):
            aa, bb, pp = carry
            kt, vt = kv_t
            qq = jnp.maximum(pp, u + kt)
            e1 = jnp.exp(pp - qq)
            e2 = jnp.exp(u + kt - qq)
            wkv_t = (e1 * aa + e2 * vt) / (e1 * bb + e2)
            qq2 = jnp.maximum(pp + w, kt)
            e1b = jnp.exp(pp + w - qq2)
            e2b = jnp.exp(kt - qq2)
            return ((e1b * aa + e2b * vt, e1b * bb + e2b, qq2), wkv_t)
        init = (jnp.zeros((B, D), x.dtype), jnp.zeros((B, D), x.dtype), jnp.full((B, D), -1e+30, x.dtype))
        _, wkv = jax.lax.scan(step, init, (k.transpose(1, 0, 2), v.transpose(1, 0, 2)))
        wkv = wkv.transpose(1, 0, 2)
        x = x + r * wkv @ Wo
        ei = _ln(x, ln2_g, ln2_b)
        probs = jax.nn.softmax(ei @ router_w, axis=-1)
        vals, idx = jax.lax.top_k(probs, TOP_K)
        wts = vals / vals.sum(-1, keepdims=True)
        tw = jnp.sum(jax.nn.one_hot(idx, E, dtype=x.dtype) * wts[..., None], axis=-2)
        exx = _shift(ei)
        mk = cm_mu_k[:, None, None, :]
        mr = cm_mu_r[:, None, None, :]
        xk_e = ei[None] * mk + exx[None] * (1.0 - mk)
        xr_e = ei[None] * mr + exx[None] * (1.0 - mr)
        k_e = jnp.square(jax.nn.relu(jnp.einsum('ebsd,edf->ebsf', xk_e, eWk)))
        kv_e = jnp.einsum('ebsf,efd->ebsd', k_e, eWv)
        r_e = jax.nn.sigmoid(jnp.einsum('ebsd,edg->ebsg', xr_e, eWr))
        expert_out = r_e * kv_e
        moe = jnp.einsum('ebsd,bse->bsd', expert_out, tw)
        return x + moe

    def _L1_ffn_ref(hidden_states, gate_w, gate_bias, w_gate, w_up, w_down, sh_gate, sh_up, sh_down):
        import jax, jax.numpy as jnp
        import numpy as np
        E = 32
        H = 256
        I = 128
        G = 8
        TKG = 4
        TOPK = 8
        NSH = 2
        SCALE = 2.5
        B, S, Hd = hidden_states.shape
        h = hidden_states.reshape(-1, Hd)
        logits = h.astype(jnp.float32) @ gate_w.T
        scores = jax.nn.sigmoid(logits)
        sc = scores + gate_bias
        grp = sc.reshape(-1, G, E // G)
        group_scores = jax.lax.top_k(grp, 2)[0].sum(-1)
        gidx = jax.lax.top_k(group_scores, TKG)[1]
        gmask = jnp.sum(jax.nn.one_hot(gidx, G, dtype=sc.dtype), axis=1)
        smask = jnp.repeat(gmask, E // G, axis=1)
        masked = jnp.where(smask > 0, sc, jnp.zeros_like(sc))
        tki = jax.lax.top_k(masked, TOPK)[1]
        tkw = jnp.take_along_axis(scores, tki, axis=1)
        tkw = tkw / (tkw.sum(-1, keepdims=True) + 1e-20)
        tkw = tkw * SCALE
        combine = (jax.nn.one_hot(tki, E, dtype=tkw.dtype) * tkw[..., None]).sum(1)
        g = jax.nn.silu(jnp.einsum('th,eih->tei', h, w_gate))
        u = jnp.einsum('th,eih->tei', h, w_up)
        routed = jnp.einsum('tei,ehi->th', g * u * combine[:, :, None], w_down)
        sg = jax.nn.silu(h @ sh_gate.T)
        shared = sg * (h @ sh_up.T) @ sh_down.T
        return (routed + shared).reshape(B, S, Hd)
    h = _L0_tok_ref(L0_tok_log_dt, L0_tok_inv_A_real, L0_tok_A_imag, L0_tok_B_ri, x, 256)
    h = jnp.concatenate([h, txt], axis=1)
    h = h + _L0_attn_ref(_layernorm(h, axis=-1), L0_attn_Wq, L0_attn_Wk, L0_attn_Wv, L0_attn_Wbeta, L0_attn_bbeta, L0_attn_Wmix, L0_attn_bmix, L0_attn_Wgate, L0_attn_bgate, L0_attn_Wout, L0_attn_bout, L0_attn_ln_g, L0_attn_ln_b)
    h = h + _L0_ffn_ref(_layernorm(h, axis=-1), L0_ffn_ln1_w, L0_ffn_ln1_b, L0_ffn_ln2_w, L0_ffn_ln2_b, L0_ffn_Wqkv, L0_ffn_bqkv, L0_ffn_Wo, L0_ffn_bo, L0_ffn_gate_W, L0_ffn_fc1_w, L0_ffn_fc1_b, L0_ffn_fc2_w, L0_ffn_fc2_b)
    h = h + _L1_attn_ref(_layernorm(h, axis=-1), L1_attn_ln1_g, L1_attn_ln1_b, L1_attn_ln2_g, L1_attn_ln2_b, L1_attn_tm_mu_k, L1_attn_tm_mu_v, L1_attn_tm_mu_r, L1_attn_time_decay, L1_attn_time_first, L1_attn_Wk, L1_attn_Wv, L1_attn_Wr, L1_attn_Wo, L1_attn_router_w, L1_attn_cm_mu_k, L1_attn_cm_mu_r, L1_attn_eWk, L1_attn_eWv, L1_attn_eWr)
    h = h + _L1_ffn_ref(_layernorm(h, axis=-1), L1_ffn_gate_w, L1_ffn_gate_bias, L1_ffn_w_gate, L1_ffn_w_up, L1_ffn_w_down, L1_ffn_sh_gate, L1_ffn_sh_up, L1_ffn_sh_down)
    return h

_drawn_inputs = setup_inputs


def setup_inputs(seed=0):
    import zlib

    import numpy as np

    out = dict(_drawn_inputs(seed))
    spreads = {'L0_attn_bbeta': (2.197200059890747, 0.6),
     'L0_attn_bmix': (0.0, 0.8),
     'L0_attn_bgate': (0.0, 0.8),
     'L0_attn_bout': (0.0, 0.1),
     'L0_attn_ln_g': (1.0, 0.2),
     'L0_attn_ln_b': (0.0, 0.1),
     'L0_ffn_ln1_w': (1.0, 0.6),
     'L0_ffn_ln1_b': (0.0, 0.654),
     'L0_ffn_ln2_w': (1.0, 0.2),
     'L0_ffn_ln2_b': (0.0, 0.1),
     'L0_ffn_bqkv': (0.0, 0.362),
     'L0_ffn_bo': (0.0, 0.1),
     'L0_ffn_fc1_b': (0.0, 0.8),
     'L0_ffn_fc2_b': (0.0, 0.61),
     'L1_attn_ln1_g': (1.0, 0.6),
     'L1_attn_ln1_b': (0.0, 0.8),
     'L1_attn_ln2_g': (1.0, 0.6),
     'L1_attn_ln2_b': (0.0, 0.8)}
    factors = {'L0_attn_Wq': 8.0,
     'L0_attn_Wk': 8.0,
     'L0_attn_Wv': 4.133,
     'L0_attn_Wbeta': 8.0,
     'L0_attn_Wmix': 8.0,
     'L0_attn_Wgate': 8.0,
     'L0_attn_Wout': 4.237,
     'L0_ffn_Wqkv': 3.94,
     'L0_ffn_Wo': 2.738,
     'L1_attn_tm_mu_k': 8.0,
     'L1_attn_tm_mu_v': 8.0,
     'L1_attn_tm_mu_r': 8.0,
     'L1_attn_time_decay': 8.0,
     'L1_attn_time_first': 8.0,
     'L1_attn_Wk': 8.0,
     'L1_attn_Wv': 8.0,
     'L1_attn_Wr': 8.0,
     'L1_attn_Wo': 8.0,
     'L1_attn_router_w': 8.0,
     'L1_attn_cm_mu_k': 8.0,
     'L1_attn_cm_mu_r': 8.0,
     'L1_attn_eWk': 8.0,
     'L1_attn_eWv': 8.0,
     'L1_attn_eWr': 8.0,
     'L1_ffn_gate_w': 64.0,
     'L1_ffn_gate_bias': 64.0,
     'L1_ffn_w_gate': 64.0,
     'L1_ffn_w_up': 56.863,
     'L1_ffn_w_down': 57.039,
     'L1_ffn_sh_gate': 41.312,
     'L1_ffn_sh_up': 36.471,
     'L1_ffn_sh_down': 36.4}
    for name, (base, spread) in spreads.items():
        noise = np.random.default_rng([zlib.crc32(name.encode()), seed]).standard_normal(out[name].shape)
        drawn = base * np.exp(spread * noise) if base else spread * noise
        out[name] = jnp.asarray(drawn.astype(out[name].dtype))
    for name, factor in factors.items():
        out[name] = (out[name] * factor).astype(out[name].dtype)
    return out
```

```python
from contextlib import ExitStack
import numpy as np
import concourse.bass as bass
from concourse import mybir

ALU = mybir.AluOpType
ACT = mybir.ActivationFunctionType
F32 = mybir.dt.float32
BF16 = mybir.dt.bfloat16
I32 = mybir.dt.int32
AX_X = mybir.AxisListType.X

P = 128
NB = 4
SEQ = 768
NC = SEQ // P
D = 256
DC = D // P
LN_EPS = 1e-5


def bc(ap, shape):
    return ap.broadcast_to(shape)


class Scope:

    def __init__(self, nc):
        self.nc, self.ctx, self.sems = nc, ExitStack(), []

    def __enter__(self):
        return self

    def __exit__(self, *a):
        return self.ctx.__exit__(*a)

    def sb(self, name, shape, dt=F32):
        return self.ctx.enter_context(self.nc.sbuf_tensor(name, shape, dt))

    def sem(self, name):
        s = self.ctx.enter_context(self.nc.semaphore(name))
        self.sems.append(s)
        return s

    def round_end(self):
        for s in self.sems:
            self.nc.gpsimd.sem_clear(s)
        self.nc.all_engine_barrier()


def chain(eng, sem):
    n = [0]

    def link(ins):
        n[0] += 1
        ins.then_inc(sem, 1)
        eng.wait_ge(sem, n[0])
    return link


def rsqrt(dve, link, x, y, t):
    link(dve.tensor_scalar(y.bitcast(I32), x.bitcast(I32), -0.5, float(0x5F3759DF), ALU.mult, ALU.add))
    for _ in range(4):
        link(dve.tensor_tensor(t, y, y, ALU.mult))
        link(dve.tensor_tensor(t, t, x, ALU.mult))
        link(dve.tensor_scalar(t, t, -0.5, 1.5, ALU.mult, ALU.add))
        link(dve.tensor_tensor(y, y, t, ALU.mult))


def layernorm(dve, link, tiles, outs, stats, mv, rs, tmp):
    n = len(tiles)
    for i, x in enumerate(tiles):
        ins = dve.bn_stats(stats[:, i, :], x)
    link(ins)
    for i in range(n):
        ins = dve.bn_aggr(mv[:, i, :], stats[:, i, :])
    link(ins)
    link(dve.tensor_scalar(tmp[:, 0, 0:n], mv[:, 0:n, 1], LN_EPS, None, ALU.add))
    rsqrt(dve, link, tmp[:, 0, 0:n], rs[:, 0:n], tmp[:, 1, 0:n])
    for i, x in enumerate(tiles):
        ins = dve.tensor_scalar(outs[i], x, mv[:, i, 0:1], rs[:, i:i + 1], ALU.subtract, ALU.mult)
    link(ins)


def accurate_exp(dve, link, x, out, n, t):
    link(dve.tensor_scalar(t, x, -87.0, 88.0, ALU.max, ALU.min))
    link(dve.tensor_scalar(out.bitcast(I32), t, 1.4426950408889634, None, ALU.mult))
    link(dve.tensor_copy(n, out.bitcast(I32)))
    link(dve.scalar_tensor_tensor(t, n, -0.693359375, t, ALU.mult, ALU.add))
    link(dve.scalar_tensor_tensor(t, n, 2.12194440e-4, t, ALU.mult, ALU.add))
    coefficients = [1.0]
    for k in range(2, 11):
        coefficients.append(coefficients[-1] / k)
    link(dve.tensor_scalar(out, t, coefficients[-1], None, ALU.mult))
    for c in reversed(coefficients[:-1]):
        link(dve.scalar_tensor_tensor(out, out, c, t, ALU.add, ALU.mult))
    link(dve.tensor_scalar(t.bitcast(I32), n, 127.0, float(1 << 23), ALU.add, ALU.mult))
    link(dve.scalar_tensor_tensor(out, out, 1.0, t, ALU.add, ALU.mult))


def ssm_tokens(nc, g):
    H, NA, NV, HG = 256, 8, 32, 64
    with Scope(nc) as s:
        cbr, cbi = s.sb("ssm_cb_re", [P, NB, H]), s.sb("ssm_cb_im", [P, NB, H])
        p1, p2 = s.sb("ssm_coarse_1", [P, NA, H]), s.sb("ssm_coarse_2", [P, NA, H])
        V = s.sb("ssm_fine", [P, NV, H])
        with Scope(nc) as u:
            inp = u.sb("ssm_in", [P, 5, H])
            cin = u.sb("ssm_c_in", [P, 2, NB, H])
            vr, vi = u.sb("ssm_vr", [P, 16, H]), u.sb("ssm_vi", [P, 16, H])
            pr, pi = u.sb("ssm_pr", [P, NA, H]), u.sb("ssm_pi", [P, NA, H])
            x = u.sb("ssm_x", [P, 8, 2, H])
            w = u.sb("ssm_w", [P, 6, H])
            t1, t2 = u.sb("ssm_t1", [P, 16, H]), u.sb("ssm_t2", [P, 16, H])
            loaded, text = u.sem("ssm_loaded"), u.sem("ssm_text_loaded")
            vchain = u.sem("ssm_vchain")
            with nc.Block() as block:
                @block.sync
                def _(sp):
                    for i, n in enumerate(("s4_ldt", "s4_are", "s4_aim", "s4_bre", "s4_bim")):
                        sp.dma_start(inp[:, i, :], g.d[n]).then_inc(loaded, 16)
                    sp.dma_start(cin[:, 0], g.d["s4_cre"]).then_inc(loaded, 16)
                    sp.dma_start(cin[:, 1], g.d["s4_cim"]).then_inc(loaded, 16)
                    for b in range(NB):
                        sp.dma_start(g.h[:, 2:NC, b, :], g.d["txt"][b].rearrange("(c p) n -> p c n", p=P)
                                     ).then_inc(text, 16)
                    sp.wait_ge(text, 16 * NB)

                @block.vector
                def _(dve):
                    link = chain(dve, vchain)

                    def mul(re, im, ar, ai, br, bi, k):
                        if re is not None:
                            dve.tensor_tensor(t1[:, 0:k], ar, br, ALU.mult)
                            link(dve.tensor_tensor(t2[:, 0:k], ai, bi, ALU.mult))
                            link(dve.tensor_tensor(re, t1[:, 0:k], t2[:, 0:k], ALU.subtract))
                        if im is not None:
                            dve.tensor_tensor(t1[:, 0:k], ar, bi, ALU.mult)
                            link(dve.tensor_tensor(t2[:, 0:k], ai, br, ALU.mult))
                            link(dve.tensor_tensor(im, t1[:, 0:k], t2[:, 0:k], ALU.add))

                    dve.memset(vr[:, 0], 1.0)
                    dve.memset(vi[:, 0], 0.0)
                    dve.memset(pr[:, 0], 1.0)
                    link(dve.memset(pi[:, 0], 0.0))
                    dve.wait_ge(loaded, 16 * 7)
                    accurate_exp(dve, link, inp[:, 0:2], w[:, 0:2], w[:, 2:4], w[:, 4:6])
                    dve.scalar_tensor_tensor(w[:, 2], w[:, 0], -0.5, w[:, 1], ALU.mult, ALU.mult)
                    link(dve.scalar_tensor_tensor(w[:, 3], w[:, 0], 0.5, inp[:, 2], ALU.mult, ALU.mult))
                    dve.tensor_tensor(w[:, 4], w[:, 3], w[:, 3], ALU.mult)
                    dve.tensor_scalar(w[:, 0], w[:, 2], -1.0, 1.0, ALU.mult, ALU.add)
                    link(dve.tensor_tensor(w[:, 5], w[:, 2], w[:, 2], ALU.mult))
                    link(dve.tensor_tensor(w[:, 0], w[:, 0], w[:, 0], ALU.mult))
                    link(dve.tensor_tensor(w[:, 0], w[:, 0], w[:, 4], ALU.add))
                    link(dve.reciprocal(w[:, 1], w[:, 0]))
                    link(dve.tensor_tensor(w[:, 5], w[:, 5], w[:, 4], ALU.add))
                    link(dve.tensor_scalar(w[:, 5], w[:, 5], -1.0, 1.0, ALU.mult, ALU.add))
                    dve.tensor_tensor(x[:, 0, 0], w[:, 5], w[:, 1], ALU.mult)
                    link(dve.scalar_tensor_tensor(x[:, 0, 1], w[:, 3], 2.0, w[:, 1], ALU.mult, ALU.mult))
                    for i in range(7):
                        mul(x[:, i + 1, 0:1], x[:, i + 1, 1:2], x[:, i, 0:1], x[:, i, 1:2], x[:, i, 0:1],
                            x[:, i, 1:2], 1)
                    link(dve.tensor_scalar(inp[:, 3:5], inp[:, 3:5], 2.0, None, ALU.mult))
                    mul(cbr[:], cbi[:], cin[:, 0], cin[:, 1], bc(inp[:, 3:4], [P, NB, H]),
                        bc(inp[:, 4:5], [P, NB, H]), NB)
                    for i in range(4):
                        k = 1 << i
                        mul(vr[:, k:2 * k], vi[:, k:2 * k], vr[:, 0:k], vi[:, 0:k],
                            bc(x[:, i, 0:1], [P, k, H]), bc(x[:, i, 1:2], [P, k, H]), k)
                    for i in range(3):
                        k = 1 << i
                        mul(pr[:, k:2 * k], pi[:, k:2 * k], pr[:, 0:k], pi[:, 0:k],
                            bc(x[:, 5 + i, 0:1], [P, k, H]), bc(x[:, 5 + i, 1:2], [P, k, H]), k)
                    top, low = slice(0, 64), slice(64, 128)
                    dve.tensor_copy(V[top, 0:16], vr[top])
                    dve.tensor_copy(V[low, 0:16], vi[low])
                    dve.tensor_copy(p1[top], pr[top])
                    dve.tensor_scalar(p1[low], pi[low], -1.0, None, ALU.mult)
                    dve.tensor_scalar(p2[top], pi[top], -1.0, None, ALU.mult)
                    dve.tensor_scalar(p2[low], pr[low], -1.0, None, ALU.mult)
                    dve.tensor_copy(w[top, 0], x[top, 4, 0])
                    dve.tensor_copy(w[low, 0], x[low, 4, 1])
                    dve.tensor_scalar(w[top, 1], x[top, 4, 1], -1.0, None, ALU.mult)
                    link(dve.tensor_copy(w[low, 1], x[low, 4, 0]))
                    dve.tensor_tensor(t1[:], vr[:], bc(w[:, 0:1], [P, 16, H]), ALU.mult)
                    link(dve.tensor_tensor(t2[:], vi[:], bc(w[:, 1:2], [P, 16, H]), ALU.mult))
                    link(dve.tensor_tensor(V[:, 16:32], t1[:], t2[:], ALU.add))
            u.round_end()
        L = s.sb("ssm_left", [P, NB, NA, HG])
        Lt = s.sb("ssm_left_t", [P, NB, NA, HG])
        ko = s.sb("ssm_out", [NB * NA, HG, NV])
        vchain, l_ready, k_ready = s.sem("ssm_vchain2"), s.sem("ssm_left_ready"), s.sem("ssm_k_ready")
        k_out, stored, back = s.sem("ssm_k_copied"), s.sem("ssm_k_stored"), s.sem("ssm_k_back")
        NBK = HG * NV // 512
        with nc.Fori(0, H // HG) as r:
            with nc.Block() as block:
                @block.vector
                def _(dve):
                    link = chain(dve, vchain)
                    hs = bass.ds(r * HG, HG)
                    dve.tensor_tensor(L[:], bc(cbr[:, :, hs].unsqueeze(2), [P, NB, NA, HG]),
                                      bc(p1[:, :, hs].unsqueeze(1), [P, NB, NA, HG]), ALU.mult)
                    link(dve.tensor_tensor(Lt[:], bc(cbi[:, :, hs].unsqueeze(2), [P, NB, NA, HG]),
                                           bc(p2[:, :, hs].unsqueeze(1), [P, NB, NA, HG]), ALU.mult))
                    dve.tensor_tensor(L[:], L[:], Lt[:], ALU.add).then_inc(l_ready, 1)

                @block.tensor
                def _(pe):
                    pe.wait_ge(l_ready, 1)
                    Lf = L[:].rearrange("p c a h -> p (c a) h")
                    for j in range(HG):
                        per = 512 // NV
                        mm = pe.matmul(g.ps[0:NB * NA, j // per, (j % per) * NV:(j % per + 1) * NV],
                                       Lf[:, :, j], V[:, :, bass.ds(r * HG + j, 1)].rearrange("p v o -> p (v o)"),
                                       start=True, stop=True)
                        if j % per == per - 1:
                            mm.then_inc(k_ready, 1)

                @block.scalar
                def _(act):
                    kof = ko[:].rearrange("p h v -> p (h v)")
                    for k in range(NBK):
                        act.wait_ge(k_ready, k + 1)
                        act.activation(kof[:, k * 512:(k + 1) * 512], g.ps[0:NB * NA, k, :], ACT.Copy
                                       ).then_inc(k_out, 1)

                @block.sync
                def _(sp):
                    sp.wait_ge(k_out, NBK)
                    for b in range(NB):
                        dst = g.scr_ssm[b][bass.ds(r * HG, HG), :].rearrange("h (a v) -> a h v", a=NA)
                        sp.dma_start(dst, ko[b * NA:(b + 1) * NA]).then_inc(stored, 16)
                    sp.wait_ge(stored, 16 * NB)
            s.round_end()
        with nc.Block() as block:
            @block.sync
            def _(sp):
                for b in range(NB):
                    sp.dma_start(g.h[:, 0:2, b, :], g.scr_ssm[b].rearrange("(c p) n -> p c n", p=P)
                                 ).then_inc(back, 16)
                sp.wait_ge(back, 16 * NB)
        s.round_end()


def deltanet(nc, g):
    NG = 4
    E1 = 33
    with Scope(nc) as s:
        wqk = s.sb("dn_wqk", [P, 2, DC, D])
        wv = s.sb("dn_wv", [P, DC, D + 40])
        wout = s.sb("dn_wout", [P, DC, D])
        rows = s.sb("dn_rows", [P, 3 * D + 40 + 16])
        masks = s.sb("dn_masks", [P, 3 * P + 2 * 4 * E1])
        selc = s.sb("dn_sel", [48, 16, P], BF16)
        identb = s.sb("dn_identb", [P, P], BF16)
        S = s.sb("dn_state", [P, NB, 2, 2 * 4 * E1])
        xn, xnb, hb = s.sb("dn_xn", [P, NB, D]), s.sb("dn_xnb", [P, NB, D]), s.sb("dn_hb", [P, NB, D])
        xnT = s.sb("dn_xnT", [P, DC, NB * P])
        qT, kT = s.sb("dn_qT", [P, 2, NB * P]), s.sb("dn_kT", [P, 2, NB * P])
        er = s.sb("dn_exp_relu", [P, 2, 2, NB * P])
        kt, vt = s.sb("dn_k", [P, NB, D]), s.sb("dn_v", [P, NB, D + 40])
        er2 = s.sb("dn_exp_relu2", [P, 2, 2, D])
        raw = s.sb("dn_gates_raw", [P, NB, 40])
        eb = s.sb("dn_gates_exp", [P, NB, 40])
        lb = s.sb("dn_logdecay", [P, NB, 16])
        gate = s.sb("dn_gate", [P, NB, 8])
        wmix = s.sb("dn_wmix", [P, NB, 16])
        mtmp = s.sb("dn_mixtmp", [P, NB, 8])
        cc = s.sb("dn_cum", [P, 2, NB, 16])
        cres = s.sb("dn_cres", [P, 2, NB, 16])
        csp = s.sb("dn_csplit", [P, NB, 3, 16], BF16)
        crows = s.sb("dn_crows", [48, NB * P], BF16)
        ec, kd, dtot = s.sb("dn_ec", [P, NB, 16]), s.sb("dn_kd", [P, NB, 16]), s.sb("dn_dtot", [P, NB, 16])
        vg = s.sb("dn_vg", [P, NB, 8, E1])
        kdk = s.sb("dn_kdk", [P, NB, 2, 8, 32])
        Eb, Db, Mb = (s.sb(f"dn_{n}", [P, 2, 4, P]) for n in ("expo", "decay", "masked"))
        zt, um = s.sb("dn_zt", [P, 2, 2, 8, E1]), s.sb("dn_um", [P, 2, 2 * 4 * E1])
        den = s.sb("dn_den", [P, 2, 16])
        yy = s.sb("dn_y2", [P, 2, 8, 32])
        y = s.sb("dn_y", [P, NB, D])
        yT = s.sb("dn_yT", [P, DC, NB * P])
        stats, mv, rs, ltmp = s.sb("dn_stats", [P, NB, 6]), s.sb("dn_mv", [P, NB, 2]), s.sb("dn_rs", [P, NB]), s.sb("dn_ltmp", [P, 2, NB])
        bout, lng, lnb, gb, floor = (rows[:, 0:D], rows[:, D:2 * D], rows[:, 2 * D:3 * D],
                                     rows[:, 3 * D:3 * D + 40], rows[:, 3 * D + 40:3 * D + 56])
        tri_le, ones, cmask = masks[:, 0:P], masks[:, P:2 * P], masks[:, 2 * P:3 * P]
        bdmask = masks[:, 3 * P:3 * P + 2 * 4 * E1]
        kt_u = kt[:].rearrange("p b (f r e) -> p b (f r) e", f=2, r=4)

        with Scope(nc) as u:
            loaded = u.sem("dn_loaded")
            with nc.Block() as block:
                @block.sync
                def _(sp):
                    for dst, n in ((wqk[:], "dn_wqk"), (wv[:], "dn_wv"), (wout[:], "dn_wout"), (rows[:], "dn_rows"),
                                   (masks[:], "dn_masks"), (selc[:], "dn_sel"), (identb[:], "identb")):
                        sp.dma_start(dst, g.d[n]).then_inc(loaded, 16)
                    sp.wait_ge(loaded, 16 * 7)

                @block.vector
                def _(dve):
                    dve.memset(S[:], 0.0)
            u.round_end()

        names = ("vchain achain pchain xn_ready xnT_psum xnT_ready fm_psum fm_act qk_ready tm_psum tm_act tm_free tm_ready "
                 "gates_raw gates_exp mix_shift decay_arg decay_log c_psum c_ready csplit_ready crows_psum crows_ready "
                 "ec_ready kd_arg kd_ready vg_ready kdk_ready ae_psum e_used m_done d_ready y_psum mm_done z_psum "
                 "z_used u_psum um_ready s_ready comb_done yT_psum yT_ready out_psum out_sum xnb_ready hb_ready").split()
        q = {n: s.sem("dn_" + n) for n in names}
        (vchain, achain, pchain, xn_ready, xnT_psum, xnT_ready, fm_psum, fm_act, qk_ready, tm_psum, tm_act, tm_free, tm_ready,
         gates_raw, gates_exp, mix_shift, decay_arg, decay_log, c_psum, c_ready, csplit_ready, crows_psum, crows_ready,
         ec_ready, kd_arg, kd_ready, vg_ready, kdk_ready, ae_psum, e_used, m_done, d_ready, y_psum, mm_done, z_psum,
         z_used, u_psum, um_ready, s_ready, comb_done, yT_psum, yT_ready, out_psum, out_sum, xnb_ready, hb_ready) = (
             q[n] for n in names)
        ps = g.ps
        tmA = [6, 0, 6, 0]
        tmB = [7, 1, 7, 1]

        with nc.Fori(0, NC) as c:
            hc = g.h[:, bass.ds(c, 1)].rearrange("p o b n -> p (o b) n")
            with nc.Block() as block:
                @block.tensor
                def _(pe):
                    pe.wait_ge(xn_ready, 1)
                    for d in range(DC):
                        for b in range(NB):
                            mm = pe.transpose(ps[:, d, b * P:(b + 1) * P], xn[:, b, d * P:(d + 1) * P], g.ident[:])
                    mm.then_inc(xnT_psum, 1)
                    pe.wait_ge(xnT_ready, 1)
                    for w in range(2):
                        for f in range(2):
                            for d in range(DC):
                                mm = pe.matmul(ps[:, 2 + 2 * w + f, :], wqk[:, w, d, f * P:(f + 1) * P], xnT[:, d, :],
                                               start=(d == 0), stop=(d == DC - 1))
                            mm.then_inc(fm_psum, 1)
                    for b in range(NB):
                        if b >= 2:
                            pe.wait_ge(tm_act, b - 1)
                        for d in range(DC):
                            pe.matmul(ps[:, tmA[b], 0:D + 40], xnT[:, d, b * P:(b + 1) * P], wv[:, d, :],
                                      start=(d == 0), stop=(d == DC - 1))
                        for d in range(DC):
                            mm = pe.matmul(ps[:, tmB[b], 0:D], xnT[:, d, b * P:(b + 1) * P], wqk[:, 1, d, :],
                                           start=(d == 0), stop=(d == DC - 1))
                        mm.then_inc(tm_psum, 1)
                    pe.wait_ge(decay_log, 1)
                    pe.wait_ge(fm_act, 4)
                    lbf = lb[:].rearrange("p b j -> p (b j)")
                    pe.matmul(ps[:, 2, 0:64], tri_le, lbf, start=True, stop=True)
                    pe.matmul(ps[:, 2, 64:128], ones, lbf, start=True, stop=True).then_inc(c_psum, 1)
                    pe.wait_ge(csplit_ready, 1)
                    crp = ps[0:48, 3, :].bitcast(BF16)
                    for b in range(NB):
                        mm = pe.transpose(crp[:, b * P:(b + 1) * P],
                                          csp[:, b].rearrange("p k j -> p (k j)"), identb[:])
                    mm.then_inc(crows_psum, 1)
                    pe.wait_ge(crows_ready, 1)
                    pe.wait_ge(qk_ready, 4)
                    pe.wait_ge(vg_ready, NB)
                    pe.wait_ge(tm_ready, NB)
                    for n in range(NB * NG + 1):
                        if n < NB * NG:
                            b, r = divmod(n, NG)
                            bs = slice(b * P, (b + 1) * P)
                            if r == 0:
                                if b >= 1:
                                    pe.wait_ge(um_ready, b)
                                for f in range(2):
                                    mm = pe.matmul(ps[:, 2 + f, 0:8 * E1], qT[:, f, bs], S[:, b, f, :],
                                                   start=True, stop=True)
                                mm.then_inc(z_psum, 1)
                            if n >= 2:
                                pe.wait_ge(m_done, n - 1)
                                pe.wait_ge(e_used, n - 1)
                            hr = slice(32 * r, 32 * r + 32)
                            for f in range(2):
                                pe.matmul(ps[:, 4 + n % 2, f * P:(f + 1) * P],
                                          kT[hr, f, bs], qT[hr, f, bs], start=True, stop=True)
                            for f in range(2):
                                for j in range(2):
                                    k = 2 * f + j
                                    mm = pe.matmul(ps[:, 6 + n % 2, k * P:(k + 1) * P], selc[:, f * 8 + j * 4 + r, :],
                                                   crows[:, bs], start=True, stop=True)
                            mm.then_inc(ae_psum, 1)
                            if r == 2:
                                pe.wait_ge(z_used, b + 1)
                                pe.wait_ge(kdk_ready, b + 1)
                                for f in range(2):
                                    for j in range(2):
                                        mm = pe.matmul(ps[:, 2 + f, j * 4 * E1:(j + 1) * 4 * E1],
                                                       kdk[:, b, j, 4 * f:4 * f + 4, :].rearrange("p h e -> p (h e)"),
                                                       vg[:, b, 4 * f:4 * f + 4, :].rearrange("p h e -> p (h e)"),
                                                       start=True, stop=True)
                                mm.then_inc(u_psum, 1)
                        if n >= 1:
                            b, r = divmod(n - 1, NG)
                            pe.wait_ge(m_done, n)
                            if r == 0 and b >= 1:
                                pe.wait_ge(comb_done, b)
                            for f in range(2):
                                for j in range(2):
                                    at = j * 4 * E1 + r * E1
                                    mm = pe.matmul(ps[:, f, at:at + E1], Mb[:, (n - 1) % 2, 2 * f + j, :],
                                                   vg[:, b, 4 * f + r, :], start=True, stop=True)
                            mm.then_inc(y_psum, 1)
                    pe.wait_ge(comb_done, NB)
                    for d in range(DC):
                        for b in range(NB):
                            mm = pe.transpose(ps[:, 6 + d, b * P:(b + 1) * P], y[:, b, d * P:(d + 1) * P], g.ident[:])
                    mm.then_inc(yT_psum, 1)
                    pe.wait_ge(yT_ready, 1)
                    for b in range(NB):
                        for d in range(DC):
                            mm = pe.matmul(ps[:, b, 0:D], yT[:, d, b * P:(b + 1) * P], wout[:, d, :],
                                           start=(d == 0), stop=(d == DC - 1))
                        mm.then_inc(out_psum, 1)

                @block.scalar
                def _(act):
                    act.wait_ge(xnT_psum, 1)
                    act.activation(xnT[:, 0, :], ps[:, 0, :], ACT.Copy)
                    act.activation(xnT[:, 1, :], ps[:, 1, :], ACT.Copy).then_inc(xnT_ready, 1)
                    for k in range(4):
                        act.wait_ge(fm_psum, k + 1)
                        if k >= 2:
                            act.wait_ge(qk_ready, k - 1)
                        act.activation(er[:, k % 2, 0, :], ps[:, 2 + k, :], ACT.Exp)
                        act.activation(er[:, k % 2, 1, :], ps[:, 2 + k, :], ACT.Relu).then_inc(fm_act, 1)
                    for b in range(NB):
                        act.wait_ge(tm_psum, b + 1)
                        if b >= 2:
                            act.wait_ge(tm_ready, b - 1)
                        act.activation(vt[:, b, :], ps[:, tmA[b], 0:D + 40], ACT.Copy)
                        act.activation(er2[:, b % 2, 0, :], ps[:, tmB[b], 0:D], ACT.Exp)
                        act.activation(er2[:, b % 2, 1, :], ps[:, tmB[b], 0:D], ACT.Relu).then_inc(tm_act, 1)
                    act.wait_ge(gates_raw, 1)
                    act.activation(eb[:, :, 0:16], raw[:, :, 0:16], ACT.Exp, scale=-1.0)
                    act.activation(eb[:, :, 32:40], raw[:, :, 32:40], ACT.Exp, scale=-1.0).then_inc(gates_exp, 1)
                    act.wait_ge(mix_shift, 1)
                    act.activation(eb[:, :, 16:32], raw[:, :, 16:32], ACT.Exp).then_inc(gates_exp, 1)
                    act.wait_ge(decay_arg, 1)
                    act.activation(lb[:], eb[:, :, 0:16], ACT.Ln).then_inc(decay_log, 1)
                    act.wait_ge(c_ready, 1)
                    act.activation(ec[:], cc[:, 0], ACT.Exp)
                    act.activation(dtot[:], cc[:, 1], ACT.Exp).then_inc(ec_ready, 1)
                    act.wait_ge(kd_arg, 1)
                    act.activation(kd[:], cres[:, 1], ACT.Exp).then_inc(kd_ready, 1)
                    act.wait_ge(crows_psum, 1)
                    act.activation(crows[:], ps[0:48, 3, 0:NB * P // 2].bitcast(BF16), ACT.Copy).then_inc(crows_ready, 1)
                    for n in range(NB * NG):
                        act.wait_ge(e_used, n + 1)
                        if n >= 2:
                            act.wait_ge(m_done, n - 1)
                        act.activation(Db[:, n % 2], Eb[:, n % 2], ACT.Exp).then_inc(d_ready, 1)
                    act.wait_ge(yT_psum, 1)
                    act.activation(yT[:, 0, :], ps[:, 6, :], ACT.Copy)
                    act.activation(yT[:, 1, :], ps[:, 7, :], ACT.Copy).then_inc(yT_ready, 1)

                @block.gpsimd
                def _(pool):
                    pool.wait_ge(xn_ready, 1)
                    pool.tensor_tensor(xnb[:], xn[:], bc(bout.unsqueeze(1), [P, NB, D]), ALU.add).then_inc(xnb_ready, 1)
                    pool.tensor_tensor(hb[:], hc, bc(lnb.unsqueeze(1), [P, NB, D]), ALU.add).then_inc(hb_ready, 1)
                    pool.wait_ge(kd_ready, 1)
                    pool.wait_ge(tm_ready, NB)
                    pool.wait_ge(vg_ready, NB)
                    for b in range(NB):
                        for j in range(2):
                            for f in range(2):
                                k = 8 * f + 4 * j
                                op = pool.tensor_tensor(kdk[:, b, j, 4 * f:4 * f + 4, :], kt_u[:, b, 4 * f:4 * f + 4, :],
                                                        bc(kd[:, b, k:k + 4].unsqueeze(2), [P, 4, 32]), ALU.mult)
                        op.then_inc(kdk_ready, 1)
                    for b in range(NB):
                        pool.wait_ge(z_psum, b + 1)
                        Sb = S[:, b].rearrange("p f (k e) -> p (f k) e", e=E1)
                        pool.tensor_tensor(Sb, Sb, bc(dtot[:, b].unsqueeze(2), [P, 16, E1]), ALU.mult).then_inc(pchain, 1)
                        pool.wait_ge(pchain, b + 1)
                        pool.wait_ge(um_ready, b + 1)
                        pool.tensor_tensor(S[:, b], S[:, b], um[:], ALU.add).then_inc(s_ready, 1)

                @block.vector
                def _(dve):
                    link = chain(dve, vchain)
                    layernorm(dve, link, [hc[:, b, :] for b in range(NB)], [xn[:, b, :] for b in range(NB)],
                              stats, mv, rs, ltmp)
                    dve.engine_nop().then_inc(xn_ready, 1)
                    for k in range(4):
                        dve.wait_ge(fm_act, k + 1)
                        dst = (qT, kT)[k // 2][:, k % 2, :]
                        dve.scalar_tensor_tensor(dst, er[:, k % 2, 0, :], 1.0, er[:, k % 2, 1, :], ALU.min, ALU.add
                                                 ).then_inc(qk_ready, 1)
                    for b in range(NB):
                        dve.wait_ge(tm_act, b + 1)
                        dve.tensor_tensor(raw[:, b], vt[:, b, D:D + 40], gb, ALU.add).then_inc(tm_free, 1)
                        dve.scalar_tensor_tensor(kt[:, b], er2[:, b % 2, 0], 1.0, er2[:, b % 2, 1], ALU.min, ALU.add
                                                 ).then_inc(tm_ready, 1)
                    dve.wait_ge(tm_free, NB)
                    dve.engine_nop().then_inc(gates_raw, 1)
                    mix = raw[:, :, 16:32].rearrange("p b (f j r) -> p b f j r", f=2, j=2)
                    mt = mtmp[:].rearrange("p b (f r) -> p b f r", f=2)
                    link(dve.tensor_tensor(mt, mix[:, :, :, 0], mix[:, :, :, 1], ALU.max))
                    dve.tensor_tensor(mix[:, :, :, 0], mix[:, :, :, 0], mt, ALU.subtract)
                    dve.tensor_tensor(mix[:, :, :, 1], mix[:, :, :, 1], mt, ALU.subtract).then_inc(mix_shift, 1)
                    dve.wait_ge(gates_exp, 1)
                    dve.tensor_scalar(eb[:, :, 0:16], eb[:, :, 0:16], 1.0, None, ALU.add)
                    link(dve.tensor_scalar(eb[:, :, 32:40], eb[:, :, 32:40], 1.0, None, ALU.add))
                    dve.reciprocal(gate[:], eb[:, :, 32:40])
                    link(dve.reciprocal(lb[:], eb[:, :, 0:16]))
                    link(dve.tensor_tensor(lb[:], lb[:], bc(floor.unsqueeze(1), [P, NB, 16]), ALU.mult))
                    dve.tensor_scalar(eb[:, :, 0:16], lb[:], 0.9999, 1e-19, ALU.min, ALU.max).then_inc(decay_arg, 1)
                    for b in range(NB):
                        vgb = vg[:, b]
                        dve.tensor_tensor(vgb[:, :, 0:32], vt[:, b, 0:D].rearrange("p (h e) -> p h e", h=8),
                                          bc(gate[:, b].unsqueeze(2), [P, 8, 32]), ALU.mult)
                        dve.tensor_copy(vgb[:, :, 32], gate[:, b]).then_inc(vg_ready, 1)
                    dve.wait_ge(gates_exp, 2)
                    em = eb[:, :, 16:32].rearrange("p b (f j r) -> p b f j r", f=2, j=2)
                    wm = wmix[:].rearrange("p b (f j r) -> p b f j r", f=2, j=2)
                    link(dve.tensor_tensor(mt, em[:, :, :, 0], em[:, :, :, 1], ALU.add))
                    link(dve.reciprocal(mt, mt))
                    dve.tensor_tensor(wm[:, :, :, 0], em[:, :, :, 0], mt, ALU.mult)
                    link(dve.tensor_tensor(wm[:, :, :, 1], em[:, :, :, 1], mt, ALU.mult))
                    dve.wait_ge(c_psum, 1)
                    dve.tensor_copy(cc[:].rearrange("p k b j -> p (k b j)"), ps[:, 2, 0:128]).then_inc(c_ready, 1)
                    dve.wait_ge(c_ready, 1)
                    dve.tensor_tensor(cres[:, 1], cc[:, 1], cc[:, 0], ALU.subtract).then_inc(kd_arg, 1)
                    link(dve.tensor_copy(csp[:, :, 0], cc[:, 0]))
                    link(dve.tensor_tensor(cres[:, 0], cc[:, 0], csp[:, :, 0], ALU.subtract))
                    link(dve.tensor_copy(csp[:, :, 1], cres[:, 0]))
                    link(dve.tensor_tensor(cres[:, 0], cres[:, 0], csp[:, :, 1], ALU.subtract))
                    dve.tensor_copy(csp[:, :, 2], cres[:, 0]).then_inc(csplit_ready, 1)
                    for n in range(NB * NG + 2):
                        if n < NB * NG:
                            b, r = divmod(n, NG)
                            dve.wait_ge(ae_psum, n + 1)
                            if n >= 2:
                                dve.wait_ge(d_ready, n - 1)
                            for f in range(2):
                                for j in range(2):
                                    k, hj = 2 * f + j, 8 * f + 4 * j + r
                                    op = dve.scalar_tensor_tensor(Eb[:, n % 2, k, :], ps[:, 6 + n % 2, k * P:(k + 1) * P],
                                                                  cc[:, 0, b, hj:hj + 1], cmask, ALU.subtract, ALU.min)
                            op.then_inc(e_used, 1)
                            if r == 0:
                                dve.wait_ge(z_psum, b + 1)
                                dve.wait_ge(ec_ready, 1)
                                dve.tensor_tensor(zt[:, b % 2], ps[:, 2:4, 0:8 * E1].rearrange("p f (k e) -> p f k e", e=E1),
                                                  bc(ec[:, b].rearrange("p (f k) -> p f k", f=2).unsqueeze(3), [P, 2, 8, E1]),
                                                  ALU.mult).then_inc(z_used, 1)
                            if r == 3:
                                dve.wait_ge(u_psum, b + 1)
                                if b >= 1:
                                    dve.wait_ge(s_ready, b)
                                dve.tensor_tensor(um[:], ps[:, 2:4, 0:8 * E1],
                                                  bc(bdmask.unsqueeze(1), [P, 2, 8 * E1]), ALU.mult).then_inc(um_ready, 1)
                        if 1 <= n <= NB * NG:
                            dve.wait_ge(d_ready, n)
                            if n >= 3:
                                dve.wait_ge(y_psum, n - 2)
                            a = ps[:, 4 + (n - 1) % 2, 0:256].rearrange("p (f t) -> p f t", f=2)
                            dve.tensor_tensor(Mb[:, (n - 1) % 2].rearrange("p (f j) t -> p f j t", f=2),
                                              Db[:, (n - 1) % 2].rearrange("p (f j) t -> p f j t", f=2),
                                              bc(a.unsqueeze(2), [P, 2, 2, P]), ALU.mult).then_inc(m_done, 1)
                        if n >= 2 and (n - 2) % NG == NG - 1:
                            b = (n - 2) // NG
                            dve.wait_ge(y_psum, n - 1)
                            yp = ps[:, 0:2, 0:8 * E1].rearrange("p f (k e) -> p f k e", e=E1)
                            zb = zt[:, b % 2]
                            link(dve.tensor_tensor(zb, zb, yp, ALU.add))
                            link(dve.tensor_scalar(den[:, 0].rearrange("p (f k) -> p f k", f=2), zb[:, :, :, 32], 1e-6,
                                                   None, ALU.add))
                            link(dve.reciprocal(den[:, 1], den[:, 0]))
                            link(dve.tensor_tensor(den[:, 0], den[:, 1], wmix[:, b], ALU.mult))
                            dw = den[:, 0].rearrange("p (f k) -> p f k", f=2)
                            for j in range(2):
                                op = dve.tensor_tensor(yy[:, j].rearrange("p (f r) e -> p f r e", f=2),
                                                       zb[:, :, 4 * j:4 * j + 4, 0:32],
                                                       bc(dw[:, :, 4 * j:4 * j + 4].unsqueeze(3), [P, 2, 4, 32]), ALU.mult)
                            link(op)
                            dve.tensor_tensor(y[:, b].rearrange("p (h e) -> p h e", e=32), yy[:, 0], yy[:, 1], ALU.add
                                              ).then_inc(comb_done, 1)
                    dve.wait_ge(xnb_ready, 1)
                    for b in range(NB):
                        dve.wait_ge(out_psum, b + 1)
                        dve.tensor_tensor(xnb[:, b], xnb[:, b], ps[:, b, 0:D], ALU.add).then_inc(out_sum, 1)
                    dve.wait_ge(out_sum, NB)
                    layernorm(dve, link, [xnb[:, b, :] for b in range(NB)], [y[:, b, :] for b in range(NB)],
                              stats, mv, rs, ltmp)
                    link(dve.tensor_tensor(y[:], y[:], bc(lng.unsqueeze(1), [P, NB, D]), ALU.mult))
                    dve.wait_ge(hb_ready, 1)
                    dve.tensor_tensor(hc, y[:], hb[:], ALU.add)
            s.round_end()


def pick_top(dve, link, vals, k, v8, sel, eq, cum, cnt, ones):
    n, E = vals.shape[1], vals.shape[2]
    for i in range(n):
        op = dve.max(v8[:, i, :], vals[:, i, :])
    link(op)
    t = bc(v8[:, 0:n, k - 1:k], [P, n, E])
    dve.tensor_tensor(eq, vals, t, ALU.is_equal)
    link(dve.tensor_tensor(sel, vals, t, ALU.is_gt))
    dve.tensor_reduce(cnt[:, 0:n], sel, AX_X, ALU.add)
    for i in range(n):
        op = dve.tensor_tensor_scan(cum[:, i, :], ones[:, 0:E], eq[:, i, :], 0.0, ALU.mult, ALU.add)
    link(op)
    link(dve.tensor_tensor(cum, cum, bc(cnt[:, 0:n].unsqueeze(2), [P, n, E]), ALU.add))
    link(dve.tensor_scalar(cum, cum, float(k), None, ALU.is_le))
    link(dve.tensor_tensor(eq, eq, cum, ALU.mult))
    link(dve.tensor_tensor(sel, sel, eq, ALU.add))


def attn_project(nc, g):
    with Scope(nc) as s:
        wqk, wv = s.sb("ap_wqk", [P, 2, DC, D]), s.sb("ap_wv", [P, DC, D])
        rows = s.sb("ap_rows", [P, 3 * D])
        qkb = s.sb("ap_qkb", [P, 4])
        nx = s.sb("ap_nx", [P, NB, D])
        nxT = s.sb("ap_nxT", [P, DC, NB * P])
        res = s.sb("ap_res", [P, 4, NB * P])
        parts = s.sb("ap_parts", [P, 4, 3, NB * P], BF16)
        stats, mv, rs, ltmp = s.sb("ap_stats", [P, NB, 6]), s.sb("ap_mv", [P, NB, 2]), s.sb("ap_rs", [P, NB]), s.sb("ap_ltmp", [P, 2, NB])
        with Scope(nc) as u:
            loaded = u.sem("ap_loaded")
            with nc.Block() as block:
                @block.sync
                def _(sp):
                    for dst, n in ((wqk[:], "at_wqk"), (wv[:], "at_wv"), (rows[:], "at_rows"), (qkb[:], "at_qkb")):
                        sp.dma_start(dst, g.d[n]).then_inc(loaded, 16)
                    sp.wait_ge(loaded, 16 * 4)

                @block.vector
                def _(dve):
                    dve.memset(g.v[:], 1.0)
            u.round_end()
        vchain, nx_ready, nxT_psum, nxT_ready = s.sem("ap_vchain"), s.sem("ap_nx"), s.sem("ap_nxT_psum"), s.sem("ap_nxT")
        qk_psum, v_psum, res_ready, part_ready, stored = (s.sem("ap_qk_psum"), s.sem("ap_v_psum"), s.sem("ap_res_ready"),
                                                          s.sem("ap_part"), s.sem("ap_stored"))
        ps = g.ps
        with nc.Fori(0, NC) as c:
            hc = g.h[:, bass.ds(c, 1)].rearrange("p o b n -> p (o b) n")
            zc = g.z[:, bass.ds(c, 1)].rearrange("p o b n -> p (o b) n")
            vc = g.v[:, bass.ds(c, 1)].rearrange("p o b h e -> p (o b) h e")
            with nc.Block() as block:
                @block.tensor
                def _(pe):
                    pe.wait_ge(nx_ready, 1)
                    for d in range(DC):
                        for b in range(NB):
                            mm = pe.transpose(ps[:, d, b * P:(b + 1) * P], nx[:, b, d * P:(d + 1) * P], g.ident[:])
                    mm.then_inc(nxT_psum, 1)
                    pe.wait_ge(nxT_ready, 1)
                    for w in range(2):
                        for f in range(2):
                            for d in range(DC):
                                mm = pe.matmul(ps[:, 2 + 2 * w + f, :], wqk[:, w, d, f * P:(f + 1) * P], nxT[:, d, :],
                                               start=(d == 0), stop=(d == DC - 1))
                            mm.then_inc(qk_psum, 1)
                    for b in range(NB):
                        for d in range(DC):
                            mm = pe.matmul(ps[:, 6 + b // 2, (b % 2) * D:(b % 2 + 1) * D], nxT[:, d, b * P:(b + 1) * P],
                                           wv[:, d, :], start=(d == 0), stop=(d == DC - 1))
                        if b % 2:
                            mm.then_inc(v_psum, 1)

                @block.scalar
                def _(act):
                    act.wait_ge(nxT_psum, 1)
                    act.activation(nxT[:, 0, :], ps[:, 0, :], ACT.Copy)
                    act.activation(nxT[:, 1, :], ps[:, 1, :], ACT.Copy).then_inc(nxT_ready, 1)
                    for part in range(3):
                        for k in range(4):
                            act.wait_ge(res_ready, 4 * part + k + 1)
                            act.activation(parts[:, k, part, :], res[:, k, :], ACT.Copy).then_inc(part_ready, 1)

                @block.sync
                def _(sp):
                    sp.wait_ge(part_ready, 12)
                    for k in range(4):
                        for part in range(3):
                            dst = g.scr_qk[k // 2, part, (k % 2) * P:(k % 2 + 1) * P, :, bass.ds(c * P, P)]
                            sp.dma_start(dst, parts[:, k, part, :].rearrange("p (b t) -> p b t", b=NB)).then_inc(stored, 16)
                    sp.wait_ge(stored, 16 * 12)

                @block.vector
                def _(dve):
                    link = chain(dve, vchain)
                    layernorm(dve, link, [hc[:, b, :] for b in range(NB)], [zc[:, b, :] for b in range(NB)],
                              stats, mv, rs, ltmp)
                    layernorm(dve, link, [zc[:, b, :] for b in range(NB)], [nx[:, b, :] for b in range(NB)],
                              stats, mv, rs, ltmp)
                    link(dve.tensor_tensor(nx[:], nx[:], bc(rows[:, 0:D].unsqueeze(1), [P, NB, D]), ALU.mult))
                    dve.tensor_tensor(nx[:], nx[:], bc(rows[:, D:2 * D].unsqueeze(1), [P, NB, D]), ALU.add
                                      ).then_inc(nx_ready, 1)
                    for k in range(4):
                        dve.wait_ge(qk_psum, k + 1)
                        dve.tensor_scalar(res[:, k, :], ps[:, 2 + k, :], qkb[:, k:k + 1], 0.25 if k < 2 else 1.0,
                                          ALU.add, ALU.mult).then_inc(res_ready, 1)
                    for m in range(2):
                        dve.wait_ge(v_psum, m + 1)
                        dve.tensor_tensor(vc[:, 2 * m:2 * m + 2, :, 0:16],
                                          ps[:, 6 + m, :].rearrange("p (b h e) -> p b h e", b=2, h=16),
                                          bc(rows[:, 2 * D:3 * D].rearrange("p (h e) -> p h e", h=16).unsqueeze(1),
                                             [P, 2, 16, 16]), ALU.add)
                    for part in range(2):
                        for k in range(4):
                            dve.wait_ge(part_ready, 4 * part + k + 1)
                            dve.tensor_tensor(res[:, k, :], res[:, k, :], parts[:, k, part, :], ALU.subtract
                                              ).then_inc(res_ready, 1)
            s.round_end()


def attn_heads(nc, g):
    NH, E = 16, 16
    KT, QT = (0, 1, 0, 2, 0, 1), (0, 0, 1, 0, 2, 1)
    blocks = [(kb, qc) for kb in range(NC) for qc in range(kb, NC)]
    at = {kq: i for i, kq in enumerate(blocks)}
    cuts = [0, 4, 8, 12, 15, 18, 21]
    pieces = []
    for a, z in zip(cuts, cuts[1:]):
        runs = []
        for i in range(a, z):
            kb, qc = blocks[i]
            if runs and runs[-1][0] == kb:
                runs[-1][2] += 1
            else:
                runs.append([kb, qc, 1, i - a])
        pieces.append((a, z - a, runs))
    NPC = len(pieces)
    with Scope(nc) as s:
        k6, q6 = s.sb("ah_k6", [96, NH, SEQ], BF16), s.sb("ah_q6", [96, NH, SEQ], BF16)
        vb = s.sb("ah_v", [P, NC, NH, E + 1])
        probs = s.sb("ah_probs", [P, 2, len(blocks) * P])
        consts = s.sb("ah_consts", [P, 4 * P], BF16)
        mx = s.sb("ah_max", [P, 2, NC])
        mres = s.sb("ah_mres", [P, NC])
        msp = s.sb("ah_msplit", [P, 2, NC, 4], BF16)
        mrow = s.sb("ah_mrow", [3, 2, SEQ], BF16)
        rden = s.sb("ah_rden", [P, NC])
        identb, qmask, kmask, minus = (consts[:, i * P:(i + 1) * P] for i in range(4))
        with Scope(nc) as u:
            loaded = u.sem("ah_loaded")
            with nc.Block() as block:
                @block.sync
                def _(sp):
                    sp.dma_start(consts[:], g.d["at_consts"]).then_inc(loaded, 16)
                    sp.wait_ge(loaded, 16)
            u.round_end()
        qk_loaded = [s.sem(f"ah_qk_loaded{i}") for i in range(4)]
        vchain, v_ready, s_psum, s_used, msp_ready, mT_psum, mT_ready, e_psum, e_done, o_psum, o_used = (
            s.sem("ah_" + n) for n in "vchain v_ready s_psum s_used msp_ready mT_psum mT_ready e_psum e_done o_psum o_used".split())
        ps = g.ps
        with nc.Fori(0, NB) as b:
            with nc.Block() as block:
                @block.sync
                def _(sp):
                    for hq in range(4):
                        for t in range(6):
                            for w, dst, part in ((0, q6, QT[t]), (1, k6, KT[t])):
                                src = g.scr_qk[w, part, 64 * hq:64 * hq + 64, bass.ds(b, 1), :]
                                sp.dma_start(dst[16 * t:16 * t + 16, 4 * hq:4 * hq + 4, :],
                                             src.rearrange("(h e) o s -> e h (o s)", e=E)).then_inc(qk_loaded[hq], 16)

                @block.gpsimd
                def _(pool):
                    pool.tensor_copy(vb[:], g.v[:, :, bass.ds(b, 1)].rearrange("p c o h e -> p c (o h) e")
                                     ).then_inc(v_ready, 1)

                @block.tensor
                def _(pe):
                    pe.wait_ge(v_ready, 1)
                    for i in range(NH + 3):
                        if i < NH:
                            if i % 4 == 0:
                                pe.wait_ge(qk_loaded[i // 4], 16 * 12)
                            for qc in range(NC):
                                n = i * NC + qc
                                bank = 2 * (n % 2)
                                if n >= 2:
                                    pe.wait_ge(s_used, n - 1)
                                k1 = min((qc + 1) * P, 512)
                                lhs = q6[:, i, qc * P:(qc + 1) * P]
                                pe.matmul(ps[:, bank, 0:k1], lhs, k6[:, i, 0:k1], start=True, stop=qc > 3)
                                if qc > 3:
                                    k2 = (qc + 1) * P
                                    pe.matmul(ps[:, bank + 1, 0:k2 - 512], lhs, k6[:, i, 512:k2], start=True, stop=False)
                                dk = (qc % 4) * P
                                pe.matmul(ps[:, bank + qc // 4, dk:dk + P], identb, qmask, start=False, stop=True
                                          ).then_inc(s_psum, 1)
                        if 1 <= i <= NH:
                            h = i - 1
                            pe.wait_ge(msp_ready, h + 1)
                            if h >= 1:
                                pe.wait_ge(mT_ready, h)
                            for qc in range(NC):
                                mm = pe.transpose(ps[0:3, 7, :].bitcast(BF16)[:, qc * P:(qc + 1) * P],
                                                  msp[:, h % 2, qc, 0:3], identb)
                            mm.then_inc(mT_psum, 1)
                        if 2 <= i <= NH + 1:
                            h = i - 2
                            pe.wait_ge(mT_ready, h + 1)
                            for p, (first, nb, runs) in enumerate(pieces):
                                n = h * NPC + p
                                bank = 4 + n % 2
                                if n >= 2:
                                    pe.wait_ge(e_done, n - 1)
                                for kb, qc, m, off in runs:
                                    o, w = ps[:, bank, off * P:(off + m) * P], slice(qc * P, (qc + m) * P)
                                    pe.matmul(o, k6[:, h, kb * P:(kb + 1) * P], q6[:, h, w], start=True, stop=False)
                                    mm = pe.matmul(o, minus[0:3, :], mrow[:, h % 2, w], start=False, stop=qc != kb)
                                    if qc == kb:
                                        mm = pe.matmul(ps[:, bank, off * P:(off + 1) * P], identb, kmask,
                                                       start=False, stop=True)
                                mm.then_inc(e_psum, 1)
                        if i >= 3:
                            h = i - 3
                            pe.wait_ge(e_done, NPC * (h + 1))
                            if h >= 1:
                                pe.wait_ge(o_used, h)
                            for qc in range(NC):
                                for kb in range(qc + 1):
                                    j = at[kb, qc]
                                    mm = pe.matmul(ps[:, 6, qc * (E + 1):(qc + 1) * (E + 1)],
                                                   probs[:, h % 2, j * P:(j + 1) * P], vb[:, kb, h, :],
                                                   start=(kb == 0), stop=(kb == qc))
                            mm.then_inc(o_psum, 1)

                @block.scalar
                def _(act):
                    for h in range(NH):
                        for p, (first, nb, runs) in enumerate(pieces):
                            act.wait_ge(e_psum, h * NPC + p + 1)
                            if p == 0 and h >= 2:
                                act.wait_ge(o_psum, h - 1)
                            act.activation(probs[:, h % 2, first * P:(first + nb) * P], ps[:, 4 + (h * NPC + p) % 2, 0:nb * P],
                                           ACT.Exp).then_inc(e_done, 1)

                @block.vector
                def _(dve):
                    link = chain(dve, vchain)
                    for i in range(NH + 3):
                        if i < NH:
                            for qc in range(NC):
                                n = i * NC + qc
                                dve.wait_ge(s_psum, n + 1)
                                src = ps[:, 2 * (n % 2):2 * (n % 2) + 2, :].rearrange("p k n -> p (k n)")
                                dve.tensor_reduce(mx[:, i % 2, qc:qc + 1], src[:, 0:(qc + 1) * P], AX_X, ALU.max
                                                  ).then_inc(s_used, 1)
                            dve.wait_ge(s_used, NC * (i + 1))
                            if i >= 2:
                                dve.wait_ge(mT_psum, i - 1)
                            mp, m = msp[:, i % 2], mx[:, i % 2]
                            link(dve.tensor_copy(mp[:, :, 0], m))
                            link(dve.tensor_tensor(mres[:], m, mp[:, :, 0], ALU.subtract))
                            link(dve.tensor_copy(mp[:, :, 1], mres[:]))
                            link(dve.tensor_tensor(mres[:], mres[:], mp[:, :, 1], ALU.subtract))
                            dve.tensor_copy(mp[:, :, 2], mres[:]).then_inc(msp_ready, 1)
                        if 1 <= i <= NH:
                            h = i - 1
                            dve.wait_ge(mT_psum, h + 1)
                            if h >= 2:
                                dve.wait_ge(e_psum, NPC * (h - 1))
                            dve.tensor_copy(mrow[:, h % 2, :], ps[0:3, 7, :].bitcast(BF16)[:, 0:SEQ]).then_inc(mT_ready, 1)
                        if i >= 3:
                            h = i - 3
                            dve.wait_ge(o_psum, h + 1)
                            o = ps[:, 6, 0:NC * (E + 1)].rearrange("p (c e) -> p c e", e=E + 1)
                            link(dve.reciprocal(rden[:], o[:, :, E]))
                            dve.tensor_tensor(g.a[:, :, bass.ds(b, 1), h * E:(h + 1) * E].rearrange("p c o e -> p c (o e)"),
                                              o[:, :, 0:E], bc(rden[:].unsqueeze(2), [P, NC, E]), ALU.mult).then_inc(o_used, 1)
            s.round_end()


def attn_finish(nc, g):
    NE = 8
    with Scope(nc) as s:
        wo, gw = s.sb("af_wo", [P, DC, D]), s.sb("af_gw", [P, DC, NE])
        rows = s.sb("af_rows", [P, 3 * D])
        b2 = s.sb("af_b2", [NE, D])
        x1, nx = s.sb("af_x1", [P, NB, D]), s.sb("af_nx", [P, NB, D])
        aT, nT = s.sb("af_aT", [P, DC, NB * P]), s.sb("af_nT", [P, DC, NB * P])
        lg, sel, eq, cum = (s.sb("af_" + n, [P, NB, NE]) for n in ("lg", "sel", "eq", "cum"))
        gt = s.sb("af_gates", [P, NB, NE])
        v8, cnt = s.sb("af_v8", [P, NB, 8]), s.sb("af_cnt", [P, NB])
        gT = s.sb("af_gT", [NE, NB * P])
        ones = s.sb("af_ones", [P, 32])
        stats, mv, rs, ltmp = s.sb("af_stats", [P, NB, 6]), s.sb("af_mv", [P, NB, 2]), s.sb("af_rs", [P, NB]), s.sb("af_ltmp", [P, 2, NB])
        with Scope(nc) as u:
            loaded = u.sem("af_loaded")
            with nc.Block() as block:
                @block.sync
                def _(sp):
                    for dst, n in ((wo[:], "at_wo"), (gw[:], "m0_gate"), (rows[:], "af_rows"), (b2[:], "m0_b2")):
                        sp.dma_start(dst, g.d[n]).then_inc(loaded, 16)
                    sp.wait_ge(loaded, 16 * 4)

                @block.vector
                def _(dve):
                    dve.memset(ones[:], 1.0)
            u.round_end()
        (vchain, aT_psum, aT_ready, out_psum, zb_ready, x1_ready, h_added, nx_ready, nT_psum, nT_ready, lg_psum, lg_ready,
         e_ready, g_ready, gT_psum, gT_ready, bias_psum, xT_ready) = (s.sem("af_" + n) for n in (
             "vchain aT_psum aT_ready out_psum zb_ready x1_ready h_added nx_ready nT_psum nT_ready lg_psum lg_ready "
             "e_ready g_ready gT_psum gT_ready bias_psum xT_ready").split())
        ps = g.ps
        with nc.Fori(0, NC) as c:
            def at_c(t):
                return t[:, bass.ds(c, 1)].rearrange("p o b n -> p (o b) n")
            hc, zc, ac, gc = at_c(g.h), at_c(g.z), at_c(g.a), at_c(g.gates0)
            with nc.Block() as block:
                @block.tensor
                def _(pe):
                    pe.wait_ge(nx_ready, 1)
                    for d in range(DC):
                        for b in range(NB):
                            mm = pe.transpose(ps[:, d, b * P:(b + 1) * P], nx[:, b, d * P:(d + 1) * P], g.ident[:])
                    mm.then_inc(aT_psum, 1)
                    pe.wait_ge(aT_ready, 1)
                    for b in range(NB):
                        for d in range(DC):
                            mm = pe.matmul(ps[:, 2 + b, 0:D], aT[:, d, b * P:(b + 1) * P], wo[:, d, :],
                                           start=(d == 0), stop=(d == DC - 1))
                        mm.then_inc(out_psum, 1)
                    pe.wait_ge(nx_ready, 2)
                    for d in range(DC):
                        for b in range(NB):
                            mm = pe.transpose(ps[:, d, b * P:(b + 1) * P], nx[:, b, d * P:(d + 1) * P], g.ident[:])
                    mm.then_inc(nT_psum, 1)
                    pe.wait_ge(nT_ready, 1)
                    for b in range(NB):
                        for d in range(DC):
                            mm = pe.matmul(ps[:, 6, b * NE:(b + 1) * NE], nT[:, d, b * P:(b + 1) * P], gw[:, d, :],
                                           start=(d == 0), stop=(d == DC - 1))
                    mm.then_inc(lg_psum, 1)
                    pe.wait_ge(g_ready, 1)
                    for b in range(NB):
                        mm = pe.transpose(ps[0:NE, 7, b * P:(b + 1) * P], gt[:, b, :], g.ident[:])
                    mm.then_inc(gT_psum, 1)
                    pe.wait_ge(gT_ready, 1)
                    for b in range(NB):
                        mm = pe.matmul(ps[:, 2 + b, 0:D], gT[:, b * P:(b + 1) * P], b2[:], start=True, stop=True)
                    mm.then_inc(bias_psum, 1)

                @block.scalar
                def _(act):
                    act.wait_ge(aT_psum, 1)
                    act.activation(aT[:, 0, :], ps[:, 0, :], ACT.Copy)
                    act.activation(aT[:, 1, :], ps[:, 1, :], ACT.Copy).then_inc(aT_ready, 1)
                    act.wait_ge(nT_psum, 1)
                    act.activation(nT[:, 0, :], ps[:, 0, :], ACT.Copy)
                    act.activation(nT[:, 1, :], ps[:, 1, :], ACT.Copy).then_inc(nT_ready, 1)
                    act.wait_ge(lg_ready, 1)
                    act.activation(gt[:], lg[:], ACT.Exp).then_inc(e_ready, 1)
                    act.wait_ge(gT_psum, 1)
                    act.activation(gT[:], ps[0:NE, 7, :], ACT.Copy).then_inc(gT_ready, 1)

                @block.gpsimd
                def _(pool):
                    pool.tensor_copy(nx[:], ac).then_inc(nx_ready, 1)
                    pool.tensor_tensor(x1[:], zc, bc(rows[:, 0:D].unsqueeze(1), [P, NB, D]), ALU.add).then_inc(zb_ready, 1)
                    pool.wait_ge(x1_ready, NB)
                    pool.tensor_tensor(hc, hc, x1[:], ALU.add).then_inc(h_added, 1)
                    pool.wait_ge(nT_ready, 1)
                    pool.tensor_copy(g.xT[:, :, bass.ds(c, 1), :].rearrange("p d o n -> p d (o n)"), nT[:]).then_inc(xT_ready, 1)

                @block.vector
                def _(dve):
                    link = chain(dve, vchain)
                    dve.wait_ge(zb_ready, 1)
                    for b in range(NB):
                        dve.wait_ge(out_psum, b + 1)
                        dve.tensor_tensor(x1[:, b], x1[:, b], ps[:, 2 + b, 0:D], ALU.add).then_inc(x1_ready, 1)
                    dve.wait_ge(x1_ready, NB)
                    dve.wait_ge(aT_psum, 1)
                    layernorm(dve, link, [x1[:, b, :] for b in range(NB)], [nx[:, b, :] for b in range(NB)],
                              stats, mv, rs, ltmp)
                    link(dve.tensor_tensor(nx[:], nx[:], bc(rows[:, D:2 * D].unsqueeze(1), [P, NB, D]), ALU.mult))
                    dve.tensor_tensor(nx[:], nx[:], bc(rows[:, 2 * D:3 * D].unsqueeze(1), [P, NB, D]), ALU.add
                                      ).then_inc(nx_ready, 1)
                    dve.wait_ge(lg_psum, 1)
                    link(dve.tensor_copy(lg[:].rearrange("p b e -> p (b e)"), ps[:, 6, 0:NB * NE]))
                    pick_top(dve, link, lg[:], 2, v8[:], sel[:], eq[:], cum[:], cnt[:], ones[:])
                    dve.tensor_tensor(lg[:], lg[:], bc(v8[:, :, 0:1], [P, NB, NE]), ALU.subtract).then_inc(lg_ready, 1)
                    dve.wait_ge(e_ready, 1)
                    link(dve.tensor_tensor(lg[:], gt[:], sel[:], ALU.mult))
                    link(dve.tensor_reduce(cnt[:], lg[:], AX_X, ALU.add))
                    link(dve.reciprocal(cnt[:], cnt[:]))
                    dve.tensor_tensor(gt[:], lg[:], bc(cnt[:].unsqueeze(2), [P, NB, NE]), ALU.mult).then_inc(g_ready, 1)
                    dve.wait_ge(g_ready, 1)
                    dve.tensor_copy(gc, gt[:])
                    dve.wait_ge(bias_psum, 1)
                    dve.wait_ge(h_added, 1)
                    dve.tensor_tensor(hc, hc, ps[:, 2:6, 0:D], ALU.add)
            s.round_end()


def moe_gelu(nc, g):
    NE, F = 8, 1024
    FC = F // P
    with Scope(nc) as s:
        w1, w2 = s.sb("mg_w1", [P, 2, DC, F]), s.sb("mg_w2", [P, 2, FC, D])
        b1 = s.sb("mg_b1", [P, 2, FC])
        hT = s.sb("mg_hT", [P, 2, FC, 512])
        def load(sp, slot, e, sem):
            sp.dma_start(w1[:, slot], g.d["m0_w1"][bass.ds(e, 1)].rearrange("o p d f -> p (o d) f")).then_inc(sem, 16)
            sp.dma_start(w2[:, slot], g.d["m0_w2"][bass.ds(e, 1)].rearrange("o p f n -> p (o f) n")).then_inc(sem, 16)
            sp.dma_start(b1[:, slot], g.d["m0_b1"][bass.ds(e, 1)].rearrange("o p f -> p (o f)")).then_inc(sem, 16)
        with Scope(nc) as u:
            loaded = u.sem("mg_loaded")
            with nc.Block() as block:
                @block.sync
                def _(sp):
                    load(sp, 0, 0, loaded)
                    sp.wait_ge(loaded, 48)
            u.round_end()
        loaded1, loaded0, h_psum, h_ready, y_psum, y_used, gp = (s.sem("mg_" + n) for n in (
            "loaded1", "loaded0", "h_psum", "h_ready", "y_psum", "y_used", "gate_picked"))
        gpair = s.sb("mg_gates", [P, 2, NC, NB])
        ps = g.ps
        NR = 2 * NC
        with nc.Fori(0, NE // 2) as r:
            e = r * 2
            with nc.Block() as block:
                @block.sync
                def _(sp):
                    load(sp, 1, e + 1, loaded1)
                    sp.wait_ge(y_psum, NB * NC)
                    sp.wait_ge(h_ready, FC * NC)
                    load(sp, 0, e + 2, loaded0)
                    sp.wait_ge(loaded1, 48)
                    sp.wait_ge(loaded0, 48)

                @block.tensor
                def _(pe):
                    for n in range(NR + 1):
                        if n < NR:
                            slot, c = divmod(n, NC)
                            if n == NC:
                                pe.wait_ge(loaded1, 48)
                            for f in range(FC):
                                k = n * FC + f
                                if k >= 4:
                                    pe.wait_ge(h_ready, k - 3)
                                for d in range(DC):
                                    mm = pe.matmul(ps[:, k % 4, :], w1[:, slot, d, f * P:(f + 1) * P], g.xT[:, d, c, :],
                                                   start=(d == 0), stop=(d == DC - 1))
                                mm.then_inc(h_psum, 1)
                        if n >= 1:
                            slot, c = divmod(n - 1, NC)
                            pe.wait_ge(h_ready, FC * n)
                            for b in range(NB):
                                k = (n - 1) * NB + b
                                if k >= 4:
                                    pe.wait_ge(y_used, k - 3)
                                for f in range(FC):
                                    mm = pe.matmul(ps[:, 4 + k % 4, 0:D], hT[:, (n - 1) % 2, f, b * P:(b + 1) * P],
                                                   w2[:, slot, f, :], start=(f == 0), stop=(f == FC - 1))
                                mm.then_inc(y_psum, 1)

                @block.scalar
                def _(act):
                    for n in range(NR):
                        slot = n // NC
                        if n == NC:
                            act.wait_ge(loaded1, 48)
                        if n >= 2:
                            act.wait_ge(y_psum, NB * (n - 1))
                        for f in range(FC):
                            act.wait_ge(h_psum, n * FC + f + 1)
                            act.activation(hT[:, n % 2, f, :], ps[:, (n * FC + f) % 4, :], ACT.Gelu,
                                           bias=b1[:, slot, f:f + 1]).then_inc(h_ready, 1)

                @block.vector
                def _(dve):
                    for k in range(2):
                        op = dve.tensor_copy(gpair[:, k], g.gates0[:, :, :, bass.ds(e + k, 1)].rearrange("p c b o -> p c (b o)"))
                    op.then_inc(gp, 1)
                    dve.wait_ge(gp, 1)
                    for n in range(NR):
                        slot, c = divmod(n, NC)
                        for b in range(NB):
                            k = n * NB + b
                            dve.wait_ge(y_psum, k + 1)
                            if n >= NC and b == 0:
                                dve.wait_ge(y_used, k - NB * NC + NB)
                            dve.scalar_tensor_tensor(g.h[:, c, b, :], ps[:, 4 + k % 4, 0:D], gpair[:, slot, c, b:b + 1],
                                                     g.h[:, c, b, :], ALU.mult, ALU.add).then_inc(y_used, 1)
            s.round_end()


def layer0_ffn(nc, g):
    with Scope(nc) as s:
        g.gates0 = s.sb("gates0", [P, NC, NB, 8])
        g.xT = s.sb("l0_xT", [P, DC, NC, NB * P])
        with Scope(nc) as t:
            g.z, g.a = t.sb("l0_z", [P, NC, NB, D]), t.sb("l0_a", [P, NC, NB, D])
            g.v = t.sb("l0_v", [P, NC, NB, 16, 17])
            attn_project(nc, g)
            attn_heads(nc, g)
            attn_finish(nc, g)
        moe_gelu(nc, g)


def time_mix(nc, g):
    NE = 8
    with Scope(nc) as s:
        wk, wo, rw = s.sb("tm_wkvr", [P, 3, DC, D]), s.sb("tm_wo", [P, DC, D]), s.sb("tm_router", [P, DC, NE])
        rows, cols = s.sb("tm_rows", [P, 4 * D]), s.sb("tm_cols", [P, 5, DC])
        hn, xn = s.sb("tm_hn", [P, NC, D]), s.sb("tm_xn", [P, NC, D])
        xT, dT = s.sb("tm_xT", [P, DC, SEQ + 1]), s.sb("tm_dT", [P, DC, SEQ])
        mix = s.sb("tm_mix", [P, 3, DC, SEQ])
        kk, vv, rr = s.sb("tm_k", [P, DC, SEQ]), s.sb("tm_v", [P, DC, SEQ]), s.sb("tm_r", [P, DC, SEQ])
        pp, aa, bb = (s.sb("tm_" + n, [P, DC, SEQ + 1]) for n in ("pp", "aa", "bb"))
        t = s.sb("tm_t", [P, 4, DC, SEQ])
        lg, pr, sel, eq, cum = (s.sb("tm_" + n, [P, NC, NE]) for n in ("lg", "pr", "sel", "eq", "cum"))
        v8, cnt = s.sb("tm_v8", [P, NC, 8]), s.sb("tm_cnt", [P, NC])
        ones = s.sb("tm_ones", [P, 32])
        stats, mv, rs, ltmp = s.sb("tm_stats", [P, NC, 6]), s.sb("tm_mv", [P, NC, 2]), s.sb("tm_rs", [P, NC]), s.sb("tm_ltmp", [P, 2, NC])
        with Scope(nc) as u:
            loaded, decay, dchain = u.sem("tm_loaded"), u.sem("tm_decay"), u.sem("tm_dchain")
            with nc.Block() as block:
                @block.sync
                def _(sp):
                    for dst, n in ((wk[:], "tm_wkvr"), (wo[:], "tm_wo"), (rw[:], "m1_router"), (rows[:], "tm_rows"),
                                   (cols[:], "tm_cols")):
                        sp.dma_start(dst, g.d[n]).then_inc(loaded, 16)
                    sp.wait_ge(loaded, 16 * 5)

                @block.scalar
                def _(act):
                    act.wait_ge(loaded, 16 * 5)
                    act.activation(cols[:, 3], cols[:, 3], ACT.Exp).then_inc(decay, 1)

                @block.vector
                def _(dve):
                    dve.memset(ones[:], 1.0)
                    dve.memset(xT[:, :, 0:1], 0.0)
                    dve.memset(pp[:, :, 0:1], -1e30)
                    dve.memset(aa[:, :, 0:1], 0.0)
                    dve.memset(bb[:, :, 0:1], 0.0)
                    dve.wait_ge(decay, 1)
                    dve.tensor_scalar(cols[:, 3], cols[:, 3], -1.0, None, ALU.mult)
            u.round_end()
        (vchain, xn_ready, xT_psum, xT_ready, mix_ready, p_psum, p_used, exp_arg, exp_done, y_ready, out_psum, x2_ready,
         ei_ready, eT_psum, eT_ready, lg_psum, sm_arg, sm_done, pool_ready, dT_ready, e_stored, tchain) = (
             s.sem("tm_" + n) for n in (
                 "vchain xn_ready xT_psum xT_ready mix_ready p_psum p_used exp_arg exp_done y_ready out_psum x2_ready "
                 "ei_ready eT_psum eT_ready lg_psum sm_arg sm_done pool_ready dT_ready e_stored pchain").split())
        ps = g.ps
        two = [ps[:, 2 * i:2 * i + 2, :].rearrange("p k n -> p (k n)") for i in range(4)]
        proj = [(w, f) for w in range(3) for f in range(2)]
        pair = [2, 3, 0, 1, 2, 3]
        prev, cur = slice(0, SEQ), slice(1, SEQ + 1)
        with nc.Fori(0, NB) as b:
            hb = g.h[:, :, bass.ds(b, 1)].rearrange("p c o n -> p c (o n)")
            with nc.Block() as block:
                @block.tensor
                def _(pe):
                    pe.wait_ge(xn_ready, 1)
                    for d in range(DC):
                        for c in range(NC):
                            mm = pe.transpose(two[d][:, c * P:(c + 1) * P], xn[:, c, d * P:(d + 1) * P], g.ident[:])
                    mm.then_inc(xT_psum, 1)
                    for i, (w, f) in enumerate(proj):
                        if f == 0:
                            pe.wait_ge(mix_ready, w + 1)
                        if i == 2:
                            pe.wait_ge(xT_ready, 1)
                        if i >= 4:
                            pe.wait_ge(p_used, i - 3)
                        for lo, hi in ((0, 512), (512, SEQ)):
                            for d in range(DC):
                                mm = pe.matmul(two[pair[i]][:, lo:hi], wk[:, w, d, f * P:(f + 1) * P],
                                               mix[:, w, d, lo:hi], start=(d == 0), stop=(d == DC - 1))
                        mm.then_inc(p_psum, 1)
                    pe.wait_ge(y_ready, 1)
                    for c in range(NC):
                        for f in range(2):
                            mm = pe.matmul(ps[:, c // 2, (c % 2) * D:(c % 2 + 1) * D], rr[:, f, c * P:(c + 1) * P],
                                           wo[:, f, :], start=(f == 0), stop=(f == 1))
                        if c % 2:
                            mm.then_inc(out_psum, 1)
                    pe.wait_ge(ei_ready, 1)
                    for d in range(DC):
                        for c in range(NC):
                            mm = pe.transpose(two[2 + d][:, c * P:(c + 1) * P], xn[:, c, d * P:(d + 1) * P], g.ident[:])
                    mm.then_inc(eT_psum, 1)
                    pe.wait_ge(eT_ready, 1)
                    for c in range(NC):
                        for d in range(DC):
                            mm = pe.matmul(ps[:, 3, c * NE:(c + 1) * NE], xT[:, d, 1 + c * P:1 + (c + 1) * P], rw[:, d, :],
                                           start=(d == 0), stop=(d == DC - 1))
                    mm.then_inc(lg_psum, 1)

                @block.scalar
                def _(act):
                    act.wait_ge(xT_psum, 1)
                    act.activation(xT[:, 0, cur], two[0][:, 0:SEQ], ACT.Copy)
                    act.activation(xT[:, 1, cur], two[1][:, 0:SEQ], ACT.Copy).then_inc(xT_ready, 1)
                    for i, (w, f) in enumerate(proj):
                        act.wait_ge(p_psum, i + 1)
                        src, dst = two[pair[i]][:, 0:SEQ], (kk, vv, rr)[w][:, f, :]
                        if w < 2:
                            act.activation(dst, src, ACT.Copy).then_inc(p_used, 1)
                        else:
                            act.activation(dst, src, ACT.Sigmoid).then_inc(p_used, 1)
                    for i in range(2):
                        act.wait_ge(exp_arg, i + 1)
                        act.activation(t[:, 2 * i:2 * i + 2], t[:, 2 * i:2 * i + 2], ACT.Exp).then_inc(exp_done, 1)
                    act.wait_ge(eT_psum, 1)
                    act.activation(xT[:, 0, cur], two[2][:, 0:SEQ], ACT.Copy)
                    act.activation(xT[:, 1, cur], two[3][:, 0:SEQ], ACT.Copy).then_inc(eT_ready, 1)
                    act.wait_ge(sm_arg, 1)
                    act.activation(pr[:], lg[:], ACT.Exp).then_inc(sm_done, 1)

                @block.gpsimd
                def _(pool):
                    pool.wait_ge(x2_ready, 1)
                    pool.tensor_tensor(hb, hb, hn[:], ALU.add).then_inc(pool_ready, 1)
                    pool.wait_ge(eT_ready, 1)
                    pool.tensor_copy(g.eT[:, :, bass.ds(b, 1), cur].rearrange("p d o n -> p d (o n)"), xT[:, :, cur]
                                     ).then_inc(e_stored, 1)
                    pool.tensor_tensor(g.dT[:, :, bass.ds(b, 1), :].rearrange("p d o n -> p d (o n)"), xT[:, :, cur],
                                       xT[:, :, prev], ALU.subtract).then_inc(dT_ready, 1)

                @block.vector
                def _(dve):
                    link = chain(dve, vchain)
                    tiles = [hb[:, c, :] for c in range(NC)]
                    hns, xns = [hn[:, c, :] for c in range(NC)], [xn[:, c, :] for c in range(NC)]
                    row = [bc(rows[:, i * D:(i + 1) * D].unsqueeze(1), [P, NC, D]) for i in range(4)]
                    layernorm(dve, link, tiles, hns, stats, mv, rs, ltmp)
                    layernorm(dve, link, hns, xns, stats, mv, rs, ltmp)
                    link(dve.tensor_tensor(xn[:], xn[:], row[0], ALU.mult))
                    dve.tensor_tensor(xn[:], xn[:], row[1], ALU.add).then_inc(xn_ready, 1)
                    dve.wait_ge(xT_ready, 1)
                    link(dve.tensor_tensor(dT[:], xT[:, :, cur], xT[:, :, prev], ALU.subtract))
                    for w in range(3):
                        for d in range(DC):
                            op = dve.scalar_tensor_tensor(mix[:, w, d, :], dT[:, d, :], cols[:, w, d:d + 1], xT[:, d, prev],
                                                          ALU.mult, ALU.add)
                        op.then_inc(mix_ready, 1)
                    dve.wait_ge(p_used, 2)
                    for f in range(2):
                        op = dve.tensor_tensor_scan(pp[:, f, cur], bc(cols[:, 3, f:f + 1], [P, SEQ]), kk[:, f, :], -1e30,
                                                    ALU.add, ALU.max)
                    link(op)
                    for f in range(2):
                        dve.tensor_scalar(t[:, 0, f, :], pp[:, f, prev], cols[:, 3, f:f + 1], None, ALU.add)
                        op = dve.tensor_scalar(t[:, 3, f, :], kk[:, f, :], cols[:, 4, f:f + 1], None, ALU.add)
                    link(op)
                    dve.tensor_tensor(t[:, 0], t[:, 0], pp[:, :, cur], ALU.subtract)
                    dve.tensor_tensor(t[:, 1], kk[:], pp[:, :, cur], ALU.subtract).then_inc(exp_arg, 1)
                    link(dve.tensor_tensor(t[:, 2], t[:, 3], pp[:, :, prev], ALU.max))
                    link(dve.tensor_tensor(t[:, 3], t[:, 3], t[:, 2], ALU.subtract))
                    dve.tensor_tensor(t[:, 2], pp[:, :, prev], t[:, 2], ALU.subtract).then_inc(exp_arg, 1)
                    dve.wait_ge(exp_done, 1)
                    dve.wait_ge(p_used, 4)
                    link(dve.tensor_tensor(kk[:], t[:, 1], vv[:], ALU.mult))
                    for f in range(2):
                        dve.tensor_tensor_scan(aa[:, f, cur], t[:, 0, f, :], kk[:, f, :], 0.0, ALU.mult, ALU.add)
                        op = dve.tensor_tensor_scan(bb[:, f, cur], t[:, 0, f, :], t[:, 1, f, :], 0.0, ALU.mult, ALU.add)
                    link(op)
                    dve.wait_ge(exp_done, 2)
                    dve.wait_ge(p_used, 6)
                    dve.tensor_tensor(t[:, 0], t[:, 2], aa[:, :, prev], ALU.mult)
                    dve.tensor_tensor(vv[:], t[:, 3], vv[:], ALU.mult)
                    link(dve.tensor_tensor(t[:, 1], t[:, 2], bb[:, :, prev], ALU.mult))
                    dve.tensor_tensor(t[:, 0], t[:, 0], vv[:], ALU.add)
                    link(dve.tensor_tensor(t[:, 1], t[:, 1], t[:, 3], ALU.add))
                    dve.tensor_tensor(rr[:], rr[:], t[:, 0], ALU.mult)
                    link(dve.reciprocal(t[:, 1], t[:, 1]))
                    dve.tensor_tensor(rr[:], rr[:], t[:, 1], ALU.mult).then_inc(y_ready, 1)
                    for m in range(NC // 2):
                        dve.wait_ge(out_psum, m + 1)
                        op = dve.tensor_tensor(hn[:, 2 * m:2 * m + 2], hn[:, 2 * m:2 * m + 2],
                                               ps[:, m, :].rearrange("p (c n) -> p c n", c=2), ALU.add)
                    op.then_inc(x2_ready, 1)
                    dve.wait_ge(x2_ready, 1)
                    layernorm(dve, link, hns, xns, stats, mv, rs, ltmp)
                    link(dve.tensor_tensor(xn[:], xn[:], row[2], ALU.mult))
                    dve.tensor_tensor(xn[:], xn[:], row[3], ALU.add).then_inc(ei_ready, 1)
                    dve.wait_ge(lg_psum, 1)
                    link(dve.tensor_copy(lg[:].rearrange("p c e -> p (c e)"), ps[:, 3, 0:NC * NE]))
                    link(dve.tensor_reduce(cnt[:], lg[:], AX_X, ALU.max))
                    dve.tensor_tensor(lg[:], lg[:], bc(cnt[:].unsqueeze(2), [P, NC, NE]), ALU.subtract).then_inc(sm_arg, 1)
                    dve.wait_ge(sm_done, 1)

                    def normalise(dst, src):
                        link(dve.tensor_reduce(cnt[:], src, AX_X, ALU.add))
                        link(dve.reciprocal(cnt[:], cnt[:]))
                        link(dve.tensor_tensor(dst, src, bc(cnt[:].unsqueeze(2), [P, NC, NE]), ALU.mult))
                    normalise(pr[:], pr[:])
                    pick_top(dve, link, pr[:], 2, v8[:], sel[:], eq[:], cum[:], cnt[:], ones[:])
                    link(dve.tensor_tensor(lg[:], pr[:], sel[:], ALU.mult))
                    normalise(g.gates1[:, :, bass.ds(b, 1), :].rearrange("p c o e -> p c (o e)"), lg[:])
            s.round_end()


def moe_channel_mix(nc, g):
    NE, F = 8, 512
    FC, T3 = F // P, 3
    BT = T3 * P
    with Scope(nc) as s:
        wk, wv, wr = s.sb("mc_wk", [P, 2, DC, F]), s.sb("mc_wv", [P, 2, FC, D]), s.sb("mc_wr", [P, 2, DC, D])
        mu = s.sb("mc_mu", [P, 2, 2 * DC])
        xk, xr = s.sb("mc_xk", [P, 2, DC, BT]), s.sb("mc_xr", [P, 2, DC, BT])
        rl, kk = s.sb("mc_relu", [P, 2, FC, BT]), s.sb("mc_k", [P, 2, FC, BT])
        sg, out = s.sb("mc_sigmoid", [P, 2, T3, D]), s.sb("mc_out", [P, 2, T3, D])
        tw = s.sb("mc_tw", [P, 2, NC, NB])

        def load(sp, slot, e, sem):
            for dst, n, pat in ((wk[:, slot], "m1_wk", "o p d f -> p (o d) f"), (wv[:, slot], "m1_wv", "o p f n -> p (o f) n"),
                                (wr[:, slot], "m1_wr", "o p d f -> p (o d) f"), (mu[:, slot], "m1_mu", "o p f -> p (o f)")):
                sp.dma_start(dst, g.d[n][bass.ds(e, 1)].rearrange(pat)).then_inc(sem, 16)
        with Scope(nc) as u:
            loaded = u.sem("mc_loaded")
            with nc.Block() as block:
                @block.sync
                def _(sp):
                    load(sp, 0, 0, loaded)
                    sp.wait_ge(loaded, 64)
            u.round_end()
        loaded1, loaded0, tw_ready, xk_ready, k_psum, relu_ready, kk_ready, r_psum, r_ready, kv_psum, o_ready, h_ready = (
            s.sem("mc_" + n) for n in
            "loaded1 loaded0 tw_ready xk_ready k_psum relu_ready kk_ready r_psum r_ready kv_psum o_ready h_ready".split())
        ps = g.ps
        NR = 2 * 2 * NB
        def where(n):
            return n // (2 * NB), (n // 2) % NB, n % 2
        with nc.Fori(0, NE // 2) as r:
            e = r * 2
            with nc.Block() as block:
                @block.sync
                def _(sp):
                    load(sp, 1, e + 1, loaded1)
                    sp.wait_ge(kv_psum, T3 * NR // 2)
                    load(sp, 0, e + 2, loaded0)
                    sp.wait_ge(loaded1, 64)
                    sp.wait_ge(loaded0, 64)

                @block.tensor
                def _(pe):
                    for n in range(NR + 1):
                        if n < NR:
                            slot = n // (2 * NB)
                            if n == NR // 2:
                                pe.wait_ge(loaded1, 64)
                            pe.wait_ge(xk_ready, n + 1)
                            for f in range(FC):
                                k = n * FC + f
                                if k >= 3:
                                    pe.wait_ge(relu_ready, k - 2)
                                for d in range(DC):
                                    mm = pe.matmul(ps[:, k % 3, 0:BT], wk[:, slot, d, f * P:(f + 1) * P], xk[:, n % 2, d, :],
                                                   start=(d == 0), stop=(d == DC - 1))
                                mm.then_inc(k_psum, 1)
                            for t in range(T3):
                                k = n * T3 + t
                                if k >= 2:
                                    pe.wait_ge(r_ready, k - 1)
                                for d in range(DC):
                                    mm = pe.matmul(ps[:, 3 + k % 2, 0:D], xr[:, n % 2, d, t * P:(t + 1) * P], wr[:, slot, d, :],
                                                   start=(d == 0), stop=(d == DC - 1))
                                mm.then_inc(r_psum, 1)
                        if n >= 1:
                            slot = (n - 1) // (2 * NB)
                            pe.wait_ge(kk_ready, n)
                            for t in range(T3):
                                k = (n - 1) * T3 + t
                                if k >= 3:
                                    pe.wait_ge(o_ready, k - 2)
                                for f in range(FC):
                                    mm = pe.matmul(ps[:, 5 + k % 3, 0:D], kk[:, (n - 1) % 2, f, t * P:(t + 1) * P],
                                                   wv[:, slot, f, :], start=(f == 0), stop=(f == FC - 1))
                                mm.then_inc(kv_psum, 1)

                @block.scalar
                def _(act):
                    for n in range(NR):
                        if n >= 2:
                            act.wait_ge(kk_ready, n - 1)
                        for f in range(FC):
                            k = n * FC + f
                            act.wait_ge(k_psum, k + 1)
                            act.activation(rl[:, n % 2, f, :], ps[:, k % 3, 0:BT], ACT.Relu).then_inc(relu_ready, 1)
                        if n >= 2:
                            act.wait_ge(o_ready, T3 * (n - 1))
                        for t in range(T3):
                            k = n * T3 + t
                            act.wait_ge(r_psum, k + 1)
                            act.activation(sg[:, n % 2, t, :], ps[:, 3 + k % 2, 0:D], ACT.Sigmoid).then_inc(r_ready, 1)

                @block.gpsimd
                def _(pool):
                    for n in range(NR + 1):
                        if n < NR:
                            pool.wait_ge(relu_ready, FC * (n + 1))
                            if n >= 2:
                                pool.wait_ge(kv_psum, T3 * (n - 1))
                            pool.tensor_tensor(kk[:, n % 2], rl[:, n % 2], rl[:, n % 2], ALU.mult).then_inc(kk_ready, 1)
                        if n >= 1:
                            _, b, half = where(n - 1)
                            pool.wait_ge(o_ready, T3 * n)
                            if n - 1 >= NR // 2:
                                pool.wait_ge(h_ready, n - NR // 2)
                            hb = g.h[:, T3 * half:T3 * half + T3, b, :]
                            pool.tensor_tensor(hb, hb, out[:, (n - 1) % 2], ALU.add).then_inc(h_ready, 1)

                @block.vector
                def _(dve):
                    for k in range(2):
                        op = dve.tensor_copy(tw[:, k], g.gates1[:, :, :, bass.ds(e + k, 1)].rearrange("p c b o -> p c (b o)"))
                    op.then_inc(tw_ready, 1)
                    dve.wait_ge(tw_ready, 1)
                    for n in range(NR + 1):
                        if n < NR:
                            slot, b, half = where(n)
                            if n == NR // 2:
                                dve.wait_ge(loaded1, 64)
                            if n >= 2:
                                dve.wait_ge(k_psum, FC * (n - 1))
                                dve.wait_ge(r_psum, T3 * (n - 1))
                            t0 = half * BT
                            for w, dst in ((0, xk), (1, xr)):
                                for d in range(DC):
                                    op = dve.scalar_tensor_tensor(dst[:, n % 2, d, :], g.dT[:, d, b, t0:t0 + BT],
                                                                  mu[:, slot, 2 * w + d:2 * w + d + 1],
                                                                  g.eT[:, d, b, t0:t0 + BT], ALU.mult, ALU.add)
                            op.then_inc(xk_ready, 1)
                        if n >= 1:
                            slot, b, half = where(n - 1)
                            if n - 1 >= 2:
                                dve.wait_ge(h_ready, n - 2)
                            for t in range(T3):
                                k = (n - 1) * T3 + t
                                dve.wait_ge(kv_psum, k + 1)
                                dve.wait_ge(r_ready, k + 1)
                                dve.scalar_tensor_tensor(out[:, (n - 1) % 2, t, :], ps[:, 5 + k % 3, 0:D],
                                                         tw[:, slot, T3 * half + t, b:b + 1], sg[:, (n - 1) % 2, t, :],
                                                         ALU.mult, ALU.mult).then_inc(o_ready, 1)
            s.round_end()


def layer1_attn(nc, g):
    with Scope(nc) as s:
        g.gates1 = s.sb("gates1", [P, NC, NB, 8])
        g.eT, g.dT = s.sb("l1_eT", [P, DC, NB, SEQ + 1]), s.sb("l1_dT", [P, DC, NB, SEQ])
        with nc.Block() as block:
            @block.vector
            def _(dve):
                dve.memset(g.eT[:], 0.0)
        time_mix(nc, g)
        moe_channel_mix(nc, g)


def route_groups(nc, g):
    NE, NGR = 32, 8
    with Scope(nc) as s:
        gw, bias = s.sb("rg_gw", [P, DC, NE]), s.sb("rg_bias", [P, NE])
        nx, nT = s.sb("rg_nx", [P, NB, D]), s.sb("rg_nT", [P, DC, NB * P])
        score, sc, sel, eq, cum, comb = (s.sb("rg_" + n, [P, NB, NE]) for n in ("score", "sc", "sel", "eq", "cum", "comb"))
        pairs = s.sb("rg_pairs", [P, NB, NGR, 6])
        gs, gsel, geq, gcum = (s.sb("rg_" + n, [P, NB, NGR]) for n in ("gs", "gsel", "geq", "gcum"))
        v8, cnt = s.sb("rg_v8", [P, NB, 8]), s.sb("rg_cnt", [P, NB])
        ones = s.sb("rg_ones", [P, 32])
        stats, mv, rs, ltmp = s.sb("rg_stats", [P, NB, 6]), s.sb("rg_mv", [P, NB, 2]), s.sb("rg_rs", [P, NB]), s.sb("rg_ltmp", [P, 2, NB])
        with Scope(nc) as u:
            loaded = u.sem("rg_loaded")
            with nc.Block() as block:
                @block.sync
                def _(sp):
                    sp.dma_start(gw[:], g.d["m2_gate"]).then_inc(loaded, 16)
                    sp.dma_start(bias[:], g.d["m2_bias"]).then_inc(loaded, 16)
                    sp.wait_ge(loaded, 32)

                @block.vector
                def _(dve):
                    dve.memset(ones[:], 1.0)
                    dve.memset(g.comb[:], 1.0)
            u.round_end()
        vchain, nx_ready, nT_psum, nT_ready, lg_psum, e_ready, xT_ready = (s.sem("rg_" + n) for n in (
            "vchain nx_ready nT_psum nT_ready lg_psum e_ready xT_ready").split())
        ps = g.ps
        with nc.Fori(0, NC) as c:
            hc = g.h[:, bass.ds(c, 1)].rearrange("p o b n -> p (o b) n")
            with nc.Block() as block:
                @block.tensor
                def _(pe):
                    pe.wait_ge(nx_ready, 1)
                    for d in range(DC):
                        for b in range(NB):
                            mm = pe.transpose(ps[:, d, b * P:(b + 1) * P], nx[:, b, d * P:(d + 1) * P], g.ident[:])
                    mm.then_inc(nT_psum, 1)
                    pe.wait_ge(nT_ready, 1)
                    for b in range(NB):
                        for d in range(DC):
                            mm = pe.matmul(ps[:, 2, b * NE:(b + 1) * NE], nT[:, d, b * P:(b + 1) * P], gw[:, d, :],
                                           start=(d == 0), stop=(d == DC - 1))
                    mm.then_inc(lg_psum, 1)

                @block.scalar
                def _(act):
                    act.wait_ge(nT_psum, 1)
                    act.activation(nT[:, 0, :], ps[:, 0, :], ACT.Copy)
                    act.activation(nT[:, 1, :], ps[:, 1, :], ACT.Copy).then_inc(nT_ready, 1)
                    act.wait_ge(lg_psum, 1)
                    act.activation(score[:].rearrange("p b e -> p (b e)"), ps[:, 2, 0:NB * NE], ACT.Exp, scale=-1.0
                                   ).then_inc(e_ready, 1)

                @block.gpsimd
                def _(pool):
                    pool.wait_ge(nT_ready, 1)
                    pool.tensor_copy(g.xT[:, :, bass.ds(c, 1), :].rearrange("p d o n -> p d (o n)"), nT[:]).then_inc(xT_ready, 1)

                @block.vector
                def _(dve):
                    link = chain(dve, vchain)
                    layernorm(dve, link, [hc[:, b, :] for b in range(NB)], [nx[:, b, :] for b in range(NB)],
                              stats, mv, rs, ltmp)
                    dve.engine_nop().then_inc(nx_ready, 1)
                    dve.wait_ge(e_ready, 1)
                    link(dve.tensor_scalar(score[:], score[:], 1.0, None, ALU.add))
                    link(dve.reciprocal(score[:], score[:]))
                    link(dve.tensor_tensor(sc[:], score[:], bc(bias[:].unsqueeze(1), [P, NB, NE]), ALU.add))
                    q = sc[:].rearrange("p b (g k) -> p b g k", g=NGR)
                    for b in range(NB):
                        dve.tensor_tensor(pairs[:, b, :, 0:3], q[:, b, :, 0:3], q[:, b, :, 1:4], ALU.add)
                        dve.tensor_tensor(pairs[:, b, :, 3:5], q[:, b, :, 0:2], q[:, b, :, 2:4], ALU.add)
                    link(dve.tensor_tensor(pairs[:, :, :, 5], q[:, :, :, 0], q[:, :, :, 3], ALU.add))
                    link(dve.tensor_reduce(gs[:], pairs[:], AX_X, ALU.max))
                    pick_top(dve, link, gs[:], 4, v8[:], gsel[:], geq[:], gcum[:], cnt[:], ones[:])
                    link(dve.tensor_tensor(q, q, bc(gsel[:].unsqueeze(3), [P, NB, NGR, 4]), ALU.mult))
                    pick_top(dve, link, sc[:], 8, v8[:], sel[:], eq[:], cum[:], cnt[:], ones[:])
                    link(dve.tensor_tensor(comb[:], sel[:], score[:], ALU.mult))
                    link(dve.tensor_reduce(cnt[:], comb[:], AX_X, ALU.add))
                    link(dve.tensor_scalar(cnt[:], cnt[:], 1e-20, None, ALU.add))
                    link(dve.reciprocal(cnt[:], cnt[:]))
                    link(dve.tensor_scalar(cnt[:], cnt[:], 2.5, None, ALU.mult))
                    dve.tensor_tensor(g.comb[:, bass.ds(c, 1), :, 0:NE].rearrange("p o b e -> p (o b) e"), comb[:],
                                      bc(cnt[:].unsqueeze(2), [P, NB, NE]), ALU.mult)
            s.round_end()


def moe_silu(nc, g, first, count, per):
    with Scope(nc) as s:
        tag = f"ms{first}_"
        w = s.sb(tag + "w", [P, per, 3 * 2 * P])
        act_g, hid = s.sb(tag + "silu", [P, 2, 512]), s.sb(tag + "hid", [P, 2, 512])
        cw = s.sb(tag + "comb", [P, per, NC, NB])

        def load(sp, slot, e, sem):
            sp.dma_start(w[:, slot], g.d["m2_w"][bass.ds(e, 1)].rearrange("o p n -> p (o n)")).then_inc(sem, 16)
        with Scope(nc) as u:
            loaded = u.sem(tag + "loaded")
            with nc.Block() as block:
                @block.sync
                def _(sp):
                    for i in range(per):
                        load(sp, i, first + i, loaded)
                    sp.wait_ge(loaded, 16 * per)
            u.round_end()
        loaded, cw_ready, gu_psum, s_ready, hid_ready, y_psum, y_used = (s.sem(tag + n) for n in (
            "next_loaded cw_ready gu_psum s_ready hid_ready y_psum y_used").split())
        ps = g.ps
        NR = per * NC
        with nc.Fori(0, count // per) as r:
            e = r * per + first
            with nc.Block() as block:
                @block.sync
                def _(sp):
                    if count > per:
                        for i in range(per):
                            sp.wait_ge(y_psum, NB * NC * (i + 1))
                            load(sp, i, e + per + i, loaded)
                        sp.wait_ge(loaded, 16 * per)

                @block.tensor
                def _(pe):
                    for n in range(NR + 1):
                        if n < NR:
                            slot, c = divmod(n, NC)
                            if n >= 2:
                                pe.wait_ge(hid_ready, n - 1)
                            for k in range(2):
                                for d in range(DC):
                                    at = (2 * k + d) * P
                                    mm = pe.matmul(ps[:, 2 * k + n % 2, :], w[:, slot, at:at + P], g.xT[:, d, c, :],
                                                   start=(d == 0), stop=(d == DC - 1))
                                mm.then_inc(gu_psum, 1)
                        if n >= 1:
                            slot, c = divmod(n - 1, NC)
                            pe.wait_ge(hid_ready, n)
                            for b in range(NB):
                                k = (n - 1) * NB + b
                                if k >= 4:
                                    pe.wait_ge(y_used, k - 3)
                                pe.matmul(ps[:, 4 + k % 4, 0:D], hid[:, (n - 1) % 2, b * P:(b + 1) * P],
                                          w[:, slot, 4 * P:4 * P + D], start=True, stop=True).then_inc(y_psum, 1)

                @block.scalar
                def _(act):
                    for n in range(NR):
                        act.wait_ge(gu_psum, 2 * n + 1)
                        if n >= 2:
                            act.wait_ge(hid_ready, n - 1)
                        act.activation(act_g[:, n % 2, :], ps[:, n % 2, :], ACT.Silu).then_inc(s_ready, 1)

                @block.vector
                def _(dve):
                    for k in range(per):
                        op = dve.tensor_copy(cw[:, k], g.comb[:, :, :, bass.ds(e + k, 1)].rearrange("p c b o -> p c (b o)"))
                    op.then_inc(cw_ready, 1)
                    dve.wait_ge(cw_ready, 1)
                    for n in range(NR + 1):
                        if n < NR:
                            dve.wait_ge(s_ready, n + 1)
                            dve.wait_ge(gu_psum, 2 * n + 2)
                            if n >= 2:
                                dve.wait_ge(y_psum, NB * (n - 1))
                            dve.tensor_tensor(hid[:, n % 2, :], act_g[:, n % 2, :], ps[:, 2 + n % 2, :], ALU.mult
                                              ).then_inc(hid_ready, 1)
                        if n >= 1:
                            slot, c = divmod(n - 1, NC)
                            if n - 1 >= NC:
                                dve.wait_ge(y_used, NB * (n - NC))
                            for b in range(NB):
                                k = (n - 1) * NB + b
                                dve.wait_ge(y_psum, k + 1)
                                dve.scalar_tensor_tensor(g.h[:, c, b, :], ps[:, 4 + k % 4, 0:D], cw[:, slot, c, b:b + 1],
                                                         g.h[:, c, b, :], ALU.mult, ALU.add).then_inc(y_used, 1)
            s.round_end()


def layer1_ffn(nc, g):
    with Scope(nc) as s:
        g.xT = s.sb("l1_xT", [P, DC, NC, NB * P])
        g.comb = s.sb("l1_comb", [P, NC, NB, 34])
        route_groups(nc, g)
        moe_silu(nc, g, 0, 32, 8)
        moe_silu(nc, g, 32, 2, 2)


class Shared:
    pass


def program(nc, d, out):
    g = Shared()
    g.d = d
    with ExitStack() as ctx:
        g.ps = ctx.enter_context(nc.psum_tensor("banks", [P, 8, 512], F32))
        g.h = ctx.enter_context(nc.sbuf_tensor("h_res", [P, NC, NB, D], F32))
        g.ident = ctx.enter_context(nc.sbuf_tensor("ident", [P, P], F32))
        g.scr_ssm = nc.dram_tensor("scr_ssm", (NB, 256, 256), F32, kind="Internal").ap()
        g.scr_qk = nc.dram_tensor("scr_qk", (2, 3, D, NB, SEQ), BF16, kind="Internal").ap()
        with Scope(nc) as s:
            loaded = s.sem("const_loaded")
            with nc.Block() as block:
                @block.sync
                def _(sp):
                    sp.dma_start(g.ident[:], d["ident"]).then_inc(loaded, 16)
                    sp.wait_ge(loaded, 16)
            s.round_end()
        for stage in STAGES:
            stage(nc, g)
        with Scope(nc) as s:
            stored = s.sem("out_stored")
            with nc.Block() as block:
                @block.sync
                def _(sp):
                    for b in range(NB):
                        sp.dma_start(out[b].rearrange("(c p) n -> p c n", p=P), g.h[:, :, b, :]).then_inc(stored, 16)
                    sp.wait_ge(stored, 16 * NB)
            s.round_end()


def lay_out(**a):
    a = {k: np.ascontiguousarray(v) for k, v in a.items()}
    o = {}

    def dup(x):
        return np.concatenate([x.T, x.T], 0)

    def rep(x):
        return np.broadcast_to(np.asarray(x).reshape(1, -1), (P, np.asarray(x).size))

    def kxn(w):
        return w.reshape(-1, P, w.shape[-1]).transpose(1, 0, 2)

    o["txt"] = a["txt"]
    o["s4_ldt"] = rep(a["L0_tok_log_dt"])
    o["s4_are"], o["s4_aim"] = dup(a["L0_tok_inv_A_real"]), dup(a["L0_tok_A_imag"])
    o["s4_bre"], o["s4_bim"] = dup(a["L0_tok_B_ri"][..., 0]), dup(a["L0_tok_B_ri"][..., 1])
    for k, n in enumerate(("s4_cre", "s4_cim")):
        x = a["x"][..., k].transpose(2, 0, 1)
        o[n] = np.concatenate([x, x], 0)
    o["ident"] = np.eye(P, dtype=np.float32)
    o["identb"] = np.eye(P, dtype=np.float32).astype(mybir.dt.np(BF16))
    order = [(f * 4 + r) * 2 + j for f in range(2) for j in range(2) for r in range(4)]
    o["dn_wqk"] = np.stack([kxn(a["L0_attn_Wq"].T), kxn(a["L0_attn_Wk"].T)], 1)
    o["dn_wv"] = kxn(np.concatenate([a["L0_attn_Wv"], a["L0_attn_Wbeta"][order], a["L0_attn_Wmix"][order],
                                     a["L0_attn_Wgate"]], 0).T)
    o["dn_wout"] = kxn(a["L0_attn_Wout"].T)
    floor = np.array([np.exp(np.float32(-0.5 ** (k // 2 + 1))) for k in order], np.float32)
    o["dn_rows"] = rep(np.concatenate([a["L0_attn_bout"], a["L0_attn_ln_g"], a["L0_attn_ln_b"], a["L0_attn_bbeta"][order],
                                       a["L0_attn_bmix"][order], a["L0_attn_bgate"], floor]))
    i = np.arange(P)
    tri = (i[:, None] <= i[None, :]).astype(np.float32)
    cm = np.where(i[:, None] <= i[None, :], 0.0, -30000.0).astype(np.float32)
    bd = (i[:, None] // 32 == (np.arange(8 * 33) // 33 % 4)[None, :]).astype(np.float32)
    o["dn_masks"] = np.concatenate([tri, np.ones((P, P), np.float32), cm, bd], 1)
    sel = np.zeros((48, 16, P), np.float32)
    for k in range(48):
        sel[k, k % 16] = 1.0
    o["dn_sel"] = sel.astype(mybir.dt.np(BF16))
    extra_layouts(a, o, rep, kxn)
    return {k: np.ascontiguousarray(v) for k, v in o.items()}


def extra_layouts(a, o, rep, kxn):
    w, bias = a["L0_ffn_Wqkv"], a["L0_ffn_bqkv"]
    o["at_wqk"] = np.stack([kxn(w[:, 0:D]), kxn(w[:, D:2 * D])], 1)
    o["at_wv"] = kxn(w[:, 2 * D:])
    o["at_rows"] = rep(np.concatenate([a["L0_ffn_ln1_w"], a["L0_ffn_ln1_b"], bias[2 * D:]]))
    o["at_qkb"] = bias[0:2 * D].reshape(4, P).T
    i = np.arange(P)
    big = np.float32(-1e30)
    qm = np.where(i[None, :] <= i[:, None], np.float32(0), big)
    o["at_consts"] = np.concatenate([np.eye(P, dtype=np.float32), qm, qm.T, -np.ones((P, P), np.float32)],
                                    1).astype(mybir.dt.np(BF16))
    o["at_wo"] = kxn(a["L0_ffn_Wo"])
    o["m0_gate"] = kxn(a["L0_ffn_gate_W"])
    o["af_rows"] = rep(np.concatenate([a["L0_ffn_bo"], a["L0_ffn_ln2_w"], a["L0_ffn_ln2_b"]]))
    o["m0_b2"] = a["L0_ffn_fc2_b"]

    def one_more(x):
        return np.concatenate([x, x[:1]], 0)
    w1 = a["L0_ffn_fc1_w"].transpose(0, 2, 1)
    o["m0_w1"] = one_more(w1.reshape(8, DC, P, 1024).transpose(0, 2, 1, 3))
    w2 = a["L0_ffn_fc2_w"].transpose(0, 2, 1)
    o["m0_w2"] = one_more(w2.reshape(8, 8, P, D).transpose(0, 2, 1, 3))
    o["m0_b1"] = one_more(a["L0_ffn_fc1_b"].reshape(8, 8, P).transpose(0, 2, 1))

    o["tm_wkvr"] = np.stack([kxn(a["L1_attn_" + n]) for n in ("Wk", "Wv", "Wr")], 1)
    o["tm_wo"] = kxn(a["L1_attn_Wo"])
    o["m1_router"] = kxn(a["L1_attn_router_w"])
    o["tm_rows"] = rep(np.concatenate([a["L1_attn_" + n] for n in ("ln1_g", "ln1_b", "ln2_g", "ln2_b")]))
    o["tm_cols"] = np.stack([a["L1_attn_" + n].reshape(DC, P).T for n in (
        "tm_mu_k", "tm_mu_v", "tm_mu_r", "time_decay", "time_first")], 1)
    o["m1_wk"] = one_more(a["L1_attn_eWk"].reshape(8, DC, P, 512).transpose(0, 2, 1, 3))
    o["m1_wv"] = one_more(a["L1_attn_eWv"].reshape(8, 4, P, D).transpose(0, 2, 1, 3))
    o["m1_wr"] = one_more(a["L1_attn_eWr"].reshape(8, DC, P, D).transpose(0, 2, 1, 3))
    mu = np.stack([a["L1_attn_cm_mu_k"], a["L1_attn_cm_mu_r"]], 1)
    o["m1_mu"] = one_more(mu.reshape(8, 2 * DC, P).transpose(0, 2, 1))
    o["m2_gate"] = kxn(a["L1_ffn_gate_w"].T)
    o["m2_bias"] = rep(a["L1_ffn_gate_bias"])
    gate = np.concatenate([a["L1_ffn_w_gate"], a["L1_ffn_sh_gate"].reshape(2, P, D)], 0)
    up = np.concatenate([a["L1_ffn_w_up"], a["L1_ffn_sh_up"].reshape(2, P, D)], 0)
    down = np.concatenate([a["L1_ffn_w_down"], a["L1_ffn_sh_down"].reshape(D, 2, P).transpose(1, 0, 2)], 0)

    def by_rows(x):
        return x.transpose(0, 2, 1).reshape(34, DC, P, P).transpose(0, 2, 1, 3).reshape(34, P, 2 * P)
    m2 = np.concatenate([by_rows(gate), by_rows(up), down.transpose(0, 2, 1)], 2)
    o["m2_w"] = np.concatenate([m2, m2[:6]], 0)


STAGES = [ssm_tokens, deltanet, layer0_ffn, layer1_attn, layer1_ffn]


def kernel(**inputs):
    import concourse.bacc as _bacc
    from concourse.bass_utils import run_bass_kernel_spmd as _run

    nc = _bacc.Bacc("TRN2", target_bir_lowering=False, num_devices=1)
    arrays = {"in_" + n: a for n, a in lay_out(**{k: np.asarray(v) for k, v in inputs.items()}).items()}
    d = {n[3:]: nc.dram_tensor(n, a.shape, mybir.dt.from_np(a.dtype), kind="ExternalInput").ap()
         for n, a in arrays.items()}
    out = nc.dram_tensor("out_h", (NB, SEQ, D), F32, kind="ExternalOutput").ap()
    program(nc, d, out)
    r = _run(nc, [arrays], core_ids=[0])
    return r.results[0]["out_h"]
```

```python
from contextlib import ExitStack
import numpy as np
import concourse.bass as bass
from concourse import mybir

ALU = mybir.AluOpType
ACT = mybir.ActivationFunctionType
F32 = mybir.dt.float32
BF16 = mybir.dt.bfloat16
I32 = mybir.dt.int32
AX_X = mybir.AxisListType.X

P = 128
NB = 4
SEQ = 768
NC = SEQ // P
D = 256
DC = D // P
LN_EPS = 1e-5


def bc(ap, shape):
    return ap.broadcast_to(shape)


class Scope:

    def __init__(self, nc, tag=""):
        self.nc, self.tag, self.ctx, self.sems = nc, tag, ExitStack(), []

    def __enter__(self):
        return self

    def __exit__(self, *a):
        return self.ctx.__exit__(*a)

    def sb(self, name, shape, dt=F32):
        return self.ctx.enter_context(self.nc.sbuf_tensor(self.tag + name, shape, dt))

    def sem(self, name):
        s = self.ctx.enter_context(self.nc.semaphore(self.tag + name))
        self.sems.append(s)
        return s

    def round_end(self, swdge=False):
        if swdge:
            self.nc.gpsimd.dma_reset()
        for s in self.sems:
            self.nc.gpsimd.sem_clear(s)
        self.nc.all_engine_barrier()


def chain(eng, sem):
    n = [0]

    def link(ins):
        n[0] += 1
        ins.then_inc(sem, 1)
        eng.wait_ge(sem, n[0])
    return link


def rsqrt(dve, link, x, y, t):
    link(dve.tensor_scalar(y.bitcast(I32), x.bitcast(I32), -0.5, float(0x5F3759DF), ALU.mult, ALU.add))
    for _ in range(3):
        link(dve.tensor_tensor(t, y, y, ALU.mult))
        link(dve.scalar_tensor_tensor(t, t, -0.5, x, ALU.mult, ALU.mult))
        link(dve.scalar_tensor_tensor(y, t, 1.5, y, ALU.add, ALU.mult))


def layernorm(dve, link, tiles, outs, stats, mv, rs, tmp):
    n = len(tiles)
    for i, x in enumerate(tiles):
        ins = dve.bn_stats(stats[:, i, :], x)
    link(ins)
    for i in range(n):
        ins = dve.bn_aggr(mv[:, i, :], stats[:, i, :])
    link(ins)
    link(dve.tensor_scalar(tmp[:, 0, 0:n], mv[:, 0:n, 1], LN_EPS, None, ALU.add))
    rsqrt(dve, link, tmp[:, 0, 0:n], rs[:, 0:n], tmp[:, 1, 0:n])
    for i, x in enumerate(tiles):
        ins = dve.tensor_scalar(outs[i], x, mv[:, i, 0:1], rs[:, i:i + 1], ALU.subtract, ALU.mult)
    link(ins)


def accurate_exp(dve, link, x, out, n, t):
    link(dve.tensor_scalar(t, x, -87.0, 88.0, ALU.max, ALU.min))
    link(dve.tensor_scalar(out.bitcast(I32), t, 1.4426950408889634, None, ALU.mult))
    link(dve.tensor_copy(n, out.bitcast(I32)))
    link(dve.scalar_tensor_tensor(t, n, -0.693359375, t, ALU.mult, ALU.add))
    link(dve.scalar_tensor_tensor(t, n, 2.12194440e-4, t, ALU.mult, ALU.add))
    coefficients = [1.0]
    for k in range(2, 11):
        coefficients.append(coefficients[-1] / k)
    link(dve.tensor_scalar(out, t, coefficients[-1], None, ALU.mult))
    for c in reversed(coefficients[:-1]):
        link(dve.scalar_tensor_tensor(out, out, c, t, ALU.add, ALU.mult))
    link(dve.tensor_scalar(t.bitcast(I32), n, 127.0, float(1 << 23), ALU.add, ALU.mult))
    link(dve.scalar_tensor_tensor(out, out, 1.0, t, ALU.add, ALU.mult))


def ssm_tokens(nc, g):
    H, NA, NV, HG = 256, 8, 32, 64
    with Scope(nc) as s:
        cbr, cbi = s.sb("ssm_cb_re", [P, NB, H]), s.sb("ssm_cb_im", [P, NB, H])
        p1, p2 = s.sb("ssm_coarse_1", [P, NA, H]), s.sb("ssm_coarse_2", [P, NA, H])
        V = s.sb("ssm_fine", [P, NV, H])
        with Scope(nc) as u:
            inp = u.sb("ssm_in", [P, 5, H])
            cin = u.sb("ssm_c_in", [P, 2, NB, H])
            vr, vi = u.sb("ssm_vr", [P, 16, H]), u.sb("ssm_vi", [P, 16, H])
            pr, pi = u.sb("ssm_pr", [P, NA, H]), u.sb("ssm_pi", [P, NA, H])
            x = u.sb("ssm_x", [P, 8, 2, H])
            w = u.sb("ssm_w", [P, 6, H])
            t1, t2 = u.sb("ssm_t1", [P, 16, H]), u.sb("ssm_t2", [P, 16, H])
            zeros = u.sb("ssm_zeros", [P, 1, 1024])
            loaded, text = u.sem("ssm_loaded"), u.sem("ssm_text_loaded")
            zeroed, cleared = u.sem("ssm_zeroed"), u.sem("ssm_cleared")
            vchain = u.sem("ssm_vchain")
            with nc.Block() as block:
                @block.sync
                def _(sp):
                    for i, n in enumerate(("s4_ldt", "s4_are", "s4_aim", "s4_bre", "s4_bim")):
                        sp.dma_start(inp[:, i, :], g.d[n]).then_inc(loaded, 16)
                    sp.dma_start(cin[:, 0], g.d["s4_cre"]).then_inc(loaded, 16)
                    sp.dma_start(cin[:, 1], g.d["s4_cim"]).then_inc(loaded, 16)
                    for b in range(NB):
                        sp.dma_start(g.h[:, 2:NC, b, :], g.d["txt"][b].rearrange("(c p) n -> p c n", p=P)
                                     ).then_inc(text, 16)
                    sp.wait_ge(zeroed, 1)
                    slots = g.slots.rearrange("(k p m n) -> k p m n", p=P, m=8, n=1024)
                    for k in range(slots.shape[0]):
                        sp.dma_start(slots[k], bc(zeros[:], [P, 8, 1024])).then_inc(cleared, 16)
                    sp.dma_start(g.scr_e[:, 0, :], zeros[0:NB, 0, 0:D]).then_inc(cleared, 16)
                    sp.wait_ge(text, 16 * NB)
                    sp.wait_ge(cleared, 16 * (slots.shape[0] + 1))

                @block.vector
                def _(dve):
                    link = chain(dve, vchain)

                    def mul(re, im, ar, ai, br, bi, k):
                        if re is not None:
                            dve.tensor_tensor(t1[:, 0:k], ar, br, ALU.mult)
                            link(dve.tensor_tensor(t2[:, 0:k], ai, bi, ALU.mult))
                            link(dve.tensor_tensor(re, t1[:, 0:k], t2[:, 0:k], ALU.subtract))
                        if im is not None:
                            dve.tensor_tensor(t1[:, 0:k], ar, bi, ALU.mult)
                            link(dve.tensor_tensor(t2[:, 0:k], ai, br, ALU.mult))
                            link(dve.tensor_tensor(im, t1[:, 0:k], t2[:, 0:k], ALU.add))

                    dve.memset(zeros[:], 0.0).then_inc(zeroed, 1)
                    dve.memset(vr[:, 0], 1.0)
                    dve.memset(vi[:, 0], 0.0)
                    dve.memset(pr[:, 0], 1.0)
                    link(dve.memset(pi[:, 0], 0.0))
                    dve.wait_ge(loaded, 16 * 7)
                    accurate_exp(dve, link, inp[:, 0:2], w[:, 0:2], w[:, 2:4], w[:, 4:6])
                    dve.scalar_tensor_tensor(w[:, 2], w[:, 0], -0.5, w[:, 1], ALU.mult, ALU.mult)
                    link(dve.scalar_tensor_tensor(w[:, 3], w[:, 0], 0.5, inp[:, 2], ALU.mult, ALU.mult))
                    dve.tensor_tensor(w[:, 4], w[:, 3], w[:, 3], ALU.mult)
                    dve.tensor_scalar(w[:, 0], w[:, 2], -1.0, 1.0, ALU.mult, ALU.add)
                    link(dve.tensor_tensor(w[:, 5], w[:, 2], w[:, 2], ALU.mult))
                    link(dve.tensor_tensor(w[:, 0], w[:, 0], w[:, 0], ALU.mult))
                    link(dve.tensor_tensor(w[:, 0], w[:, 0], w[:, 4], ALU.add))
                    link(dve.reciprocal(w[:, 1], w[:, 0]))
                    link(dve.tensor_tensor(w[:, 5], w[:, 5], w[:, 4], ALU.add))
                    link(dve.tensor_scalar(w[:, 5], w[:, 5], -1.0, 1.0, ALU.mult, ALU.add))
                    dve.tensor_tensor(x[:, 0, 0], w[:, 5], w[:, 1], ALU.mult)
                    link(dve.scalar_tensor_tensor(x[:, 0, 1], w[:, 3], 2.0, w[:, 1], ALU.mult, ALU.mult))
                    for i in range(7):
                        mul(x[:, i + 1, 0:1], x[:, i + 1, 1:2], x[:, i, 0:1], x[:, i, 1:2], x[:, i, 0:1],
                            x[:, i, 1:2], 1)
                    link(dve.tensor_scalar(inp[:, 3:5], inp[:, 3:5], 2.0, None, ALU.mult))
                    mul(cbr[:], cbi[:], cin[:, 0], cin[:, 1], bc(inp[:, 3:4], [P, NB, H]),
                        bc(inp[:, 4:5], [P, NB, H]), NB)
                    for i in range(4):
                        k = 1 << i
                        mul(vr[:, k:2 * k], vi[:, k:2 * k], vr[:, 0:k], vi[:, 0:k],
                            bc(x[:, i, 0:1], [P, k, H]), bc(x[:, i, 1:2], [P, k, H]), k)
                    for i in range(3):
                        k = 1 << i
                        mul(pr[:, k:2 * k], pi[:, k:2 * k], pr[:, 0:k], pi[:, 0:k],
                            bc(x[:, 5 + i, 0:1], [P, k, H]), bc(x[:, 5 + i, 1:2], [P, k, H]), k)
                    top, low = slice(0, 64), slice(64, 128)
                    dve.tensor_copy(V[top, 0:16], vr[top])
                    dve.tensor_copy(V[low, 0:16], vi[low])
                    dve.tensor_copy(p1[top], pr[top])
                    dve.tensor_scalar(p1[low], pi[low], -1.0, None, ALU.mult)
                    dve.tensor_scalar(p2[top], pi[top], -1.0, None, ALU.mult)
                    dve.tensor_scalar(p2[low], pr[low], -1.0, None, ALU.mult)
                    dve.tensor_copy(w[top, 0], x[top, 4, 0])
                    dve.tensor_copy(w[low, 0], x[low, 4, 1])
                    dve.tensor_scalar(w[top, 1], x[top, 4, 1], -1.0, None, ALU.mult)
                    link(dve.tensor_copy(w[low, 1], x[low, 4, 0]))
                    dve.tensor_tensor(t1[:], vr[:], bc(w[:, 0:1], [P, 16, H]), ALU.mult)
                    link(dve.tensor_tensor(t2[:], vi[:], bc(w[:, 1:2], [P, 16, H]), ALU.mult))
                    link(dve.tensor_tensor(V[:, 16:32], t1[:], t2[:], ALU.add))
            u.round_end()
        L = s.sb("ssm_left", [P, NB, NA, HG])
        Lt = s.sb("ssm_left_t", [P, NB, NA, HG])
        ko = s.sb("ssm_out", [NB * NA, HG, NV])
        vchain, l_ready, k_ready = s.sem("ssm_vchain2"), s.sem("ssm_left_ready"), s.sem("ssm_k_ready")
        k_out, stored, back = s.sem("ssm_k_copied"), s.sem("ssm_k_stored"), s.sem("ssm_k_back")
        NBK = HG * NV // 512
        with nc.Fori(0, H // HG) as r:
            with nc.Block() as block:
                @block.vector
                def _(dve):
                    link = chain(dve, vchain)
                    hs = bass.ds(r * HG, HG)
                    dve.tensor_tensor(L[:], bc(cbr[:, :, hs].unsqueeze(2), [P, NB, NA, HG]),
                                      bc(p1[:, :, hs].unsqueeze(1), [P, NB, NA, HG]), ALU.mult)
                    link(dve.tensor_tensor(Lt[:], bc(cbi[:, :, hs].unsqueeze(2), [P, NB, NA, HG]),
                                           bc(p2[:, :, hs].unsqueeze(1), [P, NB, NA, HG]), ALU.mult))
                    dve.tensor_tensor(L[:], L[:], Lt[:], ALU.add).then_inc(l_ready, 1)

                @block.tensor
                def _(pe):
                    pe.wait_ge(l_ready, 1)
                    Lf = L[:].rearrange("p c a h -> p (c a) h")
                    for j in range(HG):
                        per = 512 // NV
                        mm = pe.matmul(g.ps[0:NB * NA, j // per, (j % per) * NV:(j % per + 1) * NV],
                                       Lf[:, :, j], V[:, :, bass.ds(r * HG + j, 1)].rearrange("p v o -> p (v o)"),
                                       start=True, stop=True)
                        if j % per == per - 1:
                            mm.then_inc(k_ready, 1)

                @block.scalar
                def _(act):
                    kof = ko[:].rearrange("p h v -> p (h v)")
                    for k in range(NBK):
                        act.wait_ge(k_ready, k + 1)
                        act.activation(kof[:, k * 512:(k + 1) * 512], g.ps[0:NB * NA, k, :], ACT.Copy
                                       ).then_inc(k_out, 1)

                @block.sync
                def _(sp):
                    sp.wait_ge(k_out, NBK)
                    for b in range(NB):
                        dst = g.scr_ssm[b][bass.ds(r * HG, HG), :].rearrange("h (a v) -> a h v", a=NA)
                        sp.dma_start(dst, ko[b * NA:(b + 1) * NA]).then_inc(stored, 16)
                    sp.wait_ge(stored, 16 * NB)
            s.round_end()
        with nc.Block() as block:
            @block.sync
            def _(sp):
                for b in range(NB):
                    sp.dma_start(g.h[:, 0:2, b, :], g.scr_ssm[b].rearrange("(c p) n -> p c n", p=P)
                                 ).then_inc(back, 16)
                sp.wait_ge(back, 16 * NB)
        s.round_end()


def deltanet(nc, g):
    NG = 4
    E1 = 33
    with Scope(nc) as s:
        wqk = s.sb("dn_wqk", [P, 2, DC, D])
        wv = s.sb("dn_wv", [P, DC, D + 40])
        wout = s.sb("dn_wout", [P, DC, D])
        rows = s.sb("dn_rows", [P, 3 * D + 40 + 16])
        masks = s.sb("dn_masks", [P, 3 * P + 2 * 4 * E1])
        selc = s.sb("dn_sel", [48, 16, P], BF16)
        identb = s.sb("dn_identb", [P, P], BF16)
        S = s.sb("dn_state", [P, NB, 2, 2 * 4 * E1])
        xn, xnb, hb = s.sb("dn_xn", [P, NB, D]), s.sb("dn_xnb", [P, NB, D]), s.sb("dn_hb", [P, NB, D])
        xnT = s.sb("dn_xnT", [P, DC, NB * P])
        qT, kT = s.sb("dn_qT", [P, 2, NB * P]), s.sb("dn_kT", [P, 2, NB * P])
        er = s.sb("dn_exp_relu", [P, 2, 2, NB * P])
        kt, vt = s.sb("dn_k", [P, NB, D]), s.sb("dn_v", [P, NB, D + 40])
        er2 = s.sb("dn_exp_relu2", [P, 2, 2, D])
        raw = s.sb("dn_gates_raw", [P, NB, 40])
        eb = s.sb("dn_gates_exp", [P, NB, 40])
        lb = s.sb("dn_logdecay", [P, NB, 16])
        gate = s.sb("dn_gate", [P, NB, 8])
        wmix = s.sb("dn_wmix", [P, NB, 16])
        mtmp = s.sb("dn_mixtmp", [P, NB, 8])
        cc = s.sb("dn_cum", [P, 2, NB, 16])
        cres = s.sb("dn_cres", [P, 2, NB, 16])
        csp = s.sb("dn_csplit", [P, NB, 3, 16], BF16)
        crows = s.sb("dn_crows", [48, NB * P], BF16)
        ec, kd, dtot = s.sb("dn_ec", [P, NB, 16]), s.sb("dn_kd", [P, NB, 16]), s.sb("dn_dtot", [P, NB, 16])
        vg = s.sb("dn_vg", [P, NB, 8, E1])
        kdk = s.sb("dn_kdk", [P, NB, 2, 8, 32])
        Eb, Db, Mb = (s.sb(f"dn_{n}", [P, 2, 4, P]) for n in ("expo", "decay", "masked"))
        zt, um = s.sb("dn_zt", [P, 2, 2, 8, E1]), s.sb("dn_um", [P, 2, 2 * 4 * E1])
        den = s.sb("dn_den", [P, 2, 16])
        yy = s.sb("dn_y2", [P, 2, 8, 32])
        y = s.sb("dn_y", [P, NB, D])
        yT = s.sb("dn_yT", [P, DC, NB * P])
        stats, mv, rs, ltmp = s.sb("dn_stats", [P, NB, 6]), s.sb("dn_mv", [P, NB, 2]), s.sb("dn_rs", [P, NB]), s.sb("dn_ltmp", [P, 2, NB])
        bout, lng, lnb, gb, floor = (rows[:, 0:D], rows[:, D:2 * D], rows[:, 2 * D:3 * D],
                                     rows[:, 3 * D:3 * D + 40], rows[:, 3 * D + 40:3 * D + 56])
        tri_le, ones, cmask = masks[:, 0:P], masks[:, P:2 * P], masks[:, 2 * P:3 * P]
        bdmask = masks[:, 3 * P:3 * P + 2 * 4 * E1]
        kt_u = kt[:].rearrange("p b (f r e) -> p b (f r) e", f=2, r=4)

        with Scope(nc) as u:
            loaded = u.sem("dn_loaded")
            with nc.Block() as block:
                @block.sync
                def _(sp):
                    for dst, n in ((wqk[:], "dn_wqk"), (wv[:], "dn_wv"), (wout[:], "dn_wout"), (rows[:], "dn_rows"),
                                   (masks[:], "dn_masks"), (selc[:], "dn_sel"), (identb[:], "identb")):
                        sp.dma_start(dst, g.d[n]).then_inc(loaded, 16)
                    sp.wait_ge(loaded, 16 * 7)

                @block.vector
                def _(dve):
                    dve.memset(S[:], 0.0)
            u.round_end()

        names = ("vchain achain pchain xn_ready xnT_psum xnT_ready fm_psum fm_act qk_ready tm_psum tm_act tm_free tm_ready "
                 "gates_raw gates_exp mix_shift decay_arg decay_log c_psum c_ready csplit_ready crows_psum crows_ready "
                 "ec_ready kd_arg kd_ready vg_ready kdk_ready ae_psum e_used m_done d_ready y_psum mm_done z_psum "
                 "z_used u_psum um_ready s_ready comb_done y_read yT_psum yT_ready out_psum out_sum xnb_ready hb_ready").split()
        q = {n: s.sem("dn_" + n) for n in names}
        (vchain, achain, pchain, xn_ready, xnT_psum, xnT_ready, fm_psum, fm_act, qk_ready, tm_psum, tm_act, tm_free, tm_ready,
         gates_raw, gates_exp, mix_shift, decay_arg, decay_log, c_psum, c_ready, csplit_ready, crows_psum, crows_ready,
         ec_ready, kd_arg, kd_ready, vg_ready, kdk_ready, ae_psum, e_used, m_done, d_ready, y_psum, mm_done, z_psum,
         z_used, u_psum, um_ready, s_ready, comb_done, y_read, yT_psum, yT_ready, out_psum, out_sum, xnb_ready, hb_ready) = (
             q[n] for n in names)
        ps = g.ps
        tmA = [6, 0, 6, 0]
        tmB = [7, 1, 7, 1]

        with nc.Fori(0, NC) as c:
            hc = g.h[:, bass.ds(c, 1)].rearrange("p o b n -> p (o b) n")
            with nc.Block() as block:
                @block.tensor
                def _(pe):
                    pe.wait_ge(xn_ready, 1)
                    for d in range(DC):
                        for b in range(NB):
                            mm = pe.transpose(ps[:, d, b * P:(b + 1) * P], xn[:, b, d * P:(d + 1) * P], g.ident[:])
                    mm.then_inc(xnT_psum, 1)
                    pe.wait_ge(xnT_ready, 1)
                    for w in range(2):
                        for f in range(2):
                            for d in range(DC):
                                mm = pe.matmul(ps[:, 2 + 2 * w + f, :], wqk[:, w, d, f * P:(f + 1) * P], xnT[:, d, :],
                                               start=(d == 0), stop=(d == DC - 1))
                            mm.then_inc(fm_psum, 1)
                    for b in range(NB):
                        if b >= 2:
                            pe.wait_ge(tm_act, b - 1)
                        for d in range(DC):
                            pe.matmul(ps[:, tmA[b], 0:D + 40], xnT[:, d, b * P:(b + 1) * P], wv[:, d, :],
                                      start=(d == 0), stop=(d == DC - 1))
                        for d in range(DC):
                            mm = pe.matmul(ps[:, tmB[b], 0:D], xnT[:, d, b * P:(b + 1) * P], wqk[:, 1, d, :],
                                           start=(d == 0), stop=(d == DC - 1))
                        mm.then_inc(tm_psum, 1)
                    pe.wait_ge(decay_log, 1)
                    pe.wait_ge(fm_act, 4)
                    lbf = lb[:].rearrange("p b j -> p (b j)")
                    pe.matmul(ps[:, 2, 0:64], tri_le, lbf, start=True, stop=True)
                    pe.matmul(ps[:, 2, 64:128], ones, lbf, start=True, stop=True).then_inc(c_psum, 1)
                    pe.wait_ge(csplit_ready, 1)
                    crp = ps[0:48, 3, :].bitcast(BF16)
                    for b in range(NB):
                        mm = pe.transpose(crp[:, b * P:(b + 1) * P],
                                          csp[:, b].rearrange("p k j -> p (k j)"), identb[:])
                    mm.then_inc(crows_psum, 1)
                    pe.wait_ge(crows_ready, 1)
                    pe.wait_ge(qk_ready, 4)
                    pe.wait_ge(vg_ready, NB)
                    pe.wait_ge(tm_ready, NB)
                    for n in range(NB * NG + 2):
                        if n < NB * NG:
                            b, r = divmod(n, NG)
                            bs = slice(b * P, (b + 1) * P)
                            if r == 0:
                                if b >= 1:
                                    pe.wait_ge(um_ready, b)
                                for f in range(2):
                                    mm = pe.matmul(ps[:, 2 + f, 0:8 * E1], qT[:, f, bs], S[:, b, f, :],
                                                   start=True, stop=True)
                                mm.then_inc(z_psum, 1)
                            if n >= 2:
                                pe.wait_ge(m_done, n - 1)
                                pe.wait_ge(e_used, n - 1)
                            hr = slice(32 * r, 32 * r + 32)
                            for f in range(2):
                                pe.matmul(ps[:, 4 + n % 2, f * P:(f + 1) * P],
                                          kT[hr, f, bs], qT[hr, f, bs], start=True, stop=True)
                            for f in range(2):
                                for j in range(2):
                                    k = 2 * f + j
                                    mm = pe.matmul(ps[:, 6 + n % 2, k * P:(k + 1) * P], selc[:, f * 8 + j * 4 + r, :],
                                                   crows[:, bs], start=True, stop=True)
                            mm.then_inc(ae_psum, 1)
                            if r == 2:
                                pe.wait_ge(z_used, b + 1)
                                pe.wait_ge(kdk_ready, b + 1)
                                for f in range(2):
                                    for j in range(2):
                                        mm = pe.matmul(ps[:, 2 + f, j * 4 * E1:(j + 1) * 4 * E1],
                                                       kdk[:, b, j, 4 * f:4 * f + 4, :].rearrange("p h e -> p (h e)"),
                                                       vg[:, b, 4 * f:4 * f + 4, :].rearrange("p h e -> p (h e)"),
                                                       start=True, stop=True)
                                mm.then_inc(u_psum, 1)
                        if n >= 2:
                            b, r = divmod(n - 2, NG)
                            pe.wait_ge(m_done, n - 1)
                            if r == 0 and b >= 1:
                                pe.wait_ge(y_read, b)
                            for f in range(2):
                                for j in range(2):
                                    at = j * 4 * E1 + r * E1
                                    mm = pe.matmul(ps[:, f, at:at + E1], Mb[:, n % 2, 2 * f + j, :],
                                                   vg[:, b, 4 * f + r, :], start=True, stop=True)
                            mm.then_inc(y_psum, 1)
                    pe.wait_ge(comb_done, NB)
                    for d in range(DC):
                        for b in range(NB):
                            mm = pe.transpose(ps[:, 6 + d, b * P:(b + 1) * P], y[:, b, d * P:(d + 1) * P], g.ident[:])
                    mm.then_inc(yT_psum, 1)
                    pe.wait_ge(yT_ready, 1)
                    for b in range(NB):
                        for d in range(DC):
                            mm = pe.matmul(ps[:, b, 0:D], yT[:, d, b * P:(b + 1) * P], wout[:, d, :],
                                           start=(d == 0), stop=(d == DC - 1))
                        mm.then_inc(out_psum, 1)

                @block.scalar
                def _(act):
                    act.wait_ge(xnT_psum, 1)
                    act.activation(xnT[:, 0, :], ps[:, 0, :], ACT.Copy)
                    act.activation(xnT[:, 1, :], ps[:, 1, :], ACT.Copy).then_inc(xnT_ready, 1)
                    for k in range(4):
                        act.wait_ge(fm_psum, k + 1)
                        if k >= 2:
                            act.wait_ge(qk_ready, k - 1)
                        act.activation(er[:, k % 2, 0, :], ps[:, 2 + k, :], ACT.Exp)
                        act.activation(er[:, k % 2, 1, :], ps[:, 2 + k, :], ACT.Relu).then_inc(fm_act, 1)
                    for b in range(NB):
                        act.wait_ge(tm_psum, b + 1)
                        if b >= 2:
                            act.wait_ge(tm_ready, b - 1)
                        act.activation(vt[:, b, :], ps[:, tmA[b], 0:D + 40], ACT.Copy)
                        act.activation(er2[:, b % 2, 0, :], ps[:, tmB[b], 0:D], ACT.Exp)
                        act.activation(er2[:, b % 2, 1, :], ps[:, tmB[b], 0:D], ACT.Relu).then_inc(tm_act, 1)
                    act.wait_ge(gates_raw, 1)
                    act.activation(eb[:, :, 0:16], raw[:, :, 0:16], ACT.Exp, scale=-1.0)
                    act.activation(eb[:, :, 32:40], raw[:, :, 32:40], ACT.Exp, scale=-1.0).then_inc(gates_exp, 1)
                    act.wait_ge(mix_shift, 1)
                    act.activation(eb[:, :, 16:32], raw[:, :, 16:32], ACT.Exp).then_inc(gates_exp, 1)
                    act.wait_ge(decay_arg, 1)
                    act.activation(lb[:], eb[:, :, 0:16], ACT.Ln).then_inc(decay_log, 1)
                    act.wait_ge(c_ready, 1)
                    act.activation(ec[:], cc[:, 0], ACT.Exp)
                    act.activation(dtot[:], cc[:, 1], ACT.Exp).then_inc(ec_ready, 1)
                    act.wait_ge(kd_arg, 1)
                    act.activation(kd[:], cres[:, 1], ACT.Exp).then_inc(kd_ready, 1)
                    act.wait_ge(crows_psum, 1)
                    act.activation(crows[:], ps[0:48, 3, 0:NB * P // 2].bitcast(BF16), ACT.Copy).then_inc(crows_ready, 1)
                    for n in range(NB * NG):
                        act.wait_ge(e_used, n + 1)
                        if n >= 2:
                            act.wait_ge(m_done, n - 1)
                        act.activation(Db[:, n % 2], Eb[:, n % 2], ACT.Exp).then_inc(d_ready, 1)
                    act.wait_ge(yT_psum, 1)
                    act.activation(yT[:, 0, :], ps[:, 6, :], ACT.Copy)
                    act.activation(yT[:, 1, :], ps[:, 7, :], ACT.Copy).then_inc(yT_ready, 1)

                @block.gpsimd
                def _(pool):
                    pool.wait_ge(xn_ready, 1)
                    pool.tensor_tensor(xnb[:], xn[:], bc(bout.unsqueeze(1), [P, NB, D]), ALU.add).then_inc(xnb_ready, 1)
                    pool.tensor_tensor(hb[:], hc, bc(lnb.unsqueeze(1), [P, NB, D]), ALU.add).then_inc(hb_ready, 1)
                    pool.wait_ge(kd_ready, 1)
                    pool.wait_ge(tm_ready, NB)
                    pool.wait_ge(vg_ready, NB)
                    for b in range(NB):
                        for j in range(2):
                            for f in range(2):
                                k = 8 * f + 4 * j
                                op = pool.tensor_tensor(kdk[:, b, j, 4 * f:4 * f + 4, :], kt_u[:, b, 4 * f:4 * f + 4, :],
                                                        bc(kd[:, b, k:k + 4].unsqueeze(2), [P, 4, 32]), ALU.mult)
                        op.then_inc(kdk_ready, 1)
                    for b in range(NB):
                        pool.wait_ge(z_psum, b + 1)
                        Sb = S[:, b].rearrange("p f (k e) -> p (f k) e", e=E1)
                        pool.tensor_tensor(Sb, Sb, bc(dtot[:, b].unsqueeze(2), [P, 16, E1]), ALU.mult).then_inc(pchain, 1)
                        pool.wait_ge(pchain, b + 1)
                        pool.wait_ge(um_ready, b + 1)
                        pool.tensor_tensor(S[:, b], S[:, b], um[:], ALU.add).then_inc(s_ready, 1)

                @block.vector
                def _(dve):
                    link = chain(dve, vchain)
                    layernorm(dve, link, [hc[:, b, :] for b in range(NB)], [xn[:, b, :] for b in range(NB)],
                              stats, mv, rs, ltmp)
                    dve.engine_nop().then_inc(xn_ready, 1)
                    for k in range(4):
                        dve.wait_ge(fm_act, k + 1)
                        dst = (qT, kT)[k // 2][:, k % 2, :]
                        dve.scalar_tensor_tensor(dst, er[:, k % 2, 0, :], 1.0, er[:, k % 2, 1, :], ALU.min, ALU.add
                                                 ).then_inc(qk_ready, 1)
                    for b in range(NB):
                        dve.wait_ge(tm_act, b + 1)
                        dve.tensor_tensor(raw[:, b], vt[:, b, D:D + 40], gb, ALU.add).then_inc(tm_free, 1)
                        dve.scalar_tensor_tensor(kt[:, b], er2[:, b % 2, 0], 1.0, er2[:, b % 2, 1], ALU.min, ALU.add
                                                 ).then_inc(tm_ready, 1)
                    dve.wait_ge(tm_free, NB)
                    dve.engine_nop().then_inc(gates_raw, 1)
                    mix = raw[:, :, 16:32].rearrange("p b (f j r) -> p b f j r", f=2, j=2)
                    mt = mtmp[:].rearrange("p b (f r) -> p b f r", f=2)
                    link(dve.tensor_tensor(mt, mix[:, :, :, 0], mix[:, :, :, 1], ALU.max))
                    dve.tensor_tensor(mix[:, :, :, 0], mix[:, :, :, 0], mt, ALU.subtract)
                    dve.tensor_tensor(mix[:, :, :, 1], mix[:, :, :, 1], mt, ALU.subtract).then_inc(mix_shift, 1)
                    dve.wait_ge(gates_exp, 1)
                    dve.tensor_scalar(eb[:, :, 0:16], eb[:, :, 0:16], 1.0, None, ALU.add)
                    link(dve.tensor_scalar(eb[:, :, 32:40], eb[:, :, 32:40], 1.0, None, ALU.add))
                    dve.reciprocal(gate[:], eb[:, :, 32:40])
                    link(dve.reciprocal(lb[:], eb[:, :, 0:16]))
                    link(dve.tensor_tensor(lb[:], lb[:], bc(floor.unsqueeze(1), [P, NB, 16]), ALU.mult))
                    dve.tensor_scalar(eb[:, :, 0:16], lb[:], 0.9999, 1e-19, ALU.min, ALU.max).then_inc(decay_arg, 1)
                    for b in range(NB):
                        vgb = vg[:, b]
                        dve.tensor_tensor(vgb[:, :, 0:32], vt[:, b, 0:D].rearrange("p (h e) -> p h e", h=8),
                                          bc(gate[:, b].unsqueeze(2), [P, 8, 32]), ALU.mult)
                        dve.tensor_copy(vgb[:, :, 32], gate[:, b]).then_inc(vg_ready, 1)
                    dve.wait_ge(gates_exp, 2)
                    em = eb[:, :, 16:32].rearrange("p b (f j r) -> p b f j r", f=2, j=2)
                    wm = wmix[:].rearrange("p b (f j r) -> p b f j r", f=2, j=2)
                    link(dve.tensor_tensor(mt, em[:, :, :, 0], em[:, :, :, 1], ALU.add))
                    link(dve.reciprocal(mt, mt))
                    dve.tensor_tensor(wm[:, :, :, 0], em[:, :, :, 0], mt, ALU.mult)
                    link(dve.tensor_tensor(wm[:, :, :, 1], em[:, :, :, 1], mt, ALU.mult))
                    dve.wait_ge(c_psum, 1)
                    dve.tensor_copy(cc[:].rearrange("p k b j -> p (k b j)"), ps[:, 2, 0:128]).then_inc(c_ready, 1)
                    dve.wait_ge(c_ready, 1)
                    dve.tensor_tensor(cres[:, 1], cc[:, 1], cc[:, 0], ALU.subtract).then_inc(kd_arg, 1)
                    link(dve.tensor_copy(csp[:, :, 0], cc[:, 0]))
                    link(dve.tensor_tensor(cres[:, 0], cc[:, 0], csp[:, :, 0], ALU.subtract))
                    link(dve.tensor_copy(csp[:, :, 1], cres[:, 0]))
                    link(dve.tensor_tensor(cres[:, 0], cres[:, 0], csp[:, :, 1], ALU.subtract))
                    dve.tensor_copy(csp[:, :, 2], cres[:, 0]).then_inc(csplit_ready, 1)
                    for n in range(NB * NG + 3):
                        if 1 <= n <= NB * NG:
                            dve.wait_ge(d_ready, n)
                            if n >= 3:
                                dve.wait_ge(y_psum, n - 2)
                            a = ps[:, 4 + (n - 1) % 2, 0:256].rearrange("p (f t) -> p f t", f=2)
                            dve.tensor_tensor(Mb[:, (n - 1) % 2].rearrange("p (f j) t -> p f j t", f=2),
                                              Db[:, (n - 1) % 2].rearrange("p (f j) t -> p f j t", f=2),
                                              bc(a.unsqueeze(2), [P, 2, 2, P]), ALU.mult).then_inc(m_done, 1)
                        if n < NB * NG:
                            b, r = divmod(n, NG)
                            dve.wait_ge(ae_psum, n + 1)
                            if n >= 2:
                                dve.wait_ge(d_ready, n - 1)
                            for f in range(2):
                                for j in range(2):
                                    k, hj = 2 * f + j, 8 * f + 4 * j + r
                                    op = dve.scalar_tensor_tensor(Eb[:, n % 2, k, :], ps[:, 6 + n % 2, k * P:(k + 1) * P],
                                                                  cc[:, 0, b, hj:hj + 1], cmask, ALU.subtract, ALU.min)
                            op.then_inc(e_used, 1)
                            if r == 0:
                                dve.wait_ge(z_psum, b + 1)
                                dve.wait_ge(ec_ready, 1)
                                dve.tensor_tensor(zt[:, b % 2], ps[:, 2:4, 0:8 * E1].rearrange("p f (k e) -> p f k e", e=E1),
                                                  bc(ec[:, b].rearrange("p (f k) -> p f k", f=2).unsqueeze(3), [P, 2, 8, E1]),
                                                  ALU.mult).then_inc(z_used, 1)
                            if r == 3:
                                dve.wait_ge(u_psum, b + 1)
                                if b >= 1:
                                    dve.wait_ge(s_ready, b)
                                dve.tensor_tensor(um[:], ps[:, 2:4, 0:8 * E1],
                                                  bc(bdmask.unsqueeze(1), [P, 2, 8 * E1]), ALU.mult).then_inc(um_ready, 1)
                        if n >= 3 and (n - 3) % NG == NG - 1:
                            b = (n - 3) // NG
                            dve.wait_ge(y_psum, n - 2)
                            yp = ps[:, 0:2, 0:8 * E1].rearrange("p f (k e) -> p f k e", e=E1)
                            zb = zt[:, b % 2]
                            dve.tensor_tensor(zb, zb, yp, ALU.add).then_inc(y_read, 1)
                            dve.wait_ge(y_read, b + 1)
                            link(dve.tensor_scalar(den[:, 0].rearrange("p (f k) -> p f k", f=2), zb[:, :, :, 32], 1e-6,
                                                   None, ALU.add))
                            link(dve.reciprocal(den[:, 1], den[:, 0]))
                            link(dve.tensor_tensor(den[:, 0], den[:, 1], wmix[:, b], ALU.mult))
                            dw = den[:, 0].rearrange("p (f k) -> p f k", f=2)
                            for j in range(2):
                                op = dve.tensor_tensor(yy[:, j].rearrange("p (f r) e -> p f r e", f=2),
                                                       zb[:, :, 4 * j:4 * j + 4, 0:32],
                                                       bc(dw[:, :, 4 * j:4 * j + 4].unsqueeze(3), [P, 2, 4, 32]), ALU.mult)
                            link(op)
                            dve.tensor_tensor(y[:, b].rearrange("p (h e) -> p h e", e=32), yy[:, 0], yy[:, 1], ALU.add
                                              ).then_inc(comb_done, 1)
                    dve.wait_ge(xnb_ready, 1)
                    for b in range(NB):
                        dve.wait_ge(out_psum, b + 1)
                        dve.tensor_tensor(xnb[:, b], xnb[:, b], ps[:, b, 0:D], ALU.add).then_inc(out_sum, 1)
                    dve.wait_ge(out_sum, NB)
                    layernorm(dve, link, [xnb[:, b, :] for b in range(NB)], [y[:, b, :] for b in range(NB)],
                              stats, mv, rs, ltmp)
                    link(dve.tensor_tensor(y[:], y[:], bc(lng.unsqueeze(1), [P, NB, D]), ALU.mult))
                    dve.wait_ge(hb_ready, 1)
                    dve.tensor_tensor(hc, y[:], hb[:], ALU.add)
            s.round_end()


def pick_top(dve, link, vals, k, v8, sel, eq, cum, cnt, ones):
    n, E = vals.shape[1], vals.shape[2]
    for i in range(n):
        op = dve.max(v8[:, i, :], vals[:, i, :])
    link(op)
    t = bc(v8[:, 0:n, k - 1:k], [P, n, E])
    dve.tensor_tensor(eq, vals, t, ALU.is_equal)
    link(dve.tensor_tensor(sel, vals, t, ALU.is_gt))
    dve.tensor_reduce(cnt[:, 0:n], sel, AX_X, ALU.add)
    for i in range(n):
        op = dve.tensor_tensor_scan(cum[:, i, :], ones[:, 0:E], eq[:, i, :], 0.0, ALU.mult, ALU.add)
    link(op)
    link(dve.tensor_tensor(cum, cum, bc(cnt[:, 0:n].unsqueeze(2), [P, n, E]), ALU.add))
    link(dve.tensor_scalar(cum, cum, float(k), None, ALU.is_le))
    link(dve.tensor_tensor(eq, eq, cum, ALU.mult))
    link(dve.tensor_tensor(sel, sel, eq, ALU.add))


def attn_project(nc, g):
    with Scope(nc) as s:
        wqk, wv = s.sb("ap_wqk", [P, 2, DC, D]), s.sb("ap_wv", [P, DC, D])
        rows = s.sb("ap_rows", [P, 3 * D])
        qkb = s.sb("ap_qkb", [P, 4])
        nx2 = s.sb("ap_nx", [P, 2, NB, D])
        nxT2 = s.sb("ap_nxT", [P, 2, DC, NB * P])
        res2 = s.sb("ap_res", [P, 2, 4, NB * P])
        parts2 = s.sb("ap_parts", [P, 2, 4, 3, NB * P], BF16)
        stats, mv, rs, ltmp = s.sb("ap_stats", [P, NB, 6]), s.sb("ap_mv", [P, NB, 2]), s.sb("ap_rs", [P, NB]), s.sb("ap_ltmp", [P, 2, NB])
        with Scope(nc) as u:
            loaded = u.sem("ap_loaded")
            with nc.Block() as block:
                @block.sync
                def _(sp):
                    for dst, n in ((wqk[:], "at_wqk"), (wv[:], "at_wv"), (rows[:], "at_rows"), (qkb[:], "at_qkb")):
                        sp.dma_start(dst, g.d[n]).then_inc(loaded, 16)
                    sp.wait_ge(loaded, 16 * 4)
            u.round_end()
        vchain, nx_ready, nxT_psum, nxT_ready = s.sem("ap_vchain"), s.sem("ap_nx"), s.sem("ap_nxT_psum"), s.sem("ap_nxT")
        qk_psum, v_psum, v_used, res_ready, part_ready, stored = (s.sem("ap_qk_psum"), s.sem("ap_v_psum"), s.sem("ap_v_used"), s.sem("ap_res_ready"),
                                                          s.sem("ap_part"), s.sem("ap_stored"))
        ps = g.ps
        with nc.Fori(0, NC // 2) as r:
            def at_chunk(t, u, pat):
                return t[:, bass.ds(r * 2 + u, 1)].rearrange(pat)
            with nc.Block() as block:
                @block.tensor
                def _(pe):
                    for u in range(2):
                        nx, nxT = nx2[:, u], nxT2[:, u]
                        pe.wait_ge(nx_ready, u + 1)
                        for d in range(DC):
                            for b in range(NB):
                                mm = pe.transpose(ps[:, d, b * P:(b + 1) * P], nx[:, b, d * P:(d + 1) * P], g.ident[:])
                        mm.then_inc(nxT_psum, 1)
                        pe.wait_ge(nxT_ready, u + 1)
                        for w in range(2):
                            for f in range(2):
                                if u:
                                    pe.wait_ge(res_ready, 2 * w + f + 1)
                                for d in range(DC):
                                    mm = pe.matmul(ps[:, 2 + 2 * w + f, :], wqk[:, w, d, f * P:(f + 1) * P], nxT[:, d, :],
                                                   start=(d == 0), stop=(d == DC - 1))
                                mm.then_inc(qk_psum, 1)
                        for b in range(NB):
                            if u and b % 2 == 0:
                                pe.wait_ge(v_used, b // 2 + 1)
                            for d in range(DC):
                                mm = pe.matmul(ps[:, 6 + b // 2, (b % 2) * D:(b % 2 + 1) * D], nxT[:, d, b * P:(b + 1) * P],
                                               wv[:, d, :], start=(d == 0), stop=(d == DC - 1))
                            if b % 2:
                                mm.then_inc(v_psum, 1)

                @block.scalar
                def _(act):
                    def rows_to_sbuf(u):
                        act.wait_ge(nxT_psum, u + 1)
                        act.activation(nxT2[:, u, 0, :], ps[:, 0, :], ACT.Copy)
                        act.activation(nxT2[:, u, 1, :], ps[:, 1, :], ACT.Copy).then_inc(nxT_ready, 1)
                    rows_to_sbuf(0)
                    for u in range(2):
                        for part in range(3):
                            if u == 0 and part == 1:
                                rows_to_sbuf(1)
                            for k in range(4):
                                act.wait_ge(res_ready, 12 * u + 4 * part + k + 1)
                                act.activation(parts2[:, u, k, part, :], res2[:, u, k, :], ACT.Copy).then_inc(part_ready, 1)

                @block.sync
                def _(sp):
                    for u in range(2):
                        for part in range(3):
                            sp.wait_ge(part_ready, 12 * u + 4 * (part + 1))
                            for k in range(4):
                                dst = g.scr_qk[k // 2, part, (k % 2) * P:(k % 2 + 1) * P, :, bass.ds((r * 2 + u) * P, P)]
                                sp.dma_start(dst, parts2[:, u, k, part, :].rearrange("p (b t) -> p b t", b=NB)
                                             ).then_inc(stored, 16)
                    sp.wait_ge(stored, 16 * 24)

                @block.vector
                def _(dve):
                    link = chain(dve, vchain)

                    def norms(u):
                        hc, zc = at_chunk(g.h, u, "p o b n -> p (o b) n"), at_chunk(g.z, u, "p o b n -> p (o b) n")
                        nx = nx2[:, u]
                        layernorm(dve, link, [hc[:, b, :] for b in range(NB)], [zc[:, b, :] for b in range(NB)],
                                  stats, mv, rs, ltmp)
                        layernorm(dve, link, [zc[:, b, :] for b in range(NB)], [nx[:, b, :] for b in range(NB)],
                                  stats, mv, rs, ltmp)
                        link(dve.tensor_tensor(nx, nx, bc(rows[:, 0:D].unsqueeze(1), [P, NB, D]), ALU.mult))
                        dve.tensor_tensor(nx, nx, bc(rows[:, D:2 * D].unsqueeze(1), [P, NB, D]), ALU.add
                                          ).then_inc(nx_ready, 1)

                    def results(u):
                        vc = at_chunk(g.v, u, "p o b h e -> p (o b) h e")
                        res = res2[:, u]
                        for k in range(4):
                            dve.wait_ge(qk_psum, 4 * u + k + 1)
                            dve.tensor_scalar(res[:, k, :], ps[:, 2 + k, :], qkb[:, k:k + 1], 0.25 if k < 2 else 1.0,
                                              ALU.add, ALU.mult).then_inc(res_ready, 1)
                        for m in range(2):
                            dve.wait_ge(v_psum, 2 * u + m + 1)
                            dve.tensor_tensor(vc[:, 2 * m:2 * m + 2], ps[:, 6 + m, :].rearrange("p (b h e) -> p b h e", b=2, h=16),
                                              bc(rows[:, 2 * D:3 * D].rearrange("p (h e) -> p h e", h=16).unsqueeze(1),
                                                 [P, 2, 16, 16]), ALU.add).then_inc(v_used, 1)
                        for part in range(2):
                            for k in range(4):
                                dve.wait_ge(part_ready, 12 * u + 4 * part + k + 1)
                                dve.tensor_tensor(res[:, k, :], res[:, k, :], parts2[:, u, k, part, :], ALU.subtract
                                                  ).then_inc(res_ready, 1)
                    for u in range(2):
                        norms(u)
                    for u in range(2):
                        results(u)
            s.round_end()


def attn_heads(nc, g):
    NH, E = 16, 16
    KT, QT = (0, 1, 0, 2, 0, 1), (0, 0, 1, 0, 2, 1)
    blocks = [(kb, qc) for kb in range(NC) for qc in range(kb, NC)]
    at = {kq: i for i, kq in enumerate(blocks)}
    cuts = [0, 4, 8, 12, 15, 18, 21]
    pieces = []
    for a, z in zip(cuts, cuts[1:]):
        runs = []
        for i in range(a, z):
            kb, qc = blocks[i]
            if runs and runs[-1][0] == kb:
                runs[-1][2] += 1
            else:
                runs.append([kb, qc, 1, i - a])
        pieces.append((a, z - a, runs))
    NPC = len(pieces)
    MAX_AT = 2
    with Scope(nc) as s:
        k6, q6 = s.sb("ah_k6", [99, NH, SEQ], BF16), s.sb("ah_q6", [99, NH, SEQ], BF16)
        vb = s.sb("ah_v", [P, NC, NH // 2, 2, 4 * E])
        probs = s.sb("ah_probs", [P, 2, len(blocks) * P])
        consts = s.sb("ah_consts", [P, 3 * P], BF16)
        mx = s.sb("ah_max", [P, 2, NC])
        mres = s.sb("ah_mres", [P, NC])
        msp = s.sb("ah_msplit", [P, 2, NC, 4], BF16)
        num, den = s.sb("ah_num", [2 * E, SEQ]), s.sb("ah_den", [2 * E, SEQ])
        identb, qmask, kmask = (consts[:, i * P:(i + 1) * P] for i in range(3))
        with Scope(nc) as u:
            loaded, zeroed = u.sem("ah_loaded"), u.sem("ah_zeroed")
            with nc.Block() as block:
                @block.sync
                def _(sp):
                    sp.dma_start(consts[:], g.d["at_consts"]).then_inc(loaded, 16)
                    sp.wait_ge(loaded, 16)

                @block.vector
                def _(dve):
                    dve.memset(k6[96:99], -1.0)
                    dve.memset(vb[:], 0.0).then_inc(zeroed, 1)
                    dve.wait_ge(zeroed, 1)
                    for k in range(2):
                        sums = vb[:, :, :, k, (2 + k) * E:(3 + k) * E].rearrange("p c q e -> p (c q) e")
                        dve.memset(sums, 1.0)
            u.round_end()
        qk_loaded = [s.sem(f"ah_qk_loaded{i}") for i in range(4)]
        vchain, v_ready, s_psum, s_used, msp_ready, mT_psum, mT_ready, e_psum, e_done, o_psum, o_used, inverted, o_ready = (
            s.sem("ah_" + n) for n in "vchain v_ready s_psum s_used msp_ready mT_psum mT_ready e_psum e_done o_psum o_used inverted o_ready".split())
        ps = g.ps
        with nc.Fori(0, NB) as b:
            with nc.Block() as block:
                @block.sync
                def _(sp):
                    for hq in range(4):
                        for t in range(6):
                            for w, dst, part in ((0, q6, QT[t]), (1, k6, KT[t])):
                                src = g.scr_qk[w, part, 64 * hq:64 * hq + 64, bass.ds(b, 1), :]
                                sp.dma_start(dst[16 * t:16 * t + 16, 4 * hq:4 * hq + 4, :],
                                             src.rearrange("(h e) o s -> e h (o s)", e=E)).then_inc(qk_loaded[hq], 16)

                @block.gpsimd
                def _(pool):
                    vh = g.v[:, :, bass.ds(b, 1)].rearrange("p c o (q k) e -> p c (o q) k e", k=2)
                    for k in range(2):
                        op = pool.tensor_copy(vb[:, :, :, k, k * E:(k + 1) * E], vh[:, :, :, k, :])
                    op.then_inc(v_ready, 1)
                    for q in range(NH // 2):
                        pool.wait_ge(inverted, q + 1)
                        dst = g.aT[(q % 4) * 2 * E:(q % 4 + 1) * 2 * E, q // 4, bass.ds(b, 1), :]
                        pool.tensor_tensor(dst.rearrange("p o n -> p (o n)"), num[:], den[:], ALU.mult).then_inc(o_ready, 1)

                @block.tensor
                def _(pe):
                    pe.wait_ge(v_ready, 1)
                    def scores(i, qc):
                        n = i * NC + qc
                        bank = 2 if qc in (1, 3) else 0
                        if n >= 2:
                            pe.wait_ge(s_used, n if qc in (0, 5) else n - 1)
                        k1 = min((qc + 1) * P, 512)
                        lhs = q6[0:96, i, qc * P:(qc + 1) * P]
                        pe.matmul(ps[:, bank, 0:k1], lhs, k6[0:96, i, 0:k1], start=True, stop=qc > 3)
                        if qc > 3:
                            k2 = (qc + 1) * P
                            pe.matmul(ps[:, bank + 1, 0:k2 - 512], lhs, k6[0:96, i, 512:k2], start=True, stop=False)
                        dk = (qc % 4) * P
                        pe.matmul(ps[:, bank + qc // 4, dk:dk + P], identb, qmask, start=False, stop=True).then_inc(s_psum, 1)

                    def maxima(h):
                        pe.wait_ge(msp_ready, h + 1)
                        if h >= 1:
                            pe.wait_ge(mT_ready, h)
                        for qc in range(NC):
                            mm = pe.transpose(ps[0:3, 3, :].bitcast(BF16)[:, qc * P:(qc + 1) * P], msp[:, h % 2, qc, 0:3], identb)
                        mm.then_inc(mT_psum, 1)

                    def exponents(h, p):
                        first, nb, runs = pieces[p]
                        if p == 0:
                            pe.wait_ge(mT_ready, h + 1)
                        n = h * NPC + p
                        bank = 4 + n % 2
                        if n >= 2:
                            pe.wait_ge(e_done, n - 1)
                        for kb, qc, m, off in runs:
                            o, w = ps[:, bank, off * P:(off + m) * P], slice(qc * P, (qc + m) * P)
                            mm = pe.matmul(o, k6[:, h, kb * P:(kb + 1) * P], q6[:, h, w], start=True, stop=qc != kb)
                            if qc == kb:
                                mm = pe.matmul(ps[:, bank, off * P:(off + 1) * P], identb, kmask, start=False, stop=True)
                        mm.then_inc(e_psum, 1)

                    def outputs(h, kb):
                        if kb == 0:
                            pe.wait_ge(e_done, NPC * (h + 1))
                            if h >= 2 and h % 2 == 0:
                                pe.wait_ge(o_used, h // 2)
                        for bank, lo, hi in ((6, 0, 512), (7, 512, SEQ)):
                            lo = max(lo, kb * P)
                            if lo < hi:
                                at0 = (at[kb, kb] - kb) * P
                                last = h % 2 == 1 and kb == hi // P - 1
                                mm = pe.matmul(ps[0:4 * E, bank, lo % 512:(hi - 1) % 512 + 1], vb[:, kb, h // 2, h % 2, :],
                                               probs[:, h % 2, at0 + lo:at0 + hi], start=(kb == 0 and h % 2 == 0), stop=last)
                        if kb == NC - 1:
                            mm.then_inc(o_psum, 1)

                    for i in range(NH + 3):
                        if i < NH and i % 4 == 0:
                            pe.wait_ge(qk_loaded[i // 4], 16 * 12)
                        for j in range(NC):
                            if i < NH:
                                scores(i, j)
                            if j == MAX_AT and 1 <= i <= NH:
                                maxima(i - 1)
                            if 2 <= i <= NH + 1:
                                exponents(i - 2, j)
                            if i >= 3:
                                outputs(i - 3, j)

                @block.scalar
                def _(act):
                    def take_outputs(q):
                        act.wait_ge(o_psum, 2 * (q + 1))
                        if q >= 1:
                            act.wait_ge(o_ready, q)
                        o = ps[:, 6:8, :].rearrange("p k n -> p (k n)")
                        act.activation(num[:], o[0:2 * E, 0:SEQ], ACT.Copy)
                        act.activation(den[:], o[2 * E:4 * E, 0:SEQ], ACT.Copy).then_inc(o_used, 1)

                    for h in range(NH):
                        for p, (first, nb, runs) in enumerate(pieces):
                            if p == 0 and h >= 3 and h % 2:
                                take_outputs((h - 3) // 2)
                            act.wait_ge(e_psum, h * NPC + p + 1)
                            if p == 0 and h >= 2:
                                act.wait_ge(o_psum, h - 1)
                            act.activation(probs[:, h % 2, first * P:(first + nb) * P], ps[:, 4 + (h * NPC + p) % 2, 0:nb * P],
                                           ACT.Exp).then_inc(e_done, 1)
                    take_outputs(NH // 2 - 1)

                @block.vector
                def _(dve):
                    link = chain(dve, vchain)
                    def maxima_to_rows(h):
                        dve.wait_ge(mT_psum, h + 1)
                        dve.tensor_copy(q6[96:99, h, :], ps[0:3, 3, :].bitcast(BF16)[:, 0:SEQ]).then_inc(mT_ready, 1)

                    for i in range(NH + 5):
                        for qc in range(NC):
                            if i < NH:
                                n = i * NC + qc
                                dve.wait_ge(s_psum, n + 1)
                                bank = 2 if qc in (1, 3) else 0
                                src = ps[:, bank:bank + 2, :].rearrange("p k n -> p (k n)")
                                dve.tensor_reduce(mx[:, i % 2, qc:qc + 1], src[:, 0:(qc + 1) * P], AX_X, ALU.max
                                                  ).then_inc(s_used, 1)
                            if qc == MAX_AT and 1 <= i <= NH:
                                maxima_to_rows(i - 1)
                            if i >= 5:
                                q, k = (i - 5) // 2, (i - 5) % 2 * NC + qc
                                if k == 0:
                                    dve.wait_ge(o_used, q + 1)
                                part = slice(k * P // 2, (k + 1) * P // 2)
                                op = dve.reciprocal(den[:, part], den[:, part])
                                if k == 2 * NC - 1:
                                    op.then_inc(inverted, 1)
                        if i < NH:
                            dve.wait_ge(s_used, NC * (i + 1))
                            if i >= 2:
                                dve.wait_ge(mT_psum, i - 1)
                            mp, m = msp[:, i % 2], mx[:, i % 2]
                            link(dve.tensor_copy(mp[:, :, 0], m))
                            link(dve.tensor_tensor(mres[:], m, mp[:, :, 0], ALU.subtract))
                            link(dve.tensor_copy(mp[:, :, 1], mres[:]))
                            link(dve.tensor_tensor(mres[:], mres[:], mp[:, :, 1], ALU.subtract))
                            dve.tensor_copy(mp[:, :, 2], mres[:]).then_inc(msp_ready, 1)
            s.round_end()


def attn_finish(nc, g):
    NE = 8
    with Scope(nc) as s:
        wo, gw = s.sb("af_wo", [P, DC, D]), s.sb("af_gw", [P, DC, NE])
        rows = s.sb("af_rows", [P, 3 * D])
        b2 = s.sb("af_b2", [NE, D])
        x1, nx = s.sb("af_x1", [P, NB, D]), s.sb("af_nx", [P, NB, D])
        aT, nT = s.sb("af_aT", [P, DC, NB * P]), s.sb("af_nT", [P, DC, NB * P])
        lg, sel, eq, cum = (s.sb("af_" + n, [P, NB, NE]) for n in ("lg", "sel", "eq", "cum"))
        gt = s.sb("af_gates", [P, NB, NE])
        v8, cnt = s.sb("af_v8", [P, NB, 8]), s.sb("af_cnt", [P, NB])
        gT = s.sb("af_gT", [NE, NB * P])
        ones = s.sb("af_ones", [P, 32])
        stats, mv, rs, ltmp = s.sb("af_stats", [P, NB, 6]), s.sb("af_mv", [P, NB, 2]), s.sb("af_rs", [P, NB]), s.sb("af_ltmp", [P, 2, NB])
        with Scope(nc) as u:
            loaded = u.sem("af_loaded")
            with nc.Block() as block:
                @block.sync
                def _(sp):
                    for dst, n in ((wo[:], "at_wo"), (gw[:], "m0_gate"), (rows[:], "af_rows"), (b2[:], "m0_b2")):
                        sp.dma_start(dst, g.d[n]).then_inc(loaded, 16)
                    sp.wait_ge(loaded, 16 * 4)

                @block.vector
                def _(dve):
                    dve.memset(ones[:], 1.0)
            u.round_end()
        (vchain, aT_ready, out_psum, zb_ready, x1_ready, h_added, nx_ready, nT_psum, nT_ready, lg_psum, lg_ready,
         e_ready, g_ready, gT_psum, gT_ready, bias_psum, nx_kept) = (s.sem("af_" + n) for n in (
             "vchain aT_ready out_psum zb_ready x1_ready h_added nx_ready nT_psum nT_ready lg_psum lg_ready "
             "e_ready g_ready gT_psum gT_ready bias_psum nx_kept").split())
        ps = g.ps
        with nc.Fori(0, NC) as c:
            def at_c(t):
                return t[:, bass.ds(c, 1)].rearrange("p o b n -> p (o b) n")
            hc, zc, gc = at_c(g.h), at_c(g.z), at_c(g.gates0)
            with nc.Block() as block:
                @block.tensor
                def _(pe):
                    pe.wait_ge(aT_ready, 1)
                    for b in range(NB):
                        for d in range(DC):
                            mm = pe.matmul(ps[:, 2 + b, 0:D], aT[:, d, b * P:(b + 1) * P], wo[:, d, :],
                                           start=(d == 0), stop=(d == DC - 1))
                        mm.then_inc(out_psum, 1)
                    pe.wait_ge(nx_ready, 1)
                    for d in range(DC):
                        for b in range(NB):
                            mm = pe.transpose(ps[:, d, b * P:(b + 1) * P], nx[:, b, d * P:(d + 1) * P], g.ident[:])
                    mm.then_inc(nT_psum, 1)
                    pe.wait_ge(nT_ready, 1)
                    for b in range(NB):
                        for d in range(DC):
                            mm = pe.matmul(ps[:, 6, b * NE:(b + 1) * NE], nT[:, d, b * P:(b + 1) * P], gw[:, d, :],
                                           start=(d == 0), stop=(d == DC - 1))
                    mm.then_inc(lg_psum, 1)
                    pe.wait_ge(g_ready, 1)
                    for b in range(NB):
                        mm = pe.transpose(ps[0:NE, 7, b * P:(b + 1) * P], gt[:, b, :], g.ident[:])
                    mm.then_inc(gT_psum, 1)
                    pe.wait_ge(gT_ready, 1)
                    for b in range(NB):
                        mm = pe.matmul(ps[:, 2 + b, 0:D], gT[:, b * P:(b + 1) * P], b2[:], start=True, stop=True)
                    mm.then_inc(bias_psum, 1)

                @block.scalar
                def _(act):
                    src = g.aT[:, :, :, bass.ds(c * P, P)]
                    act.activation(aT[:].rearrange("p d (b n) -> p d b n", b=NB), src, ACT.Copy).then_inc(aT_ready, 1)
                    act.wait_ge(nT_psum, 1)
                    act.activation(nT[:, 0, :], ps[:, 0, :], ACT.Copy)
                    act.activation(nT[:, 1, :], ps[:, 1, :], ACT.Copy).then_inc(nT_ready, 1)
                    act.wait_ge(lg_ready, 1)
                    act.activation(gt[:], lg[:], ACT.Exp).then_inc(e_ready, 1)
                    act.wait_ge(gT_psum, 1)
                    act.activation(gT[:], ps[0:NE, 7, :], ACT.Copy).then_inc(gT_ready, 1)

                @block.gpsimd
                def _(pool):
                    pool.tensor_tensor(x1[:], zc, bc(rows[:, 0:D].unsqueeze(1), [P, NB, D]), ALU.add).then_inc(zb_ready, 1)
                    pool.wait_ge(x1_ready, NB)
                    pool.tensor_tensor(hc, hc, x1[:], ALU.add).then_inc(h_added, 1)
                    pool.wait_ge(nx_ready, 1)
                    pool.tensor_copy(zc, nx[:]).then_inc(nx_kept, 1)

                @block.vector
                def _(dve):
                    link = chain(dve, vchain)
                    dve.wait_ge(zb_ready, 1)
                    for b in range(NB):
                        dve.wait_ge(out_psum, b + 1)
                        dve.tensor_tensor(x1[:, b], x1[:, b], ps[:, 2 + b, 0:D], ALU.add).then_inc(x1_ready, 1)
                    dve.wait_ge(x1_ready, NB)
                    layernorm(dve, link, [x1[:, b, :] for b in range(NB)], [nx[:, b, :] for b in range(NB)],
                              stats, mv, rs, ltmp)
                    link(dve.tensor_tensor(nx[:], nx[:], bc(rows[:, D:2 * D].unsqueeze(1), [P, NB, D]), ALU.mult))
                    dve.tensor_tensor(nx[:], nx[:], bc(rows[:, 2 * D:3 * D].unsqueeze(1), [P, NB, D]), ALU.add
                                      ).then_inc(nx_ready, 1)
                    dve.wait_ge(lg_psum, 1)
                    link(dve.tensor_copy(lg[:].rearrange("p b e -> p (b e)"), ps[:, 6, 0:NB * NE]))
                    pick_top(dve, link, lg[:], 2, v8[:], sel[:], eq[:], cum[:], cnt[:], ones[:])
                    dve.tensor_tensor(lg[:], lg[:], bc(v8[:, :, 0:1], [P, NB, NE]), ALU.subtract).then_inc(lg_ready, 1)
                    dve.wait_ge(e_ready, 1)
                    link(dve.tensor_tensor(lg[:], gt[:], sel[:], ALU.mult))
                    link(dve.tensor_reduce(cnt[:], lg[:], AX_X, ALU.add))
                    link(dve.reciprocal(cnt[:], cnt[:]))
                    dve.tensor_tensor(gt[:], lg[:], bc(cnt[:].unsqueeze(2), [P, NB, NE]), ALU.mult).then_inc(g_ready, 1)
                    dve.wait_ge(g_ready, 1)
                    dve.tensor_copy(gc, gt[:])
                    dve.tensor_copy(at_c(g.sel0), sel[:])
                    dve.wait_ge(bias_psum, 1)
                    dve.wait_ge(h_added, 1)
                    dve.tensor_tensor(hc, hc, ps[:, 2:6, 0:D], ALU.add)
            s.round_end()


def time_mix(nc, g):
    NE = 8
    with Scope(nc) as s:
        wk, wo, rw = s.sb("tm_wkvr", [P, 3, DC, D]), s.sb("tm_wo", [P, DC, D]), s.sb("tm_router", [P, DC, NE])
        rows, cols = s.sb("tm_rows", [P, 4 * D]), s.sb("tm_cols", [P, 5, DC])
        hn, xn = s.sb("tm_hn", [P, NC, D]), s.sb("tm_xn", [P, NC, D])
        xT, dT = s.sb("tm_xT", [P, DC, SEQ + 1]), s.sb("tm_dT", [P, DC, SEQ])
        mix = s.sb("tm_mix", [P, 3, DC, SEQ])
        kk, vv, rr = s.sb("tm_k", [P, DC, SEQ]), s.sb("tm_v", [P, DC, SEQ]), s.sb("tm_r", [P, DC, SEQ])
        pp, aa, bb = (s.sb("tm_" + n, [P, DC, SEQ + 1]) for n in ("pp", "aa", "bb"))
        t = s.sb("tm_t", [P, 4, DC, SEQ])
        lg, pr, sel, eq, cum = (s.sb("tm_" + n, [P, NC, NE]) for n in ("lg", "pr", "sel", "eq", "cum"))
        v8, cnt = s.sb("tm_v8", [P, NC, 8]), s.sb("tm_cnt", [P, NC])
        ones = s.sb("tm_ones", [P, 32])
        stats, mv, rs, ltmp = s.sb("tm_stats", [P, NC, 6]), s.sb("tm_mv", [P, NC, 2]), s.sb("tm_rs", [P, NC]), s.sb("tm_ltmp", [P, 2, NC])
        with Scope(nc) as u:
            loaded, decay, dchain = u.sem("tm_loaded"), u.sem("tm_decay"), u.sem("tm_dchain")
            with nc.Block() as block:
                @block.sync
                def _(sp):
                    for dst, n in ((wk[:], "tm_wkvr"), (wo[:], "tm_wo"), (rw[:], "m1_router"), (rows[:], "tm_rows"),
                                   (cols[:], "tm_cols")):
                        sp.dma_start(dst, g.d[n]).then_inc(loaded, 16)
                    sp.wait_ge(loaded, 16 * 5)

                @block.scalar
                def _(act):
                    act.wait_ge(loaded, 16 * 5)
                    act.activation(cols[:, 3], cols[:, 3], ACT.Exp).then_inc(decay, 1)

                @block.vector
                def _(dve):
                    dve.memset(ones[:], 1.0)
                    dve.memset(xT[:, :, 0:1], 0.0)
                    dve.memset(pp[:, :, 0:1], -1e30)
                    dve.memset(aa[:, :, 0:1], 0.0)
                    dve.memset(bb[:, :, 0:1], 0.0)
                    dve.wait_ge(decay, 1)
                    dve.tensor_scalar(cols[:, 3], cols[:, 3], -1.0, None, ALU.mult)
            u.round_end()
        (vchain, xn_ready, xT_psum, xT_ready, mix_ready, p_psum, p_used, exp_arg, exp_done, y_ready, out_psum, x2_ready,
         ei_ready, eT_psum, eT_ready, lg_psum, sm_arg, sm_done, pool_ready, e_stored) = (
             s.sem("tm_" + n) for n in (
                 "vchain xn_ready xT_psum xT_ready mix_ready p_psum p_used exp_arg exp_done y_ready out_psum x2_ready "
                 "ei_ready eT_psum eT_ready lg_psum sm_arg sm_done pool_ready e_stored").split())
        ps = g.ps
        two = [ps[:, 2 * i:2 * i + 2, :].rearrange("p k n -> p (k n)") for i in range(4)]
        proj = [(w, f) for w in range(3) for f in range(2)]
        pair = [2, 3, 0, 1, 2, 3]
        prev, cur = slice(0, SEQ), slice(1, SEQ + 1)
        with nc.Fori(0, NB) as b:
            hb = g.h[:, :, bass.ds(b, 1)].rearrange("p c o n -> p c (o n)")
            with nc.Block() as block:
                @block.tensor
                def _(pe):
                    pe.wait_ge(xn_ready, 1)
                    for d in range(DC):
                        for c in range(NC):
                            mm = pe.transpose(two[d][:, c * P:(c + 1) * P], xn[:, c, d * P:(d + 1) * P], g.ident[:])
                    mm.then_inc(xT_psum, 1)
                    for i, (w, f) in enumerate(proj):
                        if f == 0:
                            pe.wait_ge(mix_ready, w + 1)
                        if i == 2:
                            pe.wait_ge(xT_ready, 1)
                        if i >= 4:
                            pe.wait_ge(p_used, i - 3)
                        for lo, hi in ((0, 512), (512, SEQ)):
                            for d in range(DC):
                                mm = pe.matmul(two[pair[i]][:, lo:hi], wk[:, w, d, f * P:(f + 1) * P],
                                               mix[:, w, d, lo:hi], start=(d == 0), stop=(d == DC - 1))
                        mm.then_inc(p_psum, 1)
                    pe.wait_ge(y_ready, 1)
                    for c in range(NC):
                        for f in range(2):
                            mm = pe.matmul(ps[:, c // 2, (c % 2) * D:(c % 2 + 1) * D], rr[:, f, c * P:(c + 1) * P],
                                           wo[:, f, :], start=(f == 0), stop=(f == 1))
                        if c % 2:
                            mm.then_inc(out_psum, 1)
                    pe.wait_ge(ei_ready, 1)
                    for d in range(DC):
                        for c in range(NC):
                            mm = pe.transpose(two[2 + d][:, c * P:(c + 1) * P], xn[:, c, d * P:(d + 1) * P], g.ident[:])
                    mm.then_inc(eT_psum, 1)
                    pe.wait_ge(eT_ready, 1)
                    for c in range(NC):
                        for d in range(DC):
                            mm = pe.matmul(ps[:, 3, c * NE:(c + 1) * NE], xT[:, d, 1 + c * P:1 + (c + 1) * P], rw[:, d, :],
                                           start=(d == 0), stop=(d == DC - 1))
                    mm.then_inc(lg_psum, 1)

                @block.scalar
                def _(act):
                    act.wait_ge(xT_psum, 1)
                    act.activation(xT[:, 0, cur], two[0][:, 0:SEQ], ACT.Copy)
                    act.activation(xT[:, 1, cur], two[1][:, 0:SEQ], ACT.Copy).then_inc(xT_ready, 1)
                    for i, (w, f) in enumerate(proj):
                        act.wait_ge(p_psum, i + 1)
                        src, dst = two[pair[i]][:, 0:SEQ], (kk, vv, rr)[w][:, f, :]
                        if w < 2:
                            act.activation(dst, src, ACT.Copy).then_inc(p_used, 1)
                        else:
                            act.activation(dst, src, ACT.Sigmoid).then_inc(p_used, 1)
                    for i in range(2):
                        act.wait_ge(exp_arg, i + 1)
                        act.activation(t[:, 2 * i:2 * i + 2], t[:, 2 * i:2 * i + 2], ACT.Exp).then_inc(exp_done, 1)
                    act.wait_ge(eT_psum, 1)
                    act.activation(xT[:, 0, cur], two[2][:, 0:SEQ], ACT.Copy)
                    act.activation(xT[:, 1, cur], two[3][:, 0:SEQ], ACT.Copy).then_inc(eT_ready, 1)
                    act.wait_ge(sm_arg, 1)
                    act.activation(pr[:], lg[:], ACT.Exp).then_inc(sm_done, 1)

                @block.gpsimd
                def _(pool):
                    pool.wait_ge(x2_ready, 1)
                    pool.tensor_tensor(hb, hb, hn[:], ALU.add).then_inc(pool_ready, 1)

                @block.sync
                def _(sp):
                    sp.wait_ge(ei_ready, 1)
                    dst = g.scr_e[bass.ds(b, 1), 1:SEQ + 1].rearrange("o (c p) n -> p (o c) n", p=P)
                    sp.dma_start(dst, xn[:]).then_inc(e_stored, 16)
                    sp.wait_ge(e_stored, 16)

                @block.vector
                def _(dve):
                    link = chain(dve, vchain)
                    tiles = [hb[:, c, :] for c in range(NC)]
                    hns, xns = [hn[:, c, :] for c in range(NC)], [xn[:, c, :] for c in range(NC)]
                    row = [bc(rows[:, i * D:(i + 1) * D].unsqueeze(1), [P, NC, D]) for i in range(4)]
                    layernorm(dve, link, tiles, hns, stats, mv, rs, ltmp)
                    layernorm(dve, link, hns, xns, stats, mv, rs, ltmp)
                    link(dve.tensor_tensor(xn[:], xn[:], row[0], ALU.mult))
                    dve.tensor_tensor(xn[:], xn[:], row[1], ALU.add).then_inc(xn_ready, 1)
                    dve.wait_ge(xT_ready, 1)
                    link(dve.tensor_tensor(dT[:], xT[:, :, cur], xT[:, :, prev], ALU.subtract))
                    for w in range(3):
                        for d in range(DC):
                            op = dve.scalar_tensor_tensor(mix[:, w, d, :], dT[:, d, :], cols[:, w, d:d + 1], xT[:, d, prev],
                                                          ALU.mult, ALU.add)
                        op.then_inc(mix_ready, 1)
                    dve.wait_ge(p_used, 2)
                    for f in range(2):
                        op = dve.tensor_tensor_scan(pp[:, f, cur], bc(cols[:, 3, f:f + 1], [P, SEQ]), kk[:, f, :], -1e30,
                                                    ALU.add, ALU.max)
                    link(op)
                    for f in range(2):
                        dve.tensor_scalar(t[:, 0, f, :], pp[:, f, prev], cols[:, 3, f:f + 1], None, ALU.add)
                        op = dve.tensor_scalar(t[:, 3, f, :], kk[:, f, :], cols[:, 4, f:f + 1], None, ALU.add)
                    link(op)
                    dve.tensor_tensor(t[:, 0], t[:, 0], pp[:, :, cur], ALU.subtract)
                    dve.tensor_tensor(t[:, 1], kk[:], pp[:, :, cur], ALU.subtract).then_inc(exp_arg, 1)
                    link(dve.tensor_tensor(t[:, 2], t[:, 3], pp[:, :, prev], ALU.max))
                    link(dve.tensor_tensor(t[:, 3], t[:, 3], t[:, 2], ALU.subtract))
                    dve.tensor_tensor(t[:, 2], pp[:, :, prev], t[:, 2], ALU.subtract).then_inc(exp_arg, 1)
                    dve.wait_ge(exp_done, 1)
                    dve.wait_ge(p_used, 4)
                    link(dve.tensor_tensor(kk[:], t[:, 1], vv[:], ALU.mult))
                    for f in range(2):
                        dve.tensor_tensor_scan(aa[:, f, cur], t[:, 0, f, :], kk[:, f, :], 0.0, ALU.mult, ALU.add)
                        op = dve.tensor_tensor_scan(bb[:, f, cur], t[:, 0, f, :], t[:, 1, f, :], 0.0, ALU.mult, ALU.add)
                    link(op)
                    dve.wait_ge(exp_done, 2)
                    dve.wait_ge(p_used, 6)
                    dve.tensor_tensor(t[:, 0], t[:, 2], aa[:, :, prev], ALU.mult)
                    dve.tensor_tensor(vv[:], t[:, 3], vv[:], ALU.mult)
                    link(dve.tensor_tensor(t[:, 1], t[:, 2], bb[:, :, prev], ALU.mult))
                    dve.tensor_tensor(t[:, 0], t[:, 0], vv[:], ALU.add)
                    link(dve.tensor_tensor(t[:, 1], t[:, 1], t[:, 3], ALU.add))
                    dve.tensor_tensor(rr[:], rr[:], t[:, 0], ALU.mult)
                    link(dve.reciprocal(t[:, 1], t[:, 1]))
                    dve.tensor_tensor(rr[:], rr[:], t[:, 1], ALU.mult).then_inc(y_ready, 1)
                    for m in range(NC // 2):
                        dve.wait_ge(out_psum, m + 1)
                        op = dve.tensor_tensor(hn[:, 2 * m:2 * m + 2], hn[:, 2 * m:2 * m + 2],
                                               ps[:, m, :].rearrange("p (c n) -> p c n", c=2), ALU.add)
                    op.then_inc(x2_ready, 1)
                    dve.wait_ge(x2_ready, 1)
                    layernorm(dve, link, hns, xns, stats, mv, rs, ltmp)
                    link(dve.tensor_tensor(xn[:], xn[:], row[2], ALU.mult))
                    dve.tensor_tensor(xn[:], xn[:], row[3], ALU.add).then_inc(ei_ready, 1)
                    dve.wait_ge(lg_psum, 1)
                    link(dve.tensor_copy(lg[:].rearrange("p c e -> p (c e)"), ps[:, 3, 0:NC * NE]))
                    link(dve.tensor_reduce(cnt[:], lg[:], AX_X, ALU.max))
                    dve.tensor_tensor(lg[:], lg[:], bc(cnt[:].unsqueeze(2), [P, NC, NE]), ALU.subtract).then_inc(sm_arg, 1)
                    dve.wait_ge(sm_done, 1)

                    def normalise(dst, src):
                        link(dve.tensor_reduce(cnt[:], src, AX_X, ALU.add))
                        link(dve.reciprocal(cnt[:], cnt[:]))
                        link(dve.tensor_tensor(dst, src, bc(cnt[:].unsqueeze(2), [P, NC, NE]), ALU.mult))
                    normalise(pr[:], pr[:])
                    pick_top(dve, link, pr[:], 2, v8[:], sel[:], eq[:], cum[:], cnt[:], ones[:])
                    dve.tensor_copy(g.sel1[:, :, bass.ds(b, 1), :].rearrange("p c o e -> p c (o e)"), sel[:])
                    link(dve.tensor_tensor(lg[:], pr[:], sel[:], ALU.mult))
                    normalise(g.gates1[:, :, bass.ds(b, 1), :].rearrange("p c o e -> p c (o e)"), lg[:])
            s.round_end()


def route_groups(nc, g):
    NE, NGR = 32, 8
    with Scope(nc) as s:
        gw, bias = s.sb("rg_gw", [P, DC, NE]), s.sb("rg_bias", [P, NE])
        nx, nT = s.sb("rg_nx", [P, NB, D]), s.sb("rg_nT", [P, DC, NB * P])
        score, sc, sel, eq, cum, comb = (s.sb("rg_" + n, [P, NB, NE]) for n in ("score", "sc", "sel", "eq", "cum", "comb"))
        pairs = s.sb("rg_pairs", [P, NB, NGR, 6])
        gs, gsel, geq, gcum = (s.sb("rg_" + n, [P, NB, NGR]) for n in ("gs", "gsel", "geq", "gcum"))
        v8, cnt = s.sb("rg_v8", [P, NB, 8]), s.sb("rg_cnt", [P, NB])
        ones = s.sb("rg_ones", [P, 32])
        stats, mv, rs, ltmp = s.sb("rg_stats", [P, NB, 6]), s.sb("rg_mv", [P, NB, 2]), s.sb("rg_rs", [P, NB]), s.sb("rg_ltmp", [P, 2, NB])
        with Scope(nc) as u:
            loaded = u.sem("rg_loaded")
            with nc.Block() as block:
                @block.sync
                def _(sp):
                    sp.dma_start(gw[:], g.d["m2_gate"]).then_inc(loaded, 16)
                    sp.dma_start(bias[:], g.d["m2_bias"]).then_inc(loaded, 16)
                    sp.wait_ge(loaded, 32)

                @block.vector
                def _(dve):
                    dve.memset(ones[:], 1.0)
                    dve.memset(g.comb[:], 1.0)
            u.round_end()
        vchain, nx_ready, nT_psum, nT_ready, lg_psum, e_ready, xT_ready = (s.sem("rg_" + n) for n in (
            "vchain nx_ready nT_psum nT_ready lg_psum e_ready xT_ready").split())
        ps = g.ps
        with nc.Fori(0, NC) as c:
            hc = g.h[:, bass.ds(c, 1)].rearrange("p o b n -> p (o b) n")
            with nc.Block() as block:
                @block.tensor
                def _(pe):
                    pe.wait_ge(nx_ready, 1)
                    for d in range(DC):
                        for b in range(NB):
                            mm = pe.transpose(ps[:, d, b * P:(b + 1) * P], nx[:, b, d * P:(d + 1) * P], g.ident[:])
                    mm.then_inc(nT_psum, 1)
                    pe.wait_ge(nT_ready, 1)
                    for b in range(NB):
                        for d in range(DC):
                            mm = pe.matmul(ps[:, 2, b * NE:(b + 1) * NE], nT[:, d, b * P:(b + 1) * P], gw[:, d, :],
                                           start=(d == 0), stop=(d == DC - 1))
                    mm.then_inc(lg_psum, 1)

                @block.scalar
                def _(act):
                    act.wait_ge(nT_psum, 1)
                    act.activation(nT[:, 0, :], ps[:, 0, :], ACT.Copy)
                    act.activation(nT[:, 1, :], ps[:, 1, :], ACT.Copy).then_inc(nT_ready, 1)
                    act.wait_ge(lg_psum, 1)
                    act.activation(score[:].rearrange("p b e -> p (b e)"), ps[:, 2, 0:NB * NE], ACT.Exp, scale=-1.0
                                   ).then_inc(e_ready, 1)

                @block.gpsimd
                def _(pool):
                    pool.wait_ge(nT_ready, 1)
                    pool.tensor_copy(g.xT[:, :, bass.ds(c, 1), :].rearrange("p d o n -> p d (o n)"), nT[:]).then_inc(xT_ready, 1)

                @block.vector
                def _(dve):
                    link = chain(dve, vchain)
                    layernorm(dve, link, [hc[:, b, :] for b in range(NB)], [nx[:, b, :] for b in range(NB)],
                              stats, mv, rs, ltmp)
                    dve.engine_nop().then_inc(nx_ready, 1)
                    dve.wait_ge(e_ready, 1)
                    link(dve.tensor_scalar(score[:], score[:], 1.0, None, ALU.add))
                    link(dve.reciprocal(score[:], score[:]))
                    link(dve.tensor_tensor(sc[:], score[:], bc(bias[:].unsqueeze(1), [P, NB, NE]), ALU.add))
                    q = sc[:].rearrange("p b (g k) -> p b g k", g=NGR)
                    for b in range(NB):
                        dve.tensor_tensor(pairs[:, b, :, 0:3], q[:, b, :, 0:3], q[:, b, :, 1:4], ALU.add)
                        dve.tensor_tensor(pairs[:, b, :, 3:5], q[:, b, :, 0:2], q[:, b, :, 2:4], ALU.add)
                    link(dve.tensor_tensor(pairs[:, :, :, 5], q[:, :, :, 0], q[:, :, :, 3], ALU.add))
                    link(dve.tensor_reduce(gs[:], pairs[:], AX_X, ALU.max))
                    pick_top(dve, link, gs[:], 4, v8[:], gsel[:], geq[:], gcum[:], cnt[:], ones[:])
                    link(dve.tensor_tensor(q, q, bc(gsel[:].unsqueeze(3), [P, NB, NGR, 4]), ALU.mult))
                    pick_top(dve, link, sc[:], 8, v8[:], sel[:], eq[:], cum[:], cnt[:], ones[:])
                    link(dve.tensor_tensor(comb[:], sel[:], score[:], ALU.mult))
                    link(dve.tensor_reduce(cnt[:], comb[:], AX_X, ALU.add))
                    link(dve.tensor_scalar(cnt[:], cnt[:], 1e-20, None, ALU.add))
                    link(dve.reciprocal(cnt[:], cnt[:]))
                    link(dve.tensor_scalar(cnt[:], cnt[:], 2.5, None, ALU.mult))
                    dve.tensor_tensor(g.comb[:, bass.ds(c, 1), :, 0:NE].rearrange("p o b e -> p (o b) e"), comb[:],
                                      bc(cnt[:].unsqueeze(2), [P, NB, NE]), ALU.mult)
            s.round_end()


def moe_silu(nc, g, first, count, per):
    with Scope(nc) as s:
        tag = f"ms{first}_"
        w = s.sb(tag + "w", [P, per, 3 * 2 * P])
        act_g, hid = s.sb(tag + "silu", [P, 2, 512]), s.sb(tag + "hid", [P, 2, 512])
        cw = s.sb(tag + "comb", [P, per, NC, NB])

        def load(sp, slot, e, sem):
            sp.dma_start(w[:, slot], g.d["m2_w"][bass.ds(e, 1)].rearrange("o p n -> p (o n)")).then_inc(sem, 16)
        with Scope(nc) as u:
            loaded = u.sem(tag + "loaded")
            with nc.Block() as block:
                @block.sync
                def _(sp):
                    for i in range(per):
                        load(sp, i, first + i, loaded)
                    sp.wait_ge(loaded, 16 * per)
            u.round_end()
        loaded, cw_ready, gu_psum, s_ready, hid_ready, y_psum, y_used = (s.sem(tag + n) for n in (
            "next_loaded cw_ready gu_psum s_ready hid_ready y_psum y_used").split())
        ps = g.ps
        NR = per * NC
        with nc.Fori(0, count // per) as r:
            e = r * per + first
            with nc.Block() as block:
                @block.sync
                def _(sp):
                    if count > per:
                        for i in range(per):
                            sp.wait_ge(y_psum, NB * NC * (i + 1))
                            load(sp, i, e + per + i, loaded)
                        sp.wait_ge(loaded, 16 * per)

                @block.tensor
                def _(pe):
                    for n in range(NR + 1):
                        if n < NR:
                            slot, c = divmod(n, NC)
                            if n >= 2:
                                pe.wait_ge(hid_ready, n - 1)
                            for k in range(2):
                                for d in range(DC):
                                    at = (2 * k + d) * P
                                    mm = pe.matmul(ps[:, 2 * k + n % 2, :], w[:, slot, at:at + P], g.xT[:, d, c, :],
                                                   start=(d == 0), stop=(d == DC - 1))
                                mm.then_inc(gu_psum, 1)
                        if n >= 1:
                            slot, c = divmod(n - 1, NC)
                            pe.wait_ge(hid_ready, n)
                            for b in range(NB):
                                k = (n - 1) * NB + b
                                if k >= 4:
                                    pe.wait_ge(y_used, k - 3)
                                pe.matmul(ps[:, 4 + k % 4, 0:D], hid[:, (n - 1) % 2, b * P:(b + 1) * P],
                                          w[:, slot, 4 * P:4 * P + D], start=True, stop=True).then_inc(y_psum, 1)

                @block.scalar
                def _(act):
                    for n in range(NR):
                        act.wait_ge(gu_psum, 2 * n + 1)
                        if n >= 2:
                            act.wait_ge(hid_ready, n - 1)
                        act.activation(act_g[:, n % 2, :], ps[:, n % 2, :], ACT.Silu).then_inc(s_ready, 1)

                @block.vector
                def _(dve):
                    for k in range(per):
                        op = dve.tensor_copy(cw[:, k], g.comb[:, :, :, bass.ds(e + k, 1)].rearrange("p c b o -> p c (b o)"))
                    op.then_inc(cw_ready, 1)
                    dve.wait_ge(cw_ready, 1)
                    for n in range(NR + 1):
                        if n < NR:
                            dve.wait_ge(s_ready, n + 1)
                            dve.wait_ge(gu_psum, 2 * n + 2)
                            if n >= 2:
                                dve.wait_ge(y_psum, NB * (n - 1))
                            dve.tensor_tensor(hid[:, n % 2, :], act_g[:, n % 2, :], ps[:, 2 + n % 2, :], ALU.mult
                                              ).then_inc(hid_ready, 1)
                        if n >= 1:
                            slot, c = divmod(n - 1, NC)
                            if n - 1 >= NC:
                                dve.wait_ge(y_used, NB * (n - NC))
                            for b in range(NB):
                                k = (n - 1) * NB + b
                                dve.wait_ge(y_psum, k + 1)
                                dve.scalar_tensor_tensor(g.h[:, c, b, :], ps[:, 4 + k % 4, 0:D], cw[:, slot, c, b:b + 1],
                                                         g.h[:, c, b, :], ALU.mult, ALU.add).then_inc(y_used, 1)
            s.round_end()


def layer1_ffn(nc, g):
    with Scope(nc) as s:
        g.xT = s.sb("l1_xT", [P, DC, NC, NB * P])
        g.comb = s.sb("l1_comb", [P, NC, NB, 34])
        route_groups(nc, g)
        moe_silu(nc, g, 0, 32, 8)
        moe_silu(nc, g, 32, 2, 2)


NE = 8
TS = 256
NT = NC * NB * P * 2 // TS + NE
TPR, AHEAD = 8, 4


def top2_slots(nc, g, tag, sel, gates, rows, src, width):
    NTT = NC * NB
    with Scope(nc, tag) as s:
        tri = s.sb("ts_tri", [P, 2 * P])
        iota = s.sb("ts_iota", [P, NT // 2 + NT + AHEAD])
        ones = s.sb("ts_ones", [P, NTT])
        rank, m1, m2 = (s.sb("ts_" + n, [P, NTT, NE]) for n in ("rank", "m1", "m2"))
        cnt, incl = s.sb("ts_cnt", [P, NE, NTT]), s.sb("ts_incl", [P, NE, NTT])
        NJ = NTT * P // TS
        cmp_n, cmp_t = s.sb("ts_cmp_n", [P, NE, NJ]), s.sb("ts_cmp_t", [P, NT + AHEAD, NE])
        tiles, cumt, base = (s.sb("ts_" + n, [P, NE]) for n in ("tiles", "cumt", "base"))
        pf, te = s.sb("ts_posf", [P, 2, NTT]), s.sb("ts_tile_e", [P, NT + AHEAD])
        loaded, counted, vchain, placed, scattered = (s.sem("ts_" + n) for n in
                                                      "loaded counted vchain placed scattered".split())
        ps = g.ps
        sv, gv = (t.rearrange("p c b e -> p (c b) e") for t in (sel, gates))
        with nc.Block() as block:
            @block.sync
            def _(sp):
                sp.dma_start(tri[:], g.d["ts_tri"]).then_inc(loaded, 16)
                sp.dma_start(iota[:], g.d["ts_iota"]).then_inc(loaded, 16)
                n = 32
                for dst, from_dram in src:
                    sp.dma_start(dst, from_dram).then_inc(loaded, 16)
                    n += 16
                sp.wait_ge(loaded, n)

            @block.tensor
            def _(pe):
                pe.wait_ge(loaded, 16 * (2 + len(src)))
                for k in range(2):
                    mm = pe.matmul(ps[:, k, 0:NTT * NE], tri[:, k * P:(k + 1) * P], sv.rearrange("p t e -> p (t e)"),
                                   start=True, stop=True)
                mm.then_inc(counted, 1)

            @block.vector
            def _(dve):
                link = chain(dve, vchain)
                dve.memset(ones[:], 1.0)
                dve.wait_ge(counted, 1)
                dve.tensor_copy(rank[:].rearrange("p t e -> p (t e)"), ps[:, 0, 0:NTT * NE])
                link(dve.tensor_copy(cnt[:], ps[:, 1, 0:NTT * NE].rearrange("p (t e) -> p e t", e=NE)))
                for e in range(NE):
                    op = dve.tensor_tensor_scan(incl[:, e, :], ones[:], cnt[:, e, :], 0.0, ALU.mult, ALU.add)
                link(op)
                dve.tensor_tensor(cnt[:], incl[:], cnt[:], ALU.subtract)
                link(dve.tensor_tensor(cmp_n[:], bc(incl[:, :, NTT - 1:NTT], [P, NE, NJ]),
                                       bc(iota[:, 0:NJ].unsqueeze(1), [P, NE, NJ]), ALU.is_gt))
                link(dve.tensor_reduce(tiles[:], cmp_n[:], AX_X, ALU.add))
                link(dve.tensor_tensor_scan(cumt[:], ones[:, 0:NE], tiles[:], 0.0, ALU.mult, ALU.add))
                dve.tensor_tensor(cmp_t[:], bc(iota[:, NT // 2:].unsqueeze(2), [P, NT + AHEAD, NE]),
                                  bc(cumt[:].unsqueeze(1), [P, NT + AHEAD, NE]), ALU.is_ge)
                link(dve.tensor_tensor(base[:], cumt[:], tiles[:], ALU.subtract))
                dve.tensor_reduce(te[:], cmp_t[:], AX_X, ALU.add)
                link(dve.tensor_scalar(base[:], base[:], float(TS), None, ALU.mult))
                dve.tensor_scalar(te[:], te[:], float(NE - 1), None, ALU.min)
                link(dve.tensor_tensor(cnt[:], cnt[:], bc(base[:].unsqueeze(2), [P, NE, NTT]), ALU.add))
                dve.tensor_copy(g.tile_e[:], te[:])
                link(dve.tensor_tensor(rank[:], rank[:], cnt[:].rearrange("p e t -> p t e"), ALU.add))
                link(dve.tensor_tensor(rank[:], rank[:], sv, ALU.mult))
                dve.tensor_reduce(pf[:, 0], rank[:], AX_X, ALU.add)
                link(dve.tensor_reduce(pf[:, 1], rank[:], AX_X, ALU.max))
                link(dve.tensor_tensor(pf[:, 0], pf[:, 0], pf[:, 1], ALU.subtract))
                dve.tensor_copy(g.pos[:], pf[:]).then_inc(placed, 1)
                link(dve.tensor_tensor(m1[:], rank[:], bc(pf[:, 1].unsqueeze(2), [P, NTT, NE]), ALU.is_equal))
                dve.tensor_tensor(m2[:], sv, m1[:], ALU.subtract)
                link(dve.tensor_tensor(m1[:], m1[:], gv, ALU.mult))
                link(dve.tensor_tensor(m2[:], m2[:], gv, ALU.mult))
                dve.tensor_reduce(g.pw[:, 1], m1[:], AX_X, ALU.add)
                dve.tensor_reduce(g.pw[:, 0], m2[:], AX_X, ALU.add)

            @block.gpsimd
            def _(pool):
                pool.wait_ge(loaded, 16 * (2 + len(src)))
                pool.wait_ge(placed, 1)
                to = g.slots[0:NT * TS * width].rearrange("(r n) -> r n", n=width)
                for t in range(NTT):
                    for k in range(2):
                        pool.indirect_dma_start(to, bass.IndirectOffsetOnAxis(g.pos[:, k, t:t + 1], axis=0), rows(t), None
                                                ).then_inc(scattered, 16)
                pool.wait_ge(scattered, 16 * 2 * NTT)
        s.round_end(swdge=True)


def top2_combine(nc, g, tag):
    with Scope(nc, tag) as s:
        yg = s.sb("tc_y", [P, NC, NB, 2, D])
        gathered = [s.sem(f"tc_gathered{c}") for c in range(NC)]
        added = s.sem("tc_added")
        with nc.Block() as block:
            @block.gpsimd
            def _(pool):
                for c in range(NC):
                    for b in range(NB):
                        for k in range(2):
                            at = g.pos[:, k, c * NB + b:c * NB + b + 1]
                            pool.indirect_dma_start(yg[:, c, b, k], None, g.y_slots, bass.IndirectOffsetOnAxis(at, axis=0)
                                                    ).then_inc(gathered[c], 16)
                for c in range(NC):
                    pool.wait_ge(gathered[c], 16 * 2 * NB)

            @block.vector
            def _(dve):
                for c in range(NC):
                    dve.wait_ge(gathered[c], 16 * 2 * NB)
                    for k in range(2):
                        if k:
                            dve.wait_ge(added, NB * (2 * c + 1))
                        for b in range(NB):
                            t = c * NB + b
                            dve.scalar_tensor_tensor(g.h[:, c, b, :], yg[:, c, b, k], g.pw[:, k, t:t + 1], g.h[:, c, b, :],
                                                     ALU.mult, ALU.add).then_inc(added, 1)
        s.round_end(swdge=True)


class TileLoads:

    def __init__(self, nc, g, s, tag, width, weights, x_sb):
        self.nc, self.g, self.width, self.weights, self.x = nc, g, width, weights, x_sb
        self.w_loaded = [s.sem(f"{tag}w_loaded{i}") for i in range(AHEAD)]
        self.x_loaded = [s.sem(f"{tag}x_loaded{i}") for i in range(TPR)]
        self.ids = s.sb(tag + "ids", [1, TPR + AHEAD], I32)

    def weights_of(self, sp, i, sem):
        e = sp.value_load(self.ids[0:1, i:i + 1], min_val=0, max_val=NE - 1)
        for dst, name in self.weights(i % AHEAD):
            sp.dma_start(dst, self.g.d[name][bass.ds(e, 1)].rearrange("o p n -> p (o n)")).then_inc(sem, 16)

    def rows_of(self, eng, i, tile, sem):
        src = self.g.slots.rearrange("(t h p n) -> t p h n", h=2, p=P, n=self.width)
        eng.dma_start(self.x[:, i], src[bass.ds(tile, 1)].rearrange("o p h n -> p (o h) n")).then_inc(sem, 16)


def experts_gelu(nc, g):
    F = 1024
    FC = F // P
    with Scope(nc) as s:
        wA, wB = s.sb("eg_w1", [P, AHEAD, DC * F + FC]), s.sb("eg_w2", [P, AHEAD, FC * D])
        x = s.sb("eg_x", [P, TPR, 2, D])
        xT = s.sb("eg_xT", [P, 2, DC, TS])
        hT = s.sb("eg_hT", [P, 2, FC, TS])
        y = s.sb("eg_y", [P, 2, 2, D])
        ld = TileLoads(nc, g, s, "eg_", D, lambda i: ((wA[:, i], "m0_w1"), (wB[:, i], "m0_w2")), x)
        ids_ready, xT_psum, xT_ready, h_psum, h_ready, y_psum, y_ready = (
            s.sem("eg_" + n) for n in "ids_ready xT_psum xT_ready h_psum h_ready y_psum y_ready".split())
        y_stored = [s.sem(f"eg_y_stored{i}") for i in range(2)]
        ps = g.ps
        with nc.Block() as block:
            @block.vector
            def _(dve):
                dve.tensor_copy(ld.ids[:], g.tile_e[0:1, 0:TPR + AHEAD]).then_inc(ids_ready, 1)

            @block.sync
            def _(sp):
                for i in range(TPR):
                    ld.rows_of(sp, i, i, ld.x_loaded[i])
                sp.wait_ge(ids_ready, 1)
                for i in range(AHEAD):
                    ld.weights_of(sp, i, ld.w_loaded[i])
                for i in range(TPR):
                    sp.wait_ge(ld.x_loaded[i], 16)
                for i in range(AHEAD):
                    sp.wait_ge(ld.w_loaded[i], 32)
        s.round_end()
        with nc.Fori(0, NT // TPR) as r:
            tile0 = r * TPR
            with nc.Block() as block:
                @block.sync
                def _(sp):
                    sp.wait_ge(ids_ready, 1)
                    for i in range(TPR + 1):
                        if i < TPR:
                            sp.wait_ge(xT_psum, i + 1)
                            ld.rows_of(sp, i, tile0 + TPR + i, ld.x_loaded[i])
                        if i >= 1:
                            sp.wait_ge(y_psum, 2 * i)
                            ld.weights_of(sp, i - 1 + AHEAD, ld.w_loaded[(i - 1) % AHEAD])
                            sp.wait_ge(y_ready, 2 * i)
                            store_rows(sp, g, y[:, (i - 1) % 2], tile0 + i - 1, y_stored[(i - 1) % 2])
                    for i in range(AHEAD):
                        sp.wait_ge(ld.w_loaded[i], 32 * (TPR // AHEAD))
                    for i in range(TPR):
                        sp.wait_ge(ld.x_loaded[i], 16)
                    for i in range(2):
                        sp.wait_ge(y_stored[i], 16 * (TPR // 2))

                @block.tensor
                def _(pe):
                    def transposes(i):
                        if i >= 1:
                            pe.wait_ge(xT_ready, i)
                        for d in range(DC):
                            for h in range(2):
                                mm = pe.transpose(ps[:, 6, (d * 2 + h) * P:(d * 2 + h + 1) * P], x[:, i, h, d * P:(d + 1) * P],
                                                  g.ident[:])
                        mm.then_inc(xT_psum, 1)
                    transposes(0)
                    for i in range(TPR + 1):
                        if i < TPR:
                            if i >= AHEAD:
                                pe.wait_ge(ld.w_loaded[i % AHEAD], 32 * (i // AHEAD))
                            pe.wait_ge(xT_ready, i + 1)
                            for f in range(FC):
                                k = i * FC + f
                                if k >= 4:
                                    pe.wait_ge(h_ready, k - 3)
                                for d in range(DC):
                                    mm = pe.matmul(ps[:, k % 4, 0:TS], wA[:, i % AHEAD, d * F + f * P:d * F + (f + 1) * P],
                                                   xT[:, i % 2, d, :], start=(d == 0), stop=(d == DC - 1))
                                mm.then_inc(h_psum, 1)
                        if i + 1 < TPR:
                            transposes(i + 1)
                        if i >= 1:
                            pe.wait_ge(h_ready, FC * i)
                            for h in range(2):
                                k = (i - 1) * 2 + h
                                if k >= 2:
                                    pe.wait_ge(y_ready, k - 1)
                                for f in range(FC):
                                    mm = pe.matmul(ps[:, 4 + h, 0:D], hT[:, (i - 1) % 2, f, h * P:(h + 1) * P],
                                                   wB[:, (i - 1) % AHEAD, f * D:(f + 1) * D], start=(f == 0), stop=(f == FC - 1))
                                mm.then_inc(y_psum, 1)

                @block.scalar
                def _(act):
                    for i in range(TPR):
                        if i >= 2:
                            act.wait_ge(y_psum, 2 * (i - 1))
                        for f in range(FC):
                            act.wait_ge(h_psum, i * FC + f + 1)
                            act.activation(hT[:, i % 2, f, :], ps[:, (i * FC + f) % 4, 0:TS], ACT.Gelu,
                                           bias=wA[:, i % AHEAD, DC * F + f:DC * F + f + 1]).then_inc(h_ready, 1)

                @block.vector
                def _(dve):
                    dve.tensor_copy(ld.ids[:], g.tile_e[0:1, bass.ds(tile0, TPR + AHEAD)]).then_inc(ids_ready, 1)
                    for i in range(TPR + 1):
                        if i < TPR:
                            dve.wait_ge(xT_psum, i + 1)
                            if i >= 2:
                                dve.wait_ge(h_psum, FC * (i - 1))
                            dve.tensor_copy(xT[:, i % 2].rearrange("p d n -> p (d n)"), ps[:, 6, :]).then_inc(xT_ready, 1)
                        if i >= 1:
                            if i >= 3:
                                dve.wait_ge(y_stored[(i - 1) % 2], 16 * ((i - 1) // 2))
                            for h in range(2):
                                dve.wait_ge(y_psum, 2 * (i - 1) + h + 1)
                                dve.tensor_copy(y[:, (i - 1) % 2, h], ps[:, 4 + h, 0:D]).then_inc(y_ready, 1)

            s.round_end()


def store_rows(eng, g, y, tile, sem):
    dst = g.y_slots.rearrange("(t h p) n -> t p h n", h=2, p=P)
    eng.dma_start(dst[bass.ds(tile, 1)].rearrange("o p h n -> p (o h) n"), y).then_inc(sem, 16)


def experts_channel_mix(nc, g):
    F = 512
    FC = F // P
    with Scope(nc) as s:
        w = s.sb("ec_w", [P, AHEAD, DC * F + FC * D + DC * D + 2 * DC])
        x = s.sb("ec_x", [P, TPR, 2, 2 * D])
        eT, dT = s.sb("ec_eT", [P, DC, TS]), s.sb("ec_dT", [P, DC, TS])
        xk, xr = s.sb("ec_xk", [P, 2, DC, TS]), s.sb("ec_xr", [P, 2, DC, TS])
        rl, kk = s.sb("ec_relu", [P, 2, FC, TS]), s.sb("ec_k", [P, 2, FC, TS])
        sg, y = s.sb("ec_sigmoid", [P, 2, 2, D]), s.sb("ec_y", [P, 2, 2, D])
        at_k, at_v, at_r, at_mu = 0, DC * F, DC * F + FC * D, DC * F + FC * D + DC * D
        ld = TileLoads(nc, g, s, "ec_", 2 * D, lambda i: ((w[:, i], "m1_w"),), x)
        (ids_ready, xT_psum, eT_ready, dT_ready, x_ready, k_psum, relu_ready, kk_ready, r_psum, r_ready, kv_psum, y_ready) = (
            s.sem("ec_" + n) for n in ("ids_ready xT_psum eT_ready dT_ready x_ready k_psum relu_ready kk_ready r_psum r_ready "
                                       "kv_psum y_ready").split())
        y_stored = [s.sem(f"ec_y_stored{i}") for i in range(2)]
        ps = g.ps
        with nc.Block() as block:
            @block.vector
            def _(dve):
                dve.tensor_copy(ld.ids[:], g.tile_e[0:1, 0:TPR + AHEAD]).then_inc(ids_ready, 1)

            @block.sync
            def _(sp):
                for i in range(TPR):
                    ld.rows_of(sp, i, i, ld.x_loaded[i])
                sp.wait_ge(ids_ready, 1)
                for i in range(AHEAD):
                    ld.weights_of(sp, i, ld.w_loaded[i])
                for i in range(TPR):
                    sp.wait_ge(ld.x_loaded[i], 16)
                for i in range(AHEAD):
                    sp.wait_ge(ld.w_loaded[i], 16)
        s.round_end()
        with nc.Fori(0, NT // TPR) as r:
            tile0 = r * TPR
            with nc.Block() as block:
                @block.sync
                def _(sp):
                    sp.wait_ge(ids_ready, 1)
                    for i in range(TPR + 1):
                        if i < TPR:
                            sp.wait_ge(xT_psum, i + 1)
                            ld.rows_of(sp, i, tile0 + TPR + i, ld.x_loaded[i])
                        if i >= 1:
                            sp.wait_ge(kv_psum, 2 * i)
                            ld.weights_of(sp, i - 1 + AHEAD, ld.w_loaded[(i - 1) % AHEAD])
                            sp.wait_ge(y_ready, 2 * i)
                            store_rows(sp, g, y[:, (i - 1) % 2], tile0 + i - 1, y_stored[(i - 1) % 2])
                    for i in range(AHEAD):
                        sp.wait_ge(ld.w_loaded[i], 16 * (TPR // AHEAD))
                    for i in range(TPR):
                        sp.wait_ge(ld.x_loaded[i], 16)
                    for i in range(2):
                        sp.wait_ge(y_stored[i], 16 * (TPR // 2))

                @block.tensor
                def _(pe):
                    def transposes(i):
                        if i >= 1:
                            pe.wait_ge(eT_ready, i)
                            pe.wait_ge(dT_ready, i)
                        for j in range(2):
                            for d in range(DC):
                                for h in range(2):
                                    mm = pe.transpose(ps[:, 6 + j, (d * 2 + h) * P:(d * 2 + h + 1) * P],
                                                      x[:, i, h, (j * DC + d) * P:(j * DC + d + 1) * P], g.ident[:])
                        mm.then_inc(xT_psum, 1)
                    transposes(0)
                    for i in range(TPR + 1):
                        if i < TPR:
                            if i >= AHEAD:
                                pe.wait_ge(ld.w_loaded[i % AHEAD], 16 * (i // AHEAD))
                            pe.wait_ge(x_ready, i + 1)
                            for f in range(FC):
                                k = i * FC + f
                                if k >= 2:
                                    pe.wait_ge(relu_ready, k - 1)
                                for d in range(DC):
                                    at = at_k + d * F + f * P
                                    mm = pe.matmul(ps[:, k % 2, 0:TS], w[:, i % AHEAD, at:at + P], xk[:, i % 2, d, :],
                                                   start=(d == 0), stop=(d == DC - 1))
                                mm.then_inc(k_psum, 1)
                            for h in range(2):
                                k = i * 2 + h
                                if k >= 2:
                                    pe.wait_ge(r_ready, k - 1)
                                for d in range(DC):
                                    mm = pe.matmul(ps[:, 2 + h, 0:D], xr[:, i % 2, d, h * P:(h + 1) * P],
                                                   w[:, i % AHEAD, at_r + d * D:at_r + (d + 1) * D],
                                                   start=(d == 0), stop=(d == DC - 1))
                                mm.then_inc(r_psum, 1)
                        if i + 1 < TPR:
                            transposes(i + 1)
                        if i >= 1:
                            pe.wait_ge(kk_ready, i)
                            for h in range(2):
                                k = (i - 1) * 2 + h
                                if k >= 2:
                                    pe.wait_ge(y_ready, k - 1)
                                for f in range(FC):
                                    mm = pe.matmul(ps[:, 4 + h, 0:D], kk[:, (i - 1) % 2, f, h * P:(h + 1) * P],
                                                   w[:, (i - 1) % AHEAD, at_v + f * D:at_v + (f + 1) * D],
                                                   start=(f == 0), stop=(f == FC - 1))
                                mm.then_inc(kv_psum, 1)

                @block.scalar
                def _(act):
                    def copy_before(i):
                        act.wait_ge(xT_psum, i + 1)
                        if i >= 1:
                            act.wait_ge(x_ready, i)
                        act.activation(eT[:].rearrange("p d n -> p (d n)"), ps[:, 6, :], ACT.Copy).then_inc(eT_ready, 1)
                    copy_before(0)
                    for i in range(TPR):
                        if i >= 2:
                            act.wait_ge(kk_ready, i - 1)
                        for f in range(FC):
                            k = i * FC + f
                            act.wait_ge(k_psum, k + 1)
                            act.activation(rl[:, i % 2, f, :], ps[:, k % 2, 0:TS], ACT.Relu).then_inc(relu_ready, 1)
                        if i >= 2:
                            act.wait_ge(y_ready, 2 * (i - 1))
                        for h in range(2):
                            act.wait_ge(r_psum, 2 * i + h + 1)
                            act.activation(sg[:, i % 2, h, :], ps[:, 2 + h, 0:D], ACT.Sigmoid).then_inc(r_ready, 1)
                        if i + 1 < TPR:
                            copy_before(i + 1)

                @block.vector
                def _(dve):
                    dve.tensor_copy(ld.ids[:], g.tile_e[0:1, bass.ds(tile0, TPR + AHEAD)]).then_inc(ids_ready, 1)
                    for i in range(TPR + 1):
                        if i < TPR:
                            dve.wait_ge(eT_ready, i + 1)
                            if i >= 1:
                                dve.wait_ge(x_ready, i)
                            dve.tensor_tensor(dT[:].rearrange("p d n -> p (d n)"), ps[:, 7, :],
                                              eT[:].rearrange("p d n -> p (d n)"), ALU.subtract).then_inc(dT_ready, 1)
                            dve.wait_ge(dT_ready, i + 1)
                            if i >= 2:
                                dve.wait_ge(r_psum, 2 * (i - 1))
                            if i >= AHEAD:
                                dve.wait_ge(ld.w_loaded[i % AHEAD], 16 * (i // AHEAD))
                            for m, dst in ((0, xk), (1, xr)):
                                for d in range(DC):
                                    mu = at_mu + m * DC + d
                                    op = dve.scalar_tensor_tensor(dst[:, i % 2, d, :], dT[:, d, :], w[:, i % AHEAD, mu:mu + 1],
                                                                  eT[:, d, :], ALU.mult, ALU.add)
                            op.then_inc(x_ready, 1)
                        if i >= 1:
                            if i >= 3:
                                dve.wait_ge(y_stored[(i - 1) % 2], 16 * ((i - 1) // 2))
                            dve.wait_ge(r_ready, 2 * i)
                            for h in range(2):
                                dve.wait_ge(kv_psum, 2 * (i - 1) + h + 1)
                                dve.tensor_tensor(y[:, (i - 1) % 2, h], sg[:, (i - 1) % 2, h], ps[:, 4 + h, 0:D], ALU.mult
                                                  ).then_inc(y_ready, 1)

                @block.gpsimd
                def _(pool):
                    for i in range(TPR):
                        pool.wait_ge(relu_ready, FC * (i + 1))
                        if i >= 2:
                            pool.wait_ge(kv_psum, 2 * (i - 1))
                        pool.tensor_tensor(kk[:, i % 2], rl[:, i % 2], rl[:, i % 2], ALU.mult).then_inc(kk_ready, 1)
            s.round_end()


def layer0_ffn(nc, g):
    with Scope(nc) as s:
        g.gates0, g.sel0 = s.sb("gates0", [P, NC, NB, NE]), s.sb("sel0", [P, NC, NB, NE])
        slot_tables(g, s, "l0_")
        with Scope(nc) as n:
            g.z = n.sb("l0_z", [P, NC, NB, D])
            with Scope(nc) as t:
                g.aT = t.sb("l0_aT", [P, DC, NB, SEQ])
                with Scope(nc) as v:
                    g.v = v.sb("l0_v", [P, NC, NB, 16, 16])
                    attn_project(nc, g)
                    attn_heads(nc, g)
                attn_finish(nc, g)
            top2_slots(nc, g, "l0_", g.sel0[:], g.gates0[:], lambda t: g.z[:, t // NB, t % NB, :], (), D)
        experts_gelu(nc, g)
        top2_combine(nc, g, "l0_")


def slot_tables(g, s, tag):
    g.pos, g.pw = s.sb(tag + "pos", [P, 2, NC * NB], I32), s.sb(tag + "pos_gates", [P, 2, NC * NB])
    g.tile_e = s.sb(tag + "tile_experts", [P, NT + AHEAD], I32)


def layer1_attn(nc, g):
    with Scope(nc) as s:
        g.gates1, g.sel1 = s.sb("gates1", [P, NC, NB, NE]), s.sb("sel1", [P, NC, NB, NE])
        slot_tables(g, s, "l1_")
        time_mix(nc, g)
        with Scope(nc) as n:
            e = n.sb("l1_e", [P, NC, NB, 2 * D])
            src = []
            for b in range(NB):
                for j in range(2):
                    src.append((e[:, :, b, j * D:(j + 1) * D], g.scr_e[b, j:j + SEQ].rearrange("(c p) n -> p c n", p=P)))
            top2_slots(nc, g, "l1_", g.sel1[:], g.gates1[:], lambda t: e[:, t // NB, t % NB, :], src, 2 * D)
        experts_channel_mix(nc, g)
        top2_combine(nc, g, "l1_")


class Shared:
    pass


def program(nc, d, out):
    g = Shared()
    g.d = d
    with ExitStack() as ctx:
        g.ps = ctx.enter_context(nc.psum_tensor("banks", [P, 8, 512], F32))
        g.h = ctx.enter_context(nc.sbuf_tensor("h_res", [P, NC, NB, D], F32))
        g.ident = ctx.enter_context(nc.sbuf_tensor("ident", [P, P], F32))
        g.scr_ssm = nc.dram_tensor("scr_ssm", (NB, 256, 256), F32, kind="Internal").ap()
        g.scr_qk = nc.dram_tensor("scr_qk", (2, 3, D, NB, SEQ), BF16, kind="Internal").ap()
        g.scr_e = nc.dram_tensor("scr_e", (NB, SEQ + 1, D), F32, kind="Internal").ap()
        pad = TPR * TS * 2 * D
        g.slots = nc.dram_tensor("scr_slots", (NT * TS * 2 * D + pad,), F32, kind="Internal").ap()
        g.y_slots = nc.dram_tensor("scr_y_slots", (NT * TS, D), F32, kind="Internal").ap()
        with Scope(nc) as s:
            loaded = s.sem("const_loaded")
            with nc.Block() as block:
                @block.sync
                def _(sp):
                    sp.dma_start(g.ident[:], d["ident"]).then_inc(loaded, 16)
                    sp.wait_ge(loaded, 16)
            s.round_end()
        for stage in STAGES:
            stage(nc, g)
        with Scope(nc) as s:
            stored = s.sem("out_stored")
            with nc.Block() as block:
                @block.sync
                def _(sp):
                    for b in range(NB):
                        sp.dma_start(out[b].rearrange("(c p) n -> p c n", p=P), g.h[:, :, b, :]).then_inc(stored, 16)
                    sp.wait_ge(stored, 16 * NB)
            s.round_end()


def lay_out(**a):
    a = {k: np.ascontiguousarray(v) for k, v in a.items()}
    o = {}

    def dup(x):
        return np.concatenate([x.T, x.T], 0)

    def rep(x):
        return np.broadcast_to(np.asarray(x).reshape(1, -1), (P, np.asarray(x).size))

    def kxn(w):
        return w.reshape(-1, P, w.shape[-1]).transpose(1, 0, 2)

    o["txt"] = a["txt"]
    o["s4_ldt"] = rep(a["L0_tok_log_dt"])
    o["s4_are"], o["s4_aim"] = dup(a["L0_tok_inv_A_real"]), dup(a["L0_tok_A_imag"])
    o["s4_bre"], o["s4_bim"] = dup(a["L0_tok_B_ri"][..., 0]), dup(a["L0_tok_B_ri"][..., 1])
    for k, n in enumerate(("s4_cre", "s4_cim")):
        x = a["x"][..., k].transpose(2, 0, 1)
        o[n] = np.concatenate([x, x], 0)
    o["ident"] = np.eye(P, dtype=np.float32)
    o["identb"] = np.eye(P, dtype=np.float32).astype(mybir.dt.np(BF16))
    order = [(f * 4 + r) * 2 + j for f in range(2) for j in range(2) for r in range(4)]
    o["dn_wqk"] = np.stack([kxn(a["L0_attn_Wq"].T), kxn(a["L0_attn_Wk"].T)], 1)
    o["dn_wv"] = kxn(np.concatenate([a["L0_attn_Wv"], a["L0_attn_Wbeta"][order], a["L0_attn_Wmix"][order],
                                     a["L0_attn_Wgate"]], 0).T)
    o["dn_wout"] = kxn(a["L0_attn_Wout"].T)
    floor = np.array([np.exp(np.float32(-0.5 ** (k // 2 + 1))) for k in order], np.float32)
    o["dn_rows"] = rep(np.concatenate([a["L0_attn_bout"], a["L0_attn_ln_g"], a["L0_attn_ln_b"], a["L0_attn_bbeta"][order],
                                       a["L0_attn_bmix"][order], a["L0_attn_bgate"], floor]))
    i = np.arange(P)
    tri = (i[:, None] <= i[None, :]).astype(np.float32)
    cm = np.where(i[:, None] <= i[None, :], 0.0, -30000.0).astype(np.float32)
    bd = (i[:, None] // 32 == (np.arange(8 * 33) // 33 % 4)[None, :]).astype(np.float32)
    o["dn_masks"] = np.concatenate([tri, np.ones((P, P), np.float32), cm, bd], 1)
    sel = np.zeros((48, 16, P), np.float32)
    for k in range(48):
        sel[k, k % 16] = 1.0
    o["dn_sel"] = sel.astype(mybir.dt.np(BF16))
    extra_layouts(a, o, rep, kxn)
    return {k: np.ascontiguousarray(v) for k, v in o.items()}


def extra_layouts(a, o, rep, kxn):
    w, bias = a["L0_ffn_Wqkv"], a["L0_ffn_bqkv"]
    o["at_wqk"] = np.stack([kxn(w[:, 0:D]), kxn(w[:, D:2 * D])], 1)
    o["at_wv"] = kxn(w[:, 2 * D:])
    o["at_rows"] = rep(np.concatenate([a["L0_ffn_ln1_w"], a["L0_ffn_ln1_b"], bias[2 * D:]]))
    o["at_qkb"] = bias[0:2 * D].reshape(4, P).T
    i = np.arange(P)
    big = np.float32(-1e30)
    qm = np.where(i[None, :] <= i[:, None], np.float32(0), big)
    o["at_consts"] = np.concatenate([np.eye(P, dtype=np.float32), qm, qm.T],
                                    1).astype(mybir.dt.np(BF16))
    o["at_wo"] = kxn(a["L0_ffn_Wo"])
    o["m0_gate"] = kxn(a["L0_ffn_gate_W"])
    o["af_rows"] = rep(np.concatenate([a["L0_ffn_bo"], a["L0_ffn_ln2_w"], a["L0_ffn_ln2_b"]]))
    o["m0_b2"] = a["L0_ffn_fc2_b"]

    def by_expert(x):
        return x.reshape(NE, -1, P, x.shape[-1]).transpose(0, 2, 1, 3).reshape(NE, P, -1)
    b1 = a["L0_ffn_fc1_b"].reshape(NE, 8, P).transpose(0, 2, 1)
    o["m0_w1"] = np.concatenate([by_expert(a["L0_ffn_fc1_w"].transpose(0, 2, 1)), b1], 2)
    o["m0_w2"] = by_expert(a["L0_ffn_fc2_w"].transpose(0, 2, 1))
    o["ts_tri"] = np.concatenate([(i[:, None] < i[None, :]).astype(np.float32), np.ones((P, P), np.float32)], 1)
    o["ts_iota"] = rep(np.concatenate([TS * np.arange(NT // 2), np.arange(NT + AHEAD)]).astype(np.float32))

    o["tm_wkvr"] = np.stack([kxn(a["L1_attn_" + n]) for n in ("Wk", "Wv", "Wr")], 1)
    o["tm_wo"] = kxn(a["L1_attn_Wo"])
    o["m1_router"] = kxn(a["L1_attn_router_w"])
    o["tm_rows"] = rep(np.concatenate([a["L1_attn_" + n] for n in ("ln1_g", "ln1_b", "ln2_g", "ln2_b")]))
    o["tm_cols"] = np.stack([a["L1_attn_" + n].reshape(DC, P).T for n in (
        "tm_mu_k", "tm_mu_v", "tm_mu_r", "time_decay", "time_first")], 1)
    mu = np.stack([a["L1_attn_cm_mu_k"], a["L1_attn_cm_mu_r"]], 1)
    o["m1_w"] = np.concatenate([by_expert(a["L1_attn_eWk"]), by_expert(a["L1_attn_eWv"]), by_expert(a["L1_attn_eWr"]),
                                mu.reshape(NE, 2 * DC, P).transpose(0, 2, 1)], 2)
    o["m2_gate"] = kxn(a["L1_ffn_gate_w"].T)
    o["m2_bias"] = rep(a["L1_ffn_gate_bias"])
    gate = np.concatenate([a["L1_ffn_w_gate"], a["L1_ffn_sh_gate"].reshape(2, P, D)], 0)
    up = np.concatenate([a["L1_ffn_w_up"], a["L1_ffn_sh_up"].reshape(2, P, D)], 0)
    down = np.concatenate([a["L1_ffn_w_down"], a["L1_ffn_sh_down"].reshape(D, 2, P).transpose(1, 0, 2)], 0)

    def by_rows(x):
        return x.transpose(0, 2, 1).reshape(34, DC, P, P).transpose(0, 2, 1, 3).reshape(34, P, 2 * P)
    m2 = np.concatenate([by_rows(gate), by_rows(up), down.transpose(0, 2, 1)], 2)
    o["m2_w"] = np.concatenate([m2, m2[:6]], 0)


STAGES = [ssm_tokens, deltanet, layer0_ffn, layer1_attn, layer1_ffn]


def kernel(**inputs):
    import concourse.bacc as _bacc
    from concourse.bass_utils import run_bass_kernel_spmd as _run

    nc = _bacc.Bacc("TRN2", target_bir_lowering=False, num_devices=1)
    arrays = {"in_" + n: a for n, a in lay_out(**{k: np.asarray(v) for k, v in inputs.items()}).items()}
    d = {n[3:]: nc.dram_tensor(n, a.shape, mybir.dt.from_np(a.dtype), kind="ExternalInput").ap()
         for n, a in arrays.items()}
    out = nc.dram_tensor("out_h", (NB, SEQ, D), F32, kind="ExternalOutput").ap()
    program(nc, d, out)
    r = _run(nc, [arrays], core_ids=[0])
    return r.results[0]["out_h"]
```

```python
from contextlib import ExitStack
import numpy as np
import concourse.bass as bass
from concourse import mybir

ALU = mybir.AluOpType
ACT = mybir.ActivationFunctionType
F32 = mybir.dt.float32
BF16 = mybir.dt.bfloat16
I32 = mybir.dt.int32
F32R = mybir.dt.float32r
AX_X = mybir.AxisListType.X

P = 128
NB = 4
SEQ = 768
NC = SEQ // P
D = 256
DC = D // P
LN_EPS = 1e-5


def bc(ap, shape):
    return ap.broadcast_to(shape)


class Scope:

    def __init__(self, nc, tag=""):
        self.nc, self.tag, self.ctx, self.sems = nc, tag, ExitStack(), []

    def __enter__(self):
        return self

    def __exit__(self, *a):
        return self.ctx.__exit__(*a)

    def sb(self, name, shape, dt=F32):
        return self.ctx.enter_context(self.nc.sbuf_tensor(self.tag + name, shape, dt))

    def sem(self, name):
        s = self.ctx.enter_context(self.nc.semaphore(self.tag + name))
        self.sems.append(s)
        return s

    def kept_sem(self, name):
        return self.ctx.enter_context(self.nc.semaphore(self.tag + name))

    def round_end(self, swdge=False):
        if swdge:
            self.nc.gpsimd.dma_reset()
        numbers = sorted(s.num for s in self.sems)
        while numbers:
            n = 1
            while n < len(numbers) and numbers[n] == numbers[0] + n:
                n += 1
            self.nc.gpsimd.sem_clear(range(numbers[0], numbers[0] + n))
            numbers = numbers[n:]
        self.nc.all_engine_barrier()


def chain(eng, sem):
    n = [0]

    def link(ins):
        n[0] += 1
        ins.then_inc(sem, 1)
        eng.wait_ge(sem, n[0])
    return link


def rsqrt(dve, link, x, y, t):
    link(dve.tensor_scalar(y.bitcast(I32), x.bitcast(I32), -0.5, float(0x5F3759DF), ALU.mult, ALU.add))
    for _ in range(3):
        link(dve.tensor_tensor(t, y, y, ALU.mult))
        link(dve.scalar_tensor_tensor(t, t, -0.5, x, ALU.mult, ALU.mult))
        link(dve.scalar_tensor_tensor(y, t, 1.5, y, ALU.add, ALU.mult))


def cut(dve, out, x):
    return dve.tensor_scalar(out.bitcast(I32), x.bitcast(I32), -4096, None, ALU.bitwise_and)


def layernorm(dve, link, tiles, outs, stats, mv, rs, tmp):
    n = len(tiles)
    for i, x in enumerate(tiles):
        ins = dve.bn_stats(stats[:, i, :], x)
    link(ins)
    for i in range(n):
        ins = dve.bn_aggr(mv[:, i, :], stats[:, i, :])
    link(ins)
    link(dve.tensor_scalar(tmp[:, 0, 0:n], mv[:, 0:n, 1], LN_EPS, None, ALU.add))
    rsqrt(dve, link, tmp[:, 0, 0:n], rs[:, 0:n], tmp[:, 1, 0:n])
    for i, x in enumerate(tiles):
        ins = dve.tensor_scalar(outs[i], x, mv[:, i, 0:1], rs[:, i:i + 1], ALU.subtract, ALU.mult)
    link(ins)


def accurate_exp(dve, link, x, out, n, t):
    link(dve.tensor_scalar(t, x, -87.0, 88.0, ALU.max, ALU.min))
    link(dve.tensor_scalar(out.bitcast(I32), t, 1.4426950408889634, None, ALU.mult))
    link(dve.tensor_copy(n, out.bitcast(I32)))
    link(dve.scalar_tensor_tensor(t, n, -0.693359375, t, ALU.mult, ALU.add))
    link(dve.scalar_tensor_tensor(t, n, 2.12194440e-4, t, ALU.mult, ALU.add))
    coefficients = [1.0]
    for k in range(2, 11):
        coefficients.append(coefficients[-1] / k)
    link(dve.tensor_scalar(out, t, coefficients[-1], None, ALU.mult))
    for c in reversed(coefficients[:-1]):
        link(dve.scalar_tensor_tensor(out, out, c, t, ALU.add, ALU.mult))
    link(dve.tensor_scalar(t.bitcast(I32), n, 127.0, float(1 << 23), ALU.add, ALU.mult))
    link(dve.scalar_tensor_tensor(out, out, 1.0, t, ALU.add, ALU.mult))


def ssm_tokens(nc, g):
    H, NA, NV, HG = 256, 8, 32, 64
    with Scope(nc) as s:
        cbr, cbi = s.sb("ssm_cb_re", [P, NB, H]), s.sb("ssm_cb_im", [P, NB, H])
        p1, p2 = s.sb("ssm_coarse_1", [P, NA, H]), s.sb("ssm_coarse_2", [P, NA, H])
        V = s.sb("ssm_fine", [P, NV, H])
        with Scope(nc) as u:
            inp = u.sb("ssm_in", [P, 5, H])
            cin = u.sb("ssm_c_in", [P, 2, NB, H])
            vr, vi = u.sb("ssm_vr", [P, 16, H]), u.sb("ssm_vi", [P, 16, H])
            pr, pi = u.sb("ssm_pr", [P, NA, H]), u.sb("ssm_pi", [P, NA, H])
            x = u.sb("ssm_x", [P, 8, 2, H])
            w = u.sb("ssm_w", [P, 6, H])
            t1, t2 = u.sb("ssm_t1", [P, 16, H]), u.sb("ssm_t2", [P, 16, H])
            zeros = u.sb("ssm_zeros", [P, 1, 1024])
            loaded, text = u.sem("ssm_loaded"), u.sem("ssm_text_loaded")
            zeroed, cleared = u.sem("ssm_zeroed"), u.sem("ssm_cleared")
            vchain = u.sem("ssm_vchain")
            with nc.Block() as block:
                @block.sync
                def _(sp):
                    for i, n in enumerate(("s4_ldt", "s4_are", "s4_aim", "s4_bre", "s4_bim")):
                        sp.dma_start(inp[:, i, :], g.d[n]).then_inc(loaded, 16)
                    sp.dma_start(cin[:, 0], g.d["s4_cre"]).then_inc(loaded, 16)
                    sp.dma_start(cin[:, 1], g.d["s4_cim"]).then_inc(loaded, 16)
                    for b in range(NB):
                        sp.dma_start(g.h[:, 2:NC, b, :], g.d["txt"][b].rearrange("(c p) n -> p c n", p=P)
                                     ).then_inc(text, 16)
                    sp.wait_ge(zeroed, 1)
                    slots = g.slots.rearrange("(k p m n) -> k p m n", p=P, m=8, n=1024)
                    for k in range(slots.shape[0]):
                        sp.dma_start(slots[k], bc(zeros[:], [P, 8, 1024])).then_inc(cleared, 16)
                    sp.dma_start(g.scr_e[:, 0, :], zeros[0:NB, 0, 0:D]).then_inc(cleared, 16)
                    sp.wait_ge(text, 16 * NB)
                    sp.wait_ge(cleared, 16 * (slots.shape[0] + 1))

                @block.vector
                def _(dve):
                    link = chain(dve, vchain)

                    def mul(re, im, ar, ai, br, bi, k):
                        if re is not None:
                            dve.tensor_tensor(t1[:, 0:k], ar, br, ALU.mult)
                            link(dve.tensor_tensor(t2[:, 0:k], ai, bi, ALU.mult))
                            link(dve.tensor_tensor(re, t1[:, 0:k], t2[:, 0:k], ALU.subtract))
                        if im is not None:
                            dve.tensor_tensor(t1[:, 0:k], ar, bi, ALU.mult)
                            link(dve.tensor_tensor(t2[:, 0:k], ai, br, ALU.mult))
                            link(dve.tensor_tensor(im, t1[:, 0:k], t2[:, 0:k], ALU.add))

                    dve.memset(zeros[:], 0.0).then_inc(zeroed, 1)
                    dve.memset(vr[:, 0], 1.0)
                    dve.memset(vi[:, 0], 0.0)
                    dve.memset(pr[:, 0], 1.0)
                    link(dve.memset(pi[:, 0], 0.0))
                    dve.wait_ge(loaded, 16 * 7)
                    accurate_exp(dve, link, inp[:, 0:2], w[:, 0:2], w[:, 2:4], w[:, 4:6])
                    dve.scalar_tensor_tensor(w[:, 2], w[:, 0], -0.5, w[:, 1], ALU.mult, ALU.mult)
                    link(dve.scalar_tensor_tensor(w[:, 3], w[:, 0], 0.5, inp[:, 2], ALU.mult, ALU.mult))
                    dve.tensor_tensor(w[:, 4], w[:, 3], w[:, 3], ALU.mult)
                    dve.tensor_scalar(w[:, 0], w[:, 2], -1.0, 1.0, ALU.mult, ALU.add)
                    link(dve.tensor_tensor(w[:, 5], w[:, 2], w[:, 2], ALU.mult))
                    link(dve.tensor_tensor(w[:, 0], w[:, 0], w[:, 0], ALU.mult))
                    link(dve.tensor_tensor(w[:, 0], w[:, 0], w[:, 4], ALU.add))
                    link(dve.reciprocal(w[:, 1], w[:, 0]))
                    link(dve.tensor_tensor(w[:, 5], w[:, 5], w[:, 4], ALU.add))
                    link(dve.tensor_scalar(w[:, 5], w[:, 5], -1.0, 1.0, ALU.mult, ALU.add))
                    dve.tensor_tensor(x[:, 0, 0], w[:, 5], w[:, 1], ALU.mult)
                    link(dve.scalar_tensor_tensor(x[:, 0, 1], w[:, 3], 2.0, w[:, 1], ALU.mult, ALU.mult))
                    for i in range(7):
                        mul(x[:, i + 1, 0:1], x[:, i + 1, 1:2], x[:, i, 0:1], x[:, i, 1:2], x[:, i, 0:1],
                            x[:, i, 1:2], 1)
                    link(dve.tensor_scalar(inp[:, 3:5], inp[:, 3:5], 2.0, None, ALU.mult))
                    mul(cbr[:], cbi[:], cin[:, 0], cin[:, 1], bc(inp[:, 3:4], [P, NB, H]),
                        bc(inp[:, 4:5], [P, NB, H]), NB)
                    for i in range(4):
                        k = 1 << i
                        mul(vr[:, k:2 * k], vi[:, k:2 * k], vr[:, 0:k], vi[:, 0:k],
                            bc(x[:, i, 0:1], [P, k, H]), bc(x[:, i, 1:2], [P, k, H]), k)
                    for i in range(3):
                        k = 1 << i
                        mul(pr[:, k:2 * k], pi[:, k:2 * k], pr[:, 0:k], pi[:, 0:k],
                            bc(x[:, 5 + i, 0:1], [P, k, H]), bc(x[:, 5 + i, 1:2], [P, k, H]), k)
                    top, low = slice(0, 64), slice(64, 128)
                    dve.tensor_copy(V[top, 0:16], vr[top])
                    dve.tensor_copy(V[low, 0:16], vi[low])
                    dve.tensor_copy(p1[top], pr[top])
                    dve.tensor_scalar(p1[low], pi[low], -1.0, None, ALU.mult)
                    dve.tensor_scalar(p2[top], pi[top], -1.0, None, ALU.mult)
                    dve.tensor_scalar(p2[low], pr[low], -1.0, None, ALU.mult)
                    dve.tensor_copy(w[top, 0], x[top, 4, 0])
                    dve.tensor_copy(w[low, 0], x[low, 4, 1])
                    dve.tensor_scalar(w[top, 1], x[top, 4, 1], -1.0, None, ALU.mult)
                    link(dve.tensor_copy(w[low, 1], x[low, 4, 0]))
                    dve.tensor_tensor(t1[:], vr[:], bc(w[:, 0:1], [P, 16, H]), ALU.mult)
                    link(dve.tensor_tensor(t2[:], vi[:], bc(w[:, 1:2], [P, 16, H]), ALU.mult))
                    link(dve.tensor_tensor(V[:, 16:32], t1[:], t2[:], ALU.add))
            u.round_end()
        L = s.sb("ssm_left", [P, NB, NA, HG])
        Lt = s.sb("ssm_left_t", [P, NB, NA, HG])
        ko = s.sb("ssm_out", [NB * NA, HG, NV])
        vchain, l_ready, k_ready = s.sem("ssm_vchain2"), s.sem("ssm_left_ready"), s.sem("ssm_k_ready")
        k_out, stored, back = s.sem("ssm_k_copied"), s.sem("ssm_k_stored"), s.sem("ssm_k_back")
        NBK = HG * NV // 512
        with nc.Fori(0, H // HG) as r:
            with nc.Block() as block:
                @block.vector
                def _(dve):
                    link = chain(dve, vchain)
                    hs = bass.ds(r * HG, HG)
                    dve.tensor_tensor(L[:], bc(cbr[:, :, hs].unsqueeze(2), [P, NB, NA, HG]),
                                      bc(p1[:, :, hs].unsqueeze(1), [P, NB, NA, HG]), ALU.mult)
                    link(dve.tensor_tensor(Lt[:], bc(cbi[:, :, hs].unsqueeze(2), [P, NB, NA, HG]),
                                           bc(p2[:, :, hs].unsqueeze(1), [P, NB, NA, HG]), ALU.mult))
                    dve.tensor_tensor(L[:], L[:], Lt[:], ALU.add).then_inc(l_ready, 1)

                @block.tensor
                def _(pe):
                    pe.wait_ge(l_ready, 1)
                    Lf = L[:].rearrange("p c a h -> p (c a) h")
                    for j in range(HG):
                        per = 512 // NV
                        mm = pe.matmul(g.ps[0:NB * NA, j // per, (j % per) * NV:(j % per + 1) * NV],
                                       Lf[:, :, j], V[:, :, bass.ds(r * HG + j, 1)].rearrange("p v o -> p (v o)"),
                                       start=True, stop=True)
                        if j % per == per - 1:
                            mm.then_inc(k_ready, 1)

                @block.scalar
                def _(act):
                    kof = ko[:].rearrange("p h v -> p (h v)")
                    for k in range(NBK):
                        act.wait_ge(k_ready, k + 1)
                        act.activation(kof[:, k * 512:(k + 1) * 512], g.ps[0:NB * NA, k, :], ACT.Copy
                                       ).then_inc(k_out, 1)

                @block.sync
                def _(sp):
                    sp.wait_ge(k_out, NBK)
                    for b in range(NB):
                        dst = g.scr_ssm[b][bass.ds(r * HG, HG), :].rearrange("h (a v) -> a h v", a=NA)
                        sp.dma_start(dst, ko[b * NA:(b + 1) * NA]).then_inc(stored, 16)
                    sp.wait_ge(stored, 16 * NB)
            s.round_end()
        with nc.Block() as block:
            @block.sync
            def _(sp):
                for b in range(NB):
                    sp.dma_start(g.h[:, 0:2, b, :], g.scr_ssm[b].rearrange("(c p) n -> p c n", p=P)
                                 ).then_inc(back, 16)
                sp.wait_ge(back, 16 * NB)
        s.round_end()


def deltanet(nc, g):
    NG = 4
    E1 = 33
    with Scope(nc) as s:
        wqk = s.sb("dn_wqk", [P, 2, DC, D])
        wv = s.sb("dn_wv", [P, DC, D + 40])
        wout = s.sb("dn_wout", [P, DC, D])
        rows = s.sb("dn_rows", [P, 3 * D + 40 + 16])
        masks = s.sb("dn_masks", [P, 3 * P + 2 * 4 * E1])
        selc = s.sb("dn_sel", [48, 16, P], BF16)
        identb = s.sb("dn_identb", [P, P], BF16)
        S = s.sb("dn_state", [P, NB, 2, 2 * 4 * E1])
        xn, xnb, hb = s.sb("dn_xn", [P, NB, D]), s.sb("dn_xnb", [P, NB, D]), s.sb("dn_hb", [P, NB, D])
        xnT = s.sb("dn_xnT", [P, DC, NB * P])
        qT, kT = s.sb("dn_qT", [P, 2, NB * P]), s.sb("dn_kT", [P, 2, NB * P])
        er = s.sb("dn_exp_relu", [P, 2, 2, NB * P])
        kt, vt = s.sb("dn_k", [P, NB, D]), s.sb("dn_v", [P, NB, D + 40])
        er2 = s.sb("dn_exp_relu2", [P, 2, 2, D])
        raw = s.sb("dn_gates_raw", [P, NB, 40])
        eb = s.sb("dn_gates_exp", [P, NB, 40])
        lb = s.sb("dn_logdecay", [P, NB, 16])
        gate = s.sb("dn_gate", [P, NB, 8])
        wmix = s.sb("dn_wmix", [P, NB, 16])
        mtmp = s.sb("dn_mixtmp", [P, NB, 8])
        cc = s.sb("dn_cum", [P, 2, NB, 16])
        cres = s.sb("dn_cres", [P, 2, NB, 16])
        csp = s.sb("dn_csplit", [P, NB, 3, 16], BF16)
        crows = s.sb("dn_crows", [48, NB * P], BF16)
        ec, kd, dtot = s.sb("dn_ec", [P, NB, 16]), s.sb("dn_kd", [P, NB, 16]), s.sb("dn_dtot", [P, NB, 16])
        vg = s.sb("dn_vg", [P, NB, 8, E1])
        kdk = s.sb("dn_kdk", [P, NB, 2, 8, 32])
        Eb, Db, Mb = (s.sb(f"dn_{n}", [P, 2, 4, P]) for n in ("expo", "decay", "masked"))
        zt, um = s.sb("dn_zt", [P, 2, 2, 8, E1]), s.sb("dn_um", [P, 2, 2 * 4 * E1])
        den = s.sb("dn_den", [P, 2, 16])
        yy = s.sb("dn_y2", [P, 2, 8, 32])
        y = s.sb("dn_y", [P, NB, D])
        yT = s.sb("dn_yT", [P, DC, NB * P])
        stats, mv, rs, ltmp = s.sb("dn_stats", [P, NB, 6]), s.sb("dn_mv", [P, NB, 2]), s.sb("dn_rs", [P, NB]), s.sb("dn_ltmp", [P, 2, NB])
        bout, lng, lnb, gb, floor = (rows[:, 0:D], rows[:, D:2 * D], rows[:, 2 * D:3 * D],
                                     rows[:, 3 * D:3 * D + 40], rows[:, 3 * D + 40:3 * D + 56])
        tri_le, ones, cmask = masks[:, 0:P], masks[:, P:2 * P], masks[:, 2 * P:3 * P]
        bdmask = masks[:, 3 * P:3 * P + 2 * 4 * E1]
        kt_u = kt[:].rearrange("p b (f r e) -> p b (f r) e", f=2, r=4)

        def norm(dve, link, hc):
            layernorm(dve, link, [hc[:, b, :] for b in range(NB)], [xn[:, b, :] for b in range(NB)], stats, mv, rs, ltmp)

        with Scope(nc) as u:
            loaded, first_chain = u.sem("dn_loaded"), u.sem("dn_first_chain")
            with nc.Block() as block:
                @block.sync
                def _(sp):
                    for dst, n in ((wqk[:], "dn_wqk"), (wv[:], "dn_wv"), (wout[:], "dn_wout"), (rows[:], "dn_rows"),
                                   (masks[:], "dn_masks"), (selc[:], "dn_sel"), (identb[:], "identb")):
                        sp.dma_start(dst, g.d[n]).then_inc(loaded, 16)
                    sp.wait_ge(loaded, 16 * 7)

                @block.vector
                def _(dve):
                    dve.memset(S[:], 0.0)
                    dve.memset(g.h_spare[:, NC + 1], 0.0)
                    for t in (y, xnb, hb):
                        dve.memset(t[:], 0.0)
                    norm(dve, chain(dve, first_chain), g.h[:, 0])
            u.round_end()

        names = ("vchain pchain xnT_psum xnT_ready fm_psum fm_act qk_ready tm_psum tm_act tm_free tm_ready "
                 "gates_raw gates_exp mix_shift decay_arg decay_log c_psum c_ready csplit_ready crows_psum crows_ready "
                 "ec_ready kd_arg kd_ready vg_ready kdk_ready ae_psum e_used m_done d_ready y_psum z_psum "
                 "z_used u_psum um_ready s_ready comb_done y_read yT_psum yT_ready out_psum out_sum closed xnb_ready hb_ready").split()
        q = {n: s.sem("dn_" + n) for n in names}
        (vchain, pchain, xnT_psum, xnT_ready, fm_psum, fm_act, qk_ready, tm_psum, tm_act, tm_free, tm_ready,
         gates_raw, gates_exp, mix_shift, decay_arg, decay_log, c_psum, c_ready, csplit_ready, crows_psum, crows_ready,
         ec_ready, kd_arg, kd_ready, vg_ready, kdk_ready, ae_psum, e_used, m_done, d_ready, y_psum, z_psum,
         z_used, u_psum, um_ready, s_ready, comb_done, y_read, yT_psum, yT_ready, out_psum, out_sum, closed, xnb_ready, hb_ready) = (
             q[n] for n in names)
        ps = g.ps
        tmA = [6, 0, 6, 0]
        tmB = [7, 1, 7, 1]

        def turn_y(pe):
            for d in range(DC):
                for b in range(NB):
                    mm = pe.transpose(ps[:, 6 + d, b * P:(b + 1) * P], y[:, b, d * P:(d + 1) * P], g.ident[:])
            mm.then_inc(yT_psum, 1)

        def y_to_sbuf(act):
            act.wait_ge(yT_psum, 1)
            act.activation(yT[:, 0, :], ps[:, 6, :], ACT.Copy)
            act.activation(yT[:, 1, :], ps[:, 7, :], ACT.Copy).then_inc(yT_ready, 1)

        def out_product(pe):
            pe.wait_ge(yT_ready, 1)
            for b in range(NB):
                for d in range(DC):
                    mm = pe.matmul(ps[:, 2 + b, 0:D], yT[:, d, b * P:(b + 1) * P], wout[:, d, :],
                                   start=(d == 0), stop=(d == DC - 1))
                mm.then_inc(out_psum, 1)

        def close(dve, link, hc):
            for b in range(NB):
                dve.wait_ge(out_psum, b + 1)
                dve.tensor_tensor(xnb[:, b], xnb[:, b], ps[:, 2 + b, 0:D], ALU.add).then_inc(out_sum, 1)
            dve.wait_ge(out_sum, NB)
            layernorm(dve, link, [xnb[:, b, :] for b in range(NB)], [y[:, b, :] for b in range(NB)], stats, mv, rs, ltmp)
            link(dve.tensor_tensor(y[:], y[:], bc(lng.unsqueeze(1), [P, NB, D]), ALU.mult))
            dve.tensor_tensor(hc, y[:], hb[:], ALU.add).then_inc(closed, 1)

        with nc.Fori(0, NC) as c:
            hc = g.h[:, bass.ds(c, 1)].rearrange("p o b n -> p (o b) n")
            h_prev, h_next = (g.h_spare[:, bass.ds(c + k, 1)].rearrange("p o b n -> p (o b) n") for k in (0, 2))
            with nc.Block() as block:
                @block.tensor
                def _(pe):
                    turn_y(pe)
                    for d in range(DC):
                        for b in range(NB):
                            mm = pe.transpose(ps[:, d, b * P:(b + 1) * P], xn[:, b, d * P:(d + 1) * P], g.ident[:])
                    mm.then_inc(xnT_psum, 1)
                    out_product(pe)
                    pe.wait_ge(xnT_ready, 1)
                    for b in range(NB):
                        if b >= 2:
                            pe.wait_ge(tm_act, b - 1)
                        for d in range(DC):
                            pe.matmul(ps[:, tmA[b], 0:D + 40], xnT[:, d, b * P:(b + 1) * P], wv[:, d, :],
                                      start=(d == 0), stop=(d == DC - 1))
                        for d in range(DC):
                            mm = pe.matmul(ps[:, tmB[b], 0:D], xnT[:, d, b * P:(b + 1) * P], wqk[:, 1, d, :],
                                           start=(d == 0), stop=(d == DC - 1))
                        mm.then_inc(tm_psum, 1)
                    for w in range(2):
                        for f in range(2):
                            pe.wait_ge(out_sum, 2 * w + f + 1)
                            for d in range(DC):
                                mm = pe.matmul(ps[:, 2 + 2 * w + f, :], wqk[:, w, d, f * P:(f + 1) * P], xnT[:, d, :],
                                               start=(d == 0), stop=(d == DC - 1))
                            mm.then_inc(fm_psum, 1)
                    pe.wait_ge(decay_log, 1)
                    pe.wait_ge(tm_act, NB)
                    lbf = lb[:].rearrange("p b j -> p (b j)")
                    pe.matmul(ps[:, 6, 0:64], tri_le, lbf, start=True, stop=True)
                    pe.matmul(ps[:, 6, 64:128], ones, lbf, start=True, stop=True).then_inc(c_psum, 1)
                    pe.wait_ge(csplit_ready, 1)
                    crp = ps[0:48, 7, :].bitcast(BF16)
                    for b in range(NB):
                        mm = pe.transpose(crp[:, b * P:(b + 1) * P],
                                          csp[:, b].rearrange("p k j -> p (k j)"), identb[:])
                    mm.then_inc(crows_psum, 1)
                    pe.wait_ge(crows_ready, 1)
                    pe.wait_ge(qk_ready, 4)
                    pe.wait_ge(vg_ready, NB)
                    pe.wait_ge(tm_ready, NB)
                    for n in range(NB * NG + 2):
                        if n < NB * NG:
                            b, r = divmod(n, NG)
                            bs = slice(b * P, (b + 1) * P)
                            if r == 0:
                                if b >= 1:
                                    pe.wait_ge(um_ready, b)
                                for f in range(2):
                                    mm = pe.matmul(ps[:, 2 + f, 0:8 * E1], qT[:, f, bs], S[:, b, f, :],
                                                   start=True, stop=True)
                                mm.then_inc(z_psum, 1)
                            if n >= 2:
                                pe.wait_ge(m_done, n - 1)
                                pe.wait_ge(e_used, n - 1)
                            hr = slice(32 * r, 32 * r + 32)
                            for f in range(2):
                                pe.matmul(ps[:, 4 + n % 2, f * P:(f + 1) * P],
                                          kT[hr, f, bs], qT[hr, f, bs], start=True, stop=True)
                            for f in range(2):
                                for j in range(2):
                                    k = 2 * f + j
                                    mm = pe.matmul(ps[:, 6 + n % 2, k * P:(k + 1) * P], selc[:, f * 8 + j * 4 + r, :],
                                                   crows[:, bs], start=True, stop=True)
                            mm.then_inc(ae_psum, 1)
                            if r == 2:
                                pe.wait_ge(z_used, b + 1)
                                pe.wait_ge(kdk_ready, b + 1)
                                for f in range(2):
                                    for j in range(2):
                                        mm = pe.matmul(ps[:, 2 + f, j * 4 * E1:(j + 1) * 4 * E1],
                                                       kdk[:, b, j, 4 * f:4 * f + 4, :].rearrange("p h e -> p (h e)"),
                                                       vg[:, b, 4 * f:4 * f + 4, :].rearrange("p h e -> p (h e)"),
                                                       start=True, stop=True)
                                mm.then_inc(u_psum, 1)
                        if n >= 2:
                            b, r = divmod(n - 2, NG)
                            pe.wait_ge(m_done, n - 1)
                            if r == 0 and b >= 1:
                                pe.wait_ge(y_read, b)
                            for f in range(2):
                                for j in range(2):
                                    at = j * 4 * E1 + r * E1
                                    mm = pe.matmul(ps[:, f, at:at + E1], Mb[:, n % 2, 2 * f + j, :],
                                                   vg[:, b, 4 * f + r, :], start=True, stop=True)
                            mm.then_inc(y_psum, 1)

                @block.scalar
                def _(act):
                    y_to_sbuf(act)
                    act.wait_ge(xnT_psum, 1)
                    act.activation(xnT[:, 0, :], ps[:, 0, :], ACT.Copy)
                    act.activation(xnT[:, 1, :], ps[:, 1, :], ACT.Copy).then_inc(xnT_ready, 1)
                    for b in range(NB):
                        act.wait_ge(tm_psum, b + 1)
                        if b >= 2:
                            act.wait_ge(tm_ready, b - 1)
                        act.activation(vt[:, b, :], ps[:, tmA[b], 0:D + 40], ACT.Copy)
                        act.activation(er2[:, b % 2, 0, :], ps[:, tmB[b], 0:D], ACT.Exp)
                        act.activation(er2[:, b % 2, 1, :], ps[:, tmB[b], 0:D], ACT.Relu).then_inc(tm_act, 1)
                    act.wait_ge(gates_raw, 1)
                    act.activation(eb[:, :, 0:16], raw[:, :, 0:16], ACT.Exp, scale=-1.0)
                    act.activation(eb[:, :, 32:40], raw[:, :, 32:40], ACT.Exp, scale=-1.0).then_inc(gates_exp, 1)
                    act.wait_ge(mix_shift, 1)
                    act.activation(eb[:, :, 16:32], raw[:, :, 16:32], ACT.Exp).then_inc(gates_exp, 1)
                    act.wait_ge(decay_arg, 1)
                    act.activation(lb[:], eb[:, :, 0:16], ACT.Ln).then_inc(decay_log, 1)
                    for k in range(4):
                        act.wait_ge(fm_psum, k + 1)
                        if k >= 2:
                            act.wait_ge(qk_ready, k - 1)
                        act.activation(er[:, k % 2, 0, :], ps[:, 2 + k, :], ACT.Exp)
                        act.activation(er[:, k % 2, 1, :], ps[:, 2 + k, :], ACT.Relu).then_inc(fm_act, 1)
                    act.wait_ge(c_ready, 1)
                    act.activation(ec[:], cc[:, 0], ACT.Exp)
                    act.activation(dtot[:], cc[:, 1], ACT.Exp).then_inc(ec_ready, 1)
                    act.wait_ge(kd_arg, 1)
                    act.activation(kd[:], cres[:, 1], ACT.Exp).then_inc(kd_ready, 1)
                    act.wait_ge(crows_psum, 1)
                    act.activation(crows[:], ps[0:48, 7, 0:NB * P // 2].bitcast(BF16), ACT.Copy).then_inc(crows_ready, 1)
                    for n in range(NB * NG):
                        act.wait_ge(e_used, n + 1)
                        if n >= 2:
                            act.wait_ge(m_done, n - 1)
                        act.activation(Db[:, n % 2], Eb[:, n % 2], ACT.Exp).then_inc(d_ready, 1)

                @block.gpsimd
                def _(pool):
                    pool.wait_ge(closed, 1)
                    pool.tensor_tensor(xnb[:], xn[:], bc(bout.unsqueeze(1), [P, NB, D]), ALU.add).then_inc(xnb_ready, 1)
                    pool.tensor_tensor(hb[:], hc, bc(lnb.unsqueeze(1), [P, NB, D]), ALU.add).then_inc(hb_ready, 1)
                    pool.wait_ge(kd_ready, 1)
                    pool.wait_ge(tm_ready, NB)
                    pool.wait_ge(vg_ready, NB)
                    for b in range(NB):
                        for j in range(2):
                            for f in range(2):
                                k = 8 * f + 4 * j
                                op = pool.tensor_tensor(kdk[:, b, j, 4 * f:4 * f + 4, :], kt_u[:, b, 4 * f:4 * f + 4, :],
                                                        bc(kd[:, b, k:k + 4].unsqueeze(2), [P, 4, 32]), ALU.mult)
                        op.then_inc(kdk_ready, 1)
                    for b in range(NB):
                        pool.wait_ge(z_psum, b + 1)
                        Sb = S[:, b].rearrange("p f (k e) -> p (f k) e", e=E1)
                        pool.tensor_tensor(Sb, Sb, bc(dtot[:, b].unsqueeze(2), [P, 16, E1]), ALU.mult).then_inc(pchain, 1)
                        pool.wait_ge(pchain, b + 1)
                        pool.wait_ge(um_ready, b + 1)
                        pool.tensor_tensor(S[:, b], S[:, b], um[:], ALU.add).then_inc(s_ready, 1)

                @block.vector
                def _(dve):
                    link = chain(dve, vchain)
                    close(dve, link, h_prev)
                    for b in range(NB):
                        dve.wait_ge(tm_act, b + 1)
                        dve.tensor_tensor(raw[:, b], vt[:, b, D:D + 40], gb, ALU.add).then_inc(tm_free, 1)
                        dve.scalar_tensor_tensor(kt[:, b], er2[:, b % 2, 0], 1.0, er2[:, b % 2, 1], ALU.min, ALU.add
                                                 ).then_inc(tm_ready, 1)
                    dve.wait_ge(tm_free, NB)
                    dve.engine_nop().then_inc(gates_raw, 1)
                    mix = raw[:, :, 16:32].rearrange("p b (f j r) -> p b f j r", f=2, j=2)
                    mt = mtmp[:].rearrange("p b (f r) -> p b f r", f=2)
                    link(dve.tensor_tensor(mt, mix[:, :, :, 0], mix[:, :, :, 1], ALU.max))
                    dve.tensor_tensor(mix[:, :, :, 0], mix[:, :, :, 0], mt, ALU.subtract)
                    dve.tensor_tensor(mix[:, :, :, 1], mix[:, :, :, 1], mt, ALU.subtract).then_inc(mix_shift, 1)
                    dve.wait_ge(gates_exp, 1)
                    dve.tensor_scalar(eb[:, :, 0:16], eb[:, :, 0:16], 1.0, None, ALU.add)
                    link(dve.tensor_scalar(eb[:, :, 32:40], eb[:, :, 32:40], 1.0, None, ALU.add))
                    dve.reciprocal(gate[:], eb[:, :, 32:40])
                    link(dve.reciprocal(lb[:], eb[:, :, 0:16]))
                    link(dve.tensor_tensor(lb[:], lb[:], bc(floor.unsqueeze(1), [P, NB, 16]), ALU.mult))
                    dve.tensor_scalar(eb[:, :, 0:16], lb[:], 0.9999, 1e-19, ALU.min, ALU.max).then_inc(decay_arg, 1)
                    for b in range(NB):
                        vgb = vg[:, b]
                        dve.tensor_tensor(vgb[:, :, 0:32], vt[:, b, 0:D].rearrange("p (h e) -> p h e", h=8),
                                          bc(gate[:, b].unsqueeze(2), [P, 8, 32]), ALU.mult)
                        dve.tensor_copy(vgb[:, :, 32], gate[:, b]).then_inc(vg_ready, 1)
                    dve.wait_ge(gates_exp, 2)
                    em = eb[:, :, 16:32].rearrange("p b (f j r) -> p b f j r", f=2, j=2)
                    wm = wmix[:].rearrange("p b (f j r) -> p b f j r", f=2, j=2)
                    link(dve.tensor_tensor(mt, em[:, :, :, 0], em[:, :, :, 1], ALU.add))
                    link(dve.reciprocal(mt, mt))
                    dve.tensor_tensor(wm[:, :, :, 0], em[:, :, :, 0], mt, ALU.mult)
                    link(dve.tensor_tensor(wm[:, :, :, 1], em[:, :, :, 1], mt, ALU.mult))
                    dve.wait_ge(c_psum, 1)
                    dve.tensor_copy(cc[:].rearrange("p k b j -> p (k b j)"), ps[:, 6, 0:128]).then_inc(c_ready, 1)
                    dve.wait_ge(c_ready, 1)
                    dve.tensor_tensor(cres[:, 1], cc[:, 1], cc[:, 0], ALU.subtract).then_inc(kd_arg, 1)
                    link(dve.tensor_copy(csp[:, :, 0], cc[:, 0]))
                    link(dve.tensor_tensor(cres[:, 0], cc[:, 0], csp[:, :, 0], ALU.subtract))
                    link(dve.tensor_copy(csp[:, :, 1], cres[:, 0]))
                    link(dve.tensor_tensor(cres[:, 0], cres[:, 0], csp[:, :, 1], ALU.subtract))
                    dve.tensor_copy(csp[:, :, 2], cres[:, 0]).then_inc(csplit_ready, 1)
                    for k in range(4):
                        dve.wait_ge(fm_act, k + 1)
                        dst = (qT, kT)[k // 2][:, k % 2, :]
                        dve.scalar_tensor_tensor(dst, er[:, k % 2, 0, :], 1.0, er[:, k % 2, 1, :], ALU.min, ALU.add
                                                 ).then_inc(qk_ready, 1)
                    dve.wait_ge(xnb_ready, 1)
                    norm(dve, link, h_next)
                    for n in range(NB * NG + 3):
                        if 1 <= n <= NB * NG:
                            dve.wait_ge(d_ready, n)
                            if n >= 3:
                                dve.wait_ge(y_psum, n - 2)
                            a = ps[:, 4 + (n - 1) % 2, 0:256].rearrange("p (f t) -> p f t", f=2)
                            dve.tensor_tensor(Mb[:, (n - 1) % 2].rearrange("p (f j) t -> p f j t", f=2),
                                              Db[:, (n - 1) % 2].rearrange("p (f j) t -> p f j t", f=2),
                                              bc(a.unsqueeze(2), [P, 2, 2, P]), ALU.mult).then_inc(m_done, 1)
                        if n < NB * NG:
                            b, r = divmod(n, NG)
                            dve.wait_ge(ae_psum, n + 1)
                            if n >= 2:
                                dve.wait_ge(d_ready, n - 1)
                            for f in range(2):
                                for j in range(2):
                                    k, hj = 2 * f + j, 8 * f + 4 * j + r
                                    op = dve.scalar_tensor_tensor(Eb[:, n % 2, k, :], ps[:, 6 + n % 2, k * P:(k + 1) * P],
                                                                  cc[:, 0, b, hj:hj + 1], cmask, ALU.subtract, ALU.min)
                            op.then_inc(e_used, 1)
                            if r == 0:
                                dve.wait_ge(z_psum, b + 1)
                                dve.wait_ge(ec_ready, 1)
                                dve.tensor_tensor(zt[:, b % 2], ps[:, 2:4, 0:8 * E1].rearrange("p f (k e) -> p f k e", e=E1),
                                                  bc(ec[:, b].rearrange("p (f k) -> p f k", f=2).unsqueeze(3), [P, 2, 8, E1]),
                                                  ALU.mult).then_inc(z_used, 1)
                            if r == 3:
                                dve.wait_ge(u_psum, b + 1)
                                if b >= 1:
                                    dve.wait_ge(s_ready, b)
                                dve.tensor_tensor(um[:], ps[:, 2:4, 0:8 * E1],
                                                  bc(bdmask.unsqueeze(1), [P, 2, 8 * E1]), ALU.mult).then_inc(um_ready, 1)
                        if n >= 3 and (n - 3) % NG == NG - 1:
                            b = (n - 3) // NG
                            dve.wait_ge(y_psum, n - 2)
                            yp = ps[:, 0:2, 0:8 * E1].rearrange("p f (k e) -> p f k e", e=E1)
                            zb = zt[:, b % 2]
                            dve.tensor_tensor(zb, zb, yp, ALU.add).then_inc(y_read, 1)
                            dve.wait_ge(y_read, b + 1)
                            link(dve.tensor_scalar(den[:, 0].rearrange("p (f k) -> p f k", f=2), zb[:, :, :, 32], 1e-6,
                                                   None, ALU.add))
                            link(dve.reciprocal(den[:, 1], den[:, 0]))
                            link(dve.tensor_tensor(den[:, 0], den[:, 1], wmix[:, b], ALU.mult))
                            dw = den[:, 0].rearrange("p (f k) -> p f k", f=2)
                            for j in range(2):
                                op = dve.tensor_tensor(yy[:, j].rearrange("p (f r) e -> p f r e", f=2),
                                                       zb[:, :, 4 * j:4 * j + 4, 0:32],
                                                       bc(dw[:, :, 4 * j:4 * j + 4].unsqueeze(3), [P, 2, 4, 32]), ALU.mult)
                            link(op)
                            dve.tensor_tensor(y[:, b].rearrange("p (h e) -> p h e", e=32), yy[:, 0], yy[:, 1], ALU.add
                                              ).then_inc(comb_done, 1)
            s.round_end()
        with nc.Block() as block:
            @block.tensor
            def _(pe):
                turn_y(pe)
                out_product(pe)

            @block.scalar
            def _(act):
                y_to_sbuf(act)

            @block.vector
            def _(dve):
                close(dve, chain(dve, vchain), g.h[:, NC - 1])
        s.round_end()



def pick_top(dve, link, vals, k, v8, sel, eq, cum, cnt, ones):
    n, E = vals.shape[1], vals.shape[2]
    for i in range(n):
        op = dve.max(v8[:, i, :], vals[:, i, :])
    link(op)
    t = bc(v8[:, 0:n, k - 1:k], [P, n, E])
    dve.tensor_tensor(eq, vals, t, ALU.is_equal)
    link(dve.tensor_tensor(sel, vals, t, ALU.is_gt))
    dve.tensor_reduce(cnt[:, 0:n], sel, AX_X, ALU.add)
    for i in range(n):
        op = dve.tensor_tensor_scan(cum[:, i, :], ones[:, 0:E], eq[:, i, :], 0.0, ALU.mult, ALU.add)
    link(op)
    link(dve.tensor_tensor(cum, cum, bc(cnt[:, 0:n].unsqueeze(2), [P, n, E]), ALU.add))
    link(dve.tensor_scalar(cum, cum, float(k), None, ALU.is_le))
    link(dve.tensor_tensor(eq, eq, cum, ALU.mult))
    link(dve.tensor_tensor(sel, sel, eq, ALU.add))


def attn_project(nc, g):
    with Scope(nc) as s:
        wqk, wv = s.sb("ap_wqk", [P, 2, DC, D]), s.sb("ap_wv", [P, DC, D])
        rows = s.sb("ap_rows", [P, 3 * D])
        qkb = s.sb("ap_qkb", [P, 4])
        nx2 = s.sb("ap_nx", [P, 2, NB, D])
        nxT2 = s.sb("ap_nxT", [P, 2, DC, NB * P])
        res2 = s.sb("ap_res", [P, 2, 4, NB * P])
        parts2 = s.sb("ap_parts", [P, 2, 4, 3, NB * P], BF16)
        stats, mv, rs, ltmp = s.sb("ap_stats", [P, NB, 6]), s.sb("ap_mv", [P, NB, 2]), s.sb("ap_rs", [P, NB]), s.sb("ap_ltmp", [P, 2, NB])
        with Scope(nc) as u:
            loaded = u.sem("ap_loaded")
            with nc.Block() as block:
                @block.sync
                def _(sp):
                    for dst, n in ((wqk[:], "at_wqk"), (wv[:], "at_wv"), (rows[:], "at_rows"), (qkb[:], "at_qkb")):
                        sp.dma_start(dst, g.d[n]).then_inc(loaded, 16)
                    sp.wait_ge(loaded, 16 * 4)
            u.round_end()
        vchain, nx_ready, nxT_psum, nxT_ready = s.sem("ap_vchain"), s.sem("ap_nx"), s.sem("ap_nxT_psum"), s.sem("ap_nxT")
        qk_psum, v_psum, v_used, res_ready, part_ready, stored = (s.sem("ap_qk_psum"), s.sem("ap_v_psum"), s.sem("ap_v_used"), s.sem("ap_res_ready"),
                                                          s.sem("ap_part"), s.sem("ap_stored"))
        ps = g.ps
        with nc.Fori(0, NC // 2) as r:
            def at_chunk(t, u, pat):
                return t[:, bass.ds(r * 2 + u, 1)].rearrange(pat)
            with nc.Block() as block:
                @block.tensor
                def _(pe):
                    for u in range(2):
                        nx, nxT = nx2[:, u], nxT2[:, u]
                        pe.wait_ge(nx_ready, u + 1)
                        for d in range(DC):
                            for b in range(NB):
                                mm = pe.transpose(ps[:, d, b * P:(b + 1) * P], nx[:, b, d * P:(d + 1) * P], g.ident[:])
                        mm.then_inc(nxT_psum, 1)
                        pe.wait_ge(nxT_ready, u + 1)
                        for w in range(2):
                            for f in range(2):
                                if u:
                                    pe.wait_ge(res_ready, 2 * w + f + 1)
                                for d in range(DC):
                                    mm = pe.matmul(ps[:, 2 + 2 * w + f, :], wqk[:, w, d, f * P:(f + 1) * P], nxT[:, d, :],
                                                   start=(d == 0), stop=(d == DC - 1))
                                mm.then_inc(qk_psum, 1)
                        for b in range(NB):
                            if u and b % 2 == 0:
                                pe.wait_ge(v_used, b // 2 + 1)
                            for d in range(DC):
                                mm = pe.matmul(ps[:, 6 + b // 2, (b % 2) * D:(b % 2 + 1) * D], nxT[:, d, b * P:(b + 1) * P],
                                               wv[:, d, :], start=(d == 0), stop=(d == DC - 1))
                            if b % 2:
                                mm.then_inc(v_psum, 1)

                @block.scalar
                def _(act):
                    def rows_to_sbuf(u):
                        act.wait_ge(nxT_psum, u + 1)
                        act.activation(nxT2[:, u, 0, :], ps[:, 0, :], ACT.Copy)
                        act.activation(nxT2[:, u, 1, :], ps[:, 1, :], ACT.Copy).then_inc(nxT_ready, 1)
                    rows_to_sbuf(0)
                    for u in range(2):
                        for part in range(3):
                            if u == 0 and part == 1:
                                rows_to_sbuf(1)
                            for k in range(4):
                                act.wait_ge(res_ready, 12 * u + 4 * part + k + 1)
                                act.activation(parts2[:, u, k, part, :], res2[:, u, k, :], ACT.Copy).then_inc(part_ready, 1)

                @block.sync
                def _(sp):
                    for u in range(2):
                        for part in range(3):
                            sp.wait_ge(part_ready, 12 * u + 4 * (part + 1))
                            for k in range(4):
                                dst = g.scr_qk[k // 2, part, (k % 2) * P:(k % 2 + 1) * P, :, bass.ds((r * 2 + u) * P, P)]
                                sp.dma_start(dst, parts2[:, u, k, part, :].rearrange("p (b t) -> p b t", b=NB)
                                             ).then_inc(stored, 16)
                    sp.wait_ge(stored, 16 * 24)

                @block.vector
                def _(dve):
                    link = chain(dve, vchain)

                    def norms(u):
                        hc, zc = at_chunk(g.h, u, "p o b n -> p (o b) n"), at_chunk(g.z, u, "p o b n -> p (o b) n")
                        nx = nx2[:, u]
                        layernorm(dve, link, [hc[:, b, :] for b in range(NB)], [zc[:, b, :] for b in range(NB)],
                                  stats, mv, rs, ltmp)
                        layernorm(dve, link, [zc[:, b, :] for b in range(NB)], [nx[:, b, :] for b in range(NB)],
                                  stats, mv, rs, ltmp)
                        link(dve.tensor_tensor(nx, nx, bc(rows[:, 0:D].unsqueeze(1), [P, NB, D]), ALU.mult))
                        dve.tensor_tensor(nx, nx, bc(rows[:, D:2 * D].unsqueeze(1), [P, NB, D]), ALU.add
                                          ).then_inc(nx_ready, 1)

                    def results(u):
                        vc = at_chunk(g.v, u, "p o b h e -> p (o b) h e")
                        res = res2[:, u]
                        for k in range(4):
                            dve.wait_ge(qk_psum, 4 * u + k + 1)
                            dve.tensor_scalar(res[:, k, :], ps[:, 2 + k, :], qkb[:, k:k + 1], 0.25 if k < 2 else 1.0,
                                              ALU.add, ALU.mult).then_inc(res_ready, 1)
                        for m in range(2):
                            dve.wait_ge(v_psum, 2 * u + m + 1)
                            dve.tensor_tensor(vc[:, 2 * m:2 * m + 2], ps[:, 6 + m, :].rearrange("p (b h e) -> p b h e", b=2, h=16),
                                              bc(rows[:, 2 * D:3 * D].rearrange("p (h e) -> p h e", h=16).unsqueeze(1),
                                                 [P, 2, 16, 16]), ALU.add).then_inc(v_used, 1)
                        for part in range(2):
                            for k in range(4):
                                dve.wait_ge(part_ready, 12 * u + 4 * part + k + 1)
                                dve.tensor_tensor(res[:, k, :], res[:, k, :], parts2[:, u, k, part, :], ALU.subtract
                                                  ).then_inc(res_ready, 1)
                    for u in range(2):
                        norms(u)
                    for u in range(2):
                        results(u)
            s.round_end()


def attn_heads(nc, g):
    NH, E = 16, 16
    KT, QT = (0, 1, 0, 2, 0, 1), (0, 0, 1, 0, 2, 1)
    blocks = [(kb, qc) for kb in range(NC) for qc in range(kb, NC)]
    at = {kq: i for i, kq in enumerate(blocks)}
    cuts = [0, 4, 8, 12, 15, 18, 21]
    pieces = []
    for a, z in zip(cuts, cuts[1:]):
        runs = []
        for i in range(a, z):
            kb, qc = blocks[i]
            if runs and runs[-1][0] == kb:
                runs[-1][2] += 1
            else:
                runs.append([kb, qc, 1, i - a])
        pieces.append((a, z - a, runs))
    NPC = len(pieces)
    MAX_AT = 2
    with Scope(nc) as s:
        k6, q6 = s.sb("ah_k6", [99, NH, SEQ], BF16), s.sb("ah_q6", [99, NH, SEQ], BF16)
        vb = s.sb("ah_v", [P, NC, NH // 2, 2, 4 * E])
        probs = s.sb("ah_probs", [P, 2, len(blocks) * P])
        consts = s.sb("ah_consts", [P, 3 * P], BF16)
        mx = s.sb("ah_max", [P, 2, NC])
        mres = s.sb("ah_mres", [P, NC])
        msp = s.sb("ah_msplit", [P, 2, NC, 4], BF16)
        num, den = s.sb("ah_num", [2 * E, SEQ]), s.sb("ah_den", [2 * E, SEQ])
        identb, qmask, kmask = (consts[:, i * P:(i + 1) * P] for i in range(3))
        with Scope(nc) as u:
            loaded, zeroed = u.sem("ah_loaded"), u.sem("ah_zeroed")
            with nc.Block() as block:
                @block.sync
                def _(sp):
                    sp.dma_start(consts[:], g.d["at_consts"]).then_inc(loaded, 16)
                    sp.wait_ge(loaded, 16)

                @block.gpsimd
                def _(pool):
                    pool.memset(k6[96:99], -1.0)

                @block.vector
                def _(dve):
                    dve.memset(vb[:], 0.0).then_inc(zeroed, 1)
                    dve.wait_ge(zeroed, 1)
                    for k in range(2):
                        sums = vb[:, :, :, k, (2 + k) * E:(3 + k) * E].rearrange("p c q e -> p (c q) e")
                        dve.memset(sums, 1.0)
            u.round_end()
        qk_loaded = [s.sem(f"ah_qk_loaded{i}") for i in range(4)]
        vchain, v_ready, s_psum, s_used, msp_ready, mT_psum, mT_ready, e_psum, e_done, o_psum, o_used, inverted, o_ready = (
            s.sem("ah_" + n) for n in "vchain v_ready s_psum s_used msp_ready mT_psum mT_ready e_psum e_done o_psum o_used inverted o_ready".split())
        ps = g.ps
        with nc.Fori(0, NB) as b:
            with nc.Block() as block:
                @block.sync
                def _(sp):
                    for hq in range(4):
                        for t in range(6):
                            for w, dst, part in ((0, q6, QT[t]), (1, k6, KT[t])):
                                src = g.scr_qk[w, part, 64 * hq:64 * hq + 64, bass.ds(b, 1), :]
                                sp.dma_start(dst[16 * t:16 * t + 16, 4 * hq:4 * hq + 4, :],
                                             src.rearrange("(h e) o s -> e h (o s)", e=E)).then_inc(qk_loaded[hq], 16)

                @block.gpsimd
                def _(pool):
                    vh = g.v[:, :, bass.ds(b, 1)].rearrange("p c o (q k) e -> p c (o q) k e", k=2)
                    for k in range(2):
                        op = pool.tensor_copy(vb[:, :, :, k, k * E:(k + 1) * E], vh[:, :, :, k, :])
                    op.then_inc(v_ready, 1)
                    for q in range(NH // 2):
                        pool.wait_ge(inverted, q + 1)
                        dst = g.aT[(q % 4) * 2 * E:(q % 4 + 1) * 2 * E, q // 4, bass.ds(b, 1), :]
                        pool.tensor_tensor(dst.rearrange("p o n -> p (o n)"), num[:], den[:], ALU.mult).then_inc(o_ready, 1)

                @block.tensor
                def _(pe):
                    def scores(i, qc):
                        n = i * NC + qc
                        bank = 2 if qc in (1, 3) else 0
                        if n >= 2:
                            pe.wait_ge(s_used, n if qc in (0, 5) else n - 1)
                        k1 = min((qc + 1) * P, 512)
                        lhs = q6[0:96, i, qc * P:(qc + 1) * P]
                        pe.matmul(ps[:, bank, 0:k1], lhs, k6[0:96, i, 0:k1], start=True, stop=qc > 3)
                        if qc > 3:
                            k2 = (qc + 1) * P
                            pe.matmul(ps[:, bank + 1, 0:k2 - 512], lhs, k6[0:96, i, 512:k2], start=True, stop=False)
                        dk = (qc % 4) * P
                        pe.matmul(ps[:, bank + qc // 4, dk:dk + P], identb, qmask, start=False, stop=True).then_inc(s_psum, 1)

                    def maxima(h):
                        pe.wait_ge(msp_ready, h + 1)
                        if h >= 1:
                            pe.wait_ge(mT_ready, h)
                        for qc in range(NC):
                            mm = pe.transpose(ps[0:3, 3, :].bitcast(BF16)[:, qc * P:(qc + 1) * P], msp[:, h % 2, qc, 0:3], identb)
                        mm.then_inc(mT_psum, 1)

                    def exponents(h, p):
                        first, nb, runs = pieces[p]
                        if p == 0:
                            pe.wait_ge(mT_ready, h + 1)
                        n = h * NPC + p
                        bank = 4 + n % 2
                        if n >= 2:
                            pe.wait_ge(e_done, n - 1)
                        for kb, qc, m, off in runs:
                            o, w = ps[:, bank, off * P:(off + m) * P], slice(qc * P, (qc + m) * P)
                            mm = pe.matmul(o, k6[:, h, kb * P:(kb + 1) * P], q6[:, h, w], start=True, stop=qc != kb)
                            if qc == kb:
                                mm = pe.matmul(ps[:, bank, off * P:(off + 1) * P], identb, kmask, start=False, stop=True)
                        mm.then_inc(e_psum, 1)

                    def outputs(h, kb):
                        if kb == 0:
                            pe.wait_ge(e_done, NPC * (h + 1))
                            if h >= 2 and h % 2 == 0:
                                pe.wait_ge(o_used, h // 2)
                        for bank, lo, hi in ((6, 0, 512), (7, 512, SEQ)):
                            lo = max(lo, kb * P)
                            if lo < hi:
                                at0 = (at[kb, kb] - kb) * P
                                last = h % 2 == 1 and kb == hi // P - 1
                                mm = pe.matmul(ps[0:4 * E, bank, lo % 512:(hi - 1) % 512 + 1], vb[:, kb, h // 2, h % 2, :],
                                               probs[:, h % 2, at0 + lo:at0 + hi], start=(kb == 0 and h % 2 == 0), stop=last)
                        if kb == NC - 1:
                            mm.then_inc(o_psum, 1)

                    pe.wait_ge(v_ready, 1)
                    for i in range(NH + 3):
                        if i < NH and i % 4 == 0:
                            pe.wait_ge(qk_loaded[i // 4], 16 * 12)
                        for j in range(NC):
                            if i < NH:
                                scores(i, j)
                            if j == MAX_AT and 1 <= i <= NH:
                                maxima(i - 1)
                            if 2 <= i <= NH + 1:
                                exponents(i - 2, j)
                            if i >= 3:
                                for kb in ((), (), (0,), (1,), (2, 3), (4, 5))[j]:
                                    outputs(i - 3, kb)

                @block.scalar
                def _(act):
                    def take_outputs(q):
                        act.wait_ge(o_psum, 2 * (q + 1))
                        if q >= 1:
                            act.wait_ge(o_ready, q)
                        o = ps[:, 6:8, :].rearrange("p k n -> p (k n)")
                        act.activation(num[:], o[0:2 * E, 0:SEQ], ACT.Copy)
                        act.activation(den[:], o[2 * E:4 * E, 0:SEQ], ACT.Copy).then_inc(o_used, 1)

                    for h in range(NH):
                        for p, (first, nb, runs) in enumerate(pieces):
                            if p == 0 and h >= 3 and h % 2:
                                take_outputs((h - 3) // 2)
                            act.wait_ge(e_psum, h * NPC + p + 1)
                            if p == 0 and h >= 2:
                                act.wait_ge(o_psum, h - 1)
                            act.activation(probs[:, h % 2, first * P:(first + nb) * P], ps[:, 4 + (h * NPC + p) % 2, 0:nb * P],
                                           ACT.Exp).then_inc(e_done, 1)
                    take_outputs(NH // 2 - 1)

                @block.vector
                def _(dve):
                    link = chain(dve, vchain)
                    def maxima_to_rows(h):
                        dve.wait_ge(mT_psum, h + 1)
                        dve.tensor_copy(q6[96:99, h, :], ps[0:3, 3, :].bitcast(BF16)[:, 0:SEQ]).then_inc(mT_ready, 1)

                    for i in range(NH + 5):
                        for qc in range(NC):
                            if i < NH:
                                n = i * NC + qc
                                dve.wait_ge(s_psum, n + 1)
                                bank = 2 if qc in (1, 3) else 0
                                src = ps[:, bank:bank + 2, :].rearrange("p k n -> p (k n)")
                                dve.tensor_reduce(mx[:, i % 2, qc:qc + 1], src[:, 0:(qc + 1) * P], AX_X, ALU.max
                                                  ).then_inc(s_used, 1)
                            if qc == MAX_AT and 1 <= i <= NH:
                                maxima_to_rows(i - 1)
                            if i >= 5:
                                q, k = (i - 5) // 2, (i - 5) % 2 * NC + qc
                                if k == 0:
                                    dve.wait_ge(o_used, q + 1)
                                part = slice(k * P // 2, (k + 1) * P // 2)
                                op = dve.reciprocal(den[:, part], den[:, part])
                                if k == 2 * NC - 1:
                                    op.then_inc(inverted, 1)
                        if i < NH:
                            dve.wait_ge(s_used, NC * (i + 1))
                            if i >= 2:
                                dve.wait_ge(mT_psum, i - 1)
                            mp, m = msp[:, i % 2], mx[:, i % 2]
                            link(dve.tensor_copy(mp[:, :, 0], m))
                            link(dve.tensor_tensor(mres[:], m, mp[:, :, 0], ALU.subtract))
                            link(dve.tensor_copy(mp[:, :, 1], mres[:]))
                            link(dve.tensor_tensor(mres[:], mres[:], mp[:, :, 1], ALU.subtract))
                            dve.tensor_copy(mp[:, :, 2], mres[:]).then_inc(msp_ready, 1)
            s.round_end()


def attn_finish(nc, g):
    NE = 8
    with Scope(nc) as s:
        wo, gw = s.sb("af_wo", [P, DC, D]), s.sb("af_gw", [P, DC, NE])
        rows = s.sb("af_rows", [P, 3 * D])
        b2 = s.sb("af_b2", [NE, D])
        lg_all = s.sb("af_logits", [P, NC, NB, NE])
        x1s, nxs = s.sb("af_x1", [P, 2, NB, D]), s.sb("af_nx", [P, 2, NB, D])
        aTs, nTs = s.sb("af_aT", [P, 2, DC, NB * P]), s.sb("af_nT", [P, 2, DC, NB * P])
        stats, mv, rs, ltmp = s.sb("af_stats", [P, NB, 6]), s.sb("af_mv", [P, NB, 2]), s.sb("af_rs", [P, NB]), s.sb("af_ltmp", [P, 2, NB])
        with Scope(nc) as u:
            loaded = u.sem("af_loaded")
            with nc.Block() as block:
                @block.sync
                def _(sp):
                    for dst, n in ((wo[:], "at_wo"), (gw[:], "m0_gate"), (rows[:], "af_rows"), (b2[:], "m0_b2")):
                        sp.dma_start(dst, g.d[n]).then_inc(loaded, 16)
                    sp.wait_ge(loaded, 16 * 4)
            u.round_end()
        (vchain, aT_ready, out_psum, zb_ready, x1_ready, h_added, nx_ready, nT_psum, nT_ready, lg_psum, nx_kept) = (
            s.sem("af_" + n) for n in ("vchain aT_ready out_psum zb_ready x1_ready h_added nx_ready nT_psum nT_ready lg_psum "
                                       "nx_kept").split())
        ps = g.ps
        with nc.Fori(0, NC // 2) as r:
            def at_u(t, u):
                return t[:, bass.ds(r * 2 + u, 1)].rearrange("p o b n -> p (o b) n")
            with nc.Block() as block:
                @block.tensor
                def _(pe):
                    for u in range(2):
                        pe.wait_ge(aT_ready, u + 1)
                        for b in range(NB):
                            if u:
                                pe.wait_ge(x1_ready, b + 1)
                            for d in range(DC):
                                mm = pe.matmul(ps[:, 2 + b, 0:D], aTs[:, u, d, b * P:(b + 1) * P], wo[:, d, :],
                                               start=(d == 0), stop=(d == DC - 1))
                            mm.then_inc(out_psum, 1)
                    for u in range(2):
                        pe.wait_ge(nx_ready, u + 1)
                        for d in range(DC):
                            for b in range(NB):
                                mm = pe.transpose(ps[:, d, b * P:(b + 1) * P], nxs[:, u, b, d * P:(d + 1) * P], g.ident[:])
                        mm.then_inc(nT_psum, 1)
                        pe.wait_ge(nT_ready, u + 1)
                        for b in range(NB):
                            for d in range(DC):
                                mm = pe.matmul(ps[:, 6 + u, b * NE:(b + 1) * NE], nTs[:, u, d, b * P:(b + 1) * P], gw[:, d, :],
                                               start=(d == 0), stop=(d == DC - 1))
                        mm.then_inc(lg_psum, 1)

                @block.scalar
                def _(act):
                    for u in range(2):
                        src = g.aT[:, :, :, bass.ds((r * 2 + u) * P, P)]
                        act.activation(aTs[:, u].rearrange("p d (b n) -> p d b n", b=NB), src, ACT.Copy).then_inc(aT_ready, 1)
                    for u in range(2):
                        act.wait_ge(nT_psum, u + 1)
                        act.activation(nTs[:, u, 0, :], ps[:, 0, :], ACT.Copy)
                        act.activation(nTs[:, u, 1, :], ps[:, 1, :], ACT.Copy).then_inc(nT_ready, 1)

                @block.gpsimd
                def _(pool):
                    for u in range(2):
                        pool.tensor_tensor(x1s[:, u], at_u(g.z, u), bc(rows[:, 0:D].unsqueeze(1), [P, NB, D]), ALU.add
                                           ).then_inc(zb_ready, 1)
                    for u in range(2):
                        pool.wait_ge(x1_ready, NB * (u + 1))
                        pool.tensor_tensor(at_u(g.h, u), at_u(g.h, u), x1s[:, u], ALU.add).then_inc(h_added, 1)
                        pool.wait_ge(nx_ready, u + 1)
                        pool.tensor_copy(at_u(g.z, u), nxs[:, u]).then_inc(nx_kept, 1)

                @block.vector
                def _(dve):
                    link = chain(dve, vchain)
                    for u in range(2):
                        x1, nx = x1s[:, u], nxs[:, u]
                        dve.wait_ge(zb_ready, u + 1)
                        for b in range(NB):
                            dve.wait_ge(out_psum, NB * u + b + 1)
                            dve.tensor_tensor(x1[:, b], x1[:, b], ps[:, 2 + b, 0:D], ALU.add).then_inc(x1_ready, 1)
                        dve.wait_ge(x1_ready, NB * (u + 1))
                        layernorm(dve, link, [x1[:, b, :] for b in range(NB)], [nx[:, b, :] for b in range(NB)],
                                  stats, mv, rs, ltmp)
                        link(dve.tensor_tensor(nx, nx, bc(rows[:, D:2 * D].unsqueeze(1), [P, NB, D]), ALU.mult))
                        dve.tensor_tensor(nx, nx, bc(rows[:, 2 * D:3 * D].unsqueeze(1), [P, NB, D]), ALU.add
                                          ).then_inc(nx_ready, 1)
                    for u in range(2):
                        dve.wait_ge(lg_psum, u + 1)
                        dve.tensor_copy(at_u(lg_all, u), ps[:, 6 + u, 0:NB * NE].rearrange("p (b e) -> p b e", b=NB))
            s.round_end()
        top2_gates(nc, g, lg_all, b2)


def top2_gates(nc, g, lg_all, b2):
    NE, NTT = 8, NC * NB
    with Scope(nc) as s:
        sel, eq, cum, gt = (s.sb("tg_" + n, [P, NTT, NE]) for n in ("sel", "eq", "cum", "gates"))
        v8, cnt = s.sb("tg_v8", [P, NTT, 8]), s.sb("tg_cnt", [P, NTT])
        gT = s.sb("tg_gT", [NE, NTT * P])
        ones = s.sb("tg_ones", [P, 32])
        vchain, lg_ready, e_ready, g_ready, gT_psum, gT_ready, bias_psum, bias_used = (
            s.sem("tg_" + n) for n in "vchain lg_ready e_ready g_ready gT_psum gT_ready bias_psum bias_used".split())
        ps, PER = g.ps, 4
        lg = lg_all[:].rearrange("p c b e -> p (c b) e")
        with nc.Block() as block:
            @block.tensor
            def _(pe):
                pe.wait_ge(g_ready, 1)
                for k in range(NC):
                    for b in range(NB):
                        mm = pe.transpose(ps[0:NE, k, b * P:(b + 1) * P], gt[:, k * NB + b, :], g.ident[:])
                    mm.then_inc(gT_psum, 1)
                for c in range(NC):
                    pe.wait_ge(gT_ready, NC)
                    if c >= PER:
                        pe.wait_ge(bias_used, c - PER + 1)
                    for b in range(NB):
                        mm = pe.matmul(ps[:, 2 * (c % PER) + b // 2, (b % 2) * D:(b % 2 + 1) * D],
                                       gT[:, (c * NB + b) * P:(c * NB + b + 1) * P], b2[:], start=True, stop=True)
                    mm.then_inc(bias_psum, 1)

            @block.scalar
            def _(act):
                act.wait_ge(lg_ready, 1)
                act.activation(gt[:], lg, ACT.Exp).then_inc(e_ready, 1)
                for k in range(NC):
                    act.wait_ge(gT_psum, k + 1)
                    act.activation(gT[:, k * NB * P:(k + 1) * NB * P], ps[0:NE, k, :], ACT.Copy).then_inc(gT_ready, 1)

            @block.vector
            def _(dve):
                link = chain(dve, vchain)
                link(dve.memset(ones[:], 1.0))
                pick_top(dve, link, lg, 2, v8[:], sel[:], eq[:], cum[:], cnt[:], ones[:])
                dve.tensor_tensor(lg, lg, bc(v8[:, :, 0:1], [P, NTT, NE]), ALU.subtract).then_inc(lg_ready, 1)
                dve.tensor_copy(g.sel0[:].rearrange("p c b e -> p (c b) e"), sel[:])
                dve.wait_ge(e_ready, 1)
                link(dve.tensor_tensor(lg, gt[:], sel[:], ALU.mult))
                link(dve.tensor_reduce(cnt[:], lg, AX_X, ALU.add))
                link(dve.reciprocal(cnt[:], cnt[:]))
                dve.tensor_tensor(gt[:], lg, bc(cnt[:].unsqueeze(2), [P, NTT, NE]), ALU.mult).then_inc(g_ready, 1)
                dve.wait_ge(g_ready, 1)
                dve.tensor_copy(g.gates0[:].rearrange("p c b e -> p (c b) e"), gt[:])
                for c in range(NC):
                    dve.wait_ge(bias_psum, c + 1)
                    bank = 2 * (c % PER)
                    dve.tensor_tensor(g.h[:, c].rearrange("p b n -> p (b n)"), g.h[:, c].rearrange("p b n -> p (b n)"),
                                      ps[:, bank:bank + 2, :].rearrange("p k n -> p (k n)"), ALU.add).then_inc(bias_used, 1)
        s.round_end()


def time_mix(nc, g):
    NE = 8
    with Scope(nc) as s:
        wk, wo, rw = s.sb("tm_wkvr", [P, 3, DC, D]), s.sb("tm_wo", [P, DC, D]), s.sb("tm_router", [P, DC, NE])
        rows, cols = s.sb("tm_rows", [P, 4 * D]), s.sb("tm_cols", [P, 5, DC])
        hn, xn = s.sb("tm_hn", [P, NC, D]), s.sb("tm_xn", [P, NC, D])
        xT, dT = s.sb("tm_xT", [P, DC, SEQ + 1]), s.sb("tm_dT", [P, DC, SEQ])
        mix = s.sb("tm_mix", [P, 3, DC, SEQ])
        kk, vv, rr = s.sb("tm_k", [P, DC, SEQ]), s.sb("tm_v", [P, DC, SEQ]), s.sb("tm_r", [P, DC, SEQ])
        pp, aa, bb = (s.sb("tm_" + n, [P, DC, SEQ + 1]) for n in ("pp", "aa", "bb"))
        t = s.sb("tm_t", [P, 4, DC, SEQ])
        stats, mv, rs, ltmp = s.sb("tm_stats", [P, NC, 6]), s.sb("tm_mv", [P, NC, 2]), s.sb("tm_rs", [P, NC]), s.sb("tm_ltmp", [P, 2, NC])
        with Scope(nc) as u:
            loaded, decay = u.sem("tm_loaded"), u.sem("tm_decay")
            with nc.Block() as block:
                @block.sync
                def _(sp):
                    for dst, n in ((wk[:], "tm_wkvr"), (wo[:], "tm_wo"), (rw[:], "m1_router"), (rows[:], "tm_rows"),
                                   (cols[:], "tm_cols")):
                        sp.dma_start(dst, g.d[n]).then_inc(loaded, 16)
                    sp.wait_ge(loaded, 16 * 5)

                @block.scalar
                def _(act):
                    act.wait_ge(loaded, 16 * 5)
                    act.activation(cols[:, 3], cols[:, 3], ACT.Exp).then_inc(decay, 1)

                @block.vector
                def _(dve):
                    dve.memset(xT[:, :, 0:1], 0.0)
                    dve.memset(pp[:, :, 0:1], -1e30)
                    dve.memset(aa[:, :, 0:1], 0.0)
                    dve.memset(bb[:, :, 0:1], 0.0)
                    dve.wait_ge(decay, 1)
                    dve.tensor_scalar(cols[:, 3], cols[:, 3], -1.0, None, ALU.mult)
            u.round_end()
        (vchain, xn_ready, xT_psum, xT_ready, mix_ready, p_psum, p_used, exp_arg, exp_done, y_ready, out_psum, x2_ready,
         ei_ready, eT_psum, eT_ready, lg_psum, pool_ready, e_stored) = (
             s.sem("tm_" + n) for n in (
                 "vchain xn_ready xT_psum xT_ready mix_ready p_psum p_used exp_arg exp_done y_ready out_psum x2_ready "
                 "ei_ready eT_psum eT_ready lg_psum pool_ready e_stored").split())
        ps = g.ps
        two = [ps[:, 2 * i:2 * i + 2, :].rearrange("p k n -> p (k n)") for i in range(4)]
        proj = [(w, f) for w in range(3) for f in range(2)]
        pair = [2, 3, 0, 1, 2, 3]
        prev, cur = slice(0, SEQ), slice(1, SEQ + 1)
        with nc.Fori(0, NB) as b:
            hb = g.h[:, :, bass.ds(b, 1)].rearrange("p c o n -> p c (o n)")
            with nc.Block() as block:
                @block.tensor
                def _(pe):
                    pe.wait_ge(xn_ready, 1)
                    for d in range(DC):
                        for c in range(NC):
                            mm = pe.transpose(two[d][:, c * P:(c + 1) * P], xn[:, c, d * P:(d + 1) * P], g.ident[:])
                    mm.then_inc(xT_psum, 1)
                    for i, (w, f) in enumerate(proj):
                        if f == 0:
                            pe.wait_ge(mix_ready, w + 1)
                        if i == 2:
                            pe.wait_ge(xT_ready, 1)
                        if i >= 4:
                            pe.wait_ge(p_used, i - 3)
                        for lo, hi in ((0, 512), (512, SEQ)):
                            for d in range(DC):
                                mm = pe.matmul(two[pair[i]][:, lo:hi], wk[:, w, d, f * P:(f + 1) * P],
                                               mix[:, w, d, lo:hi], start=(d == 0), stop=(d == DC - 1))
                        mm.then_inc(p_psum, 1)
                    pe.wait_ge(y_ready, 1)
                    for c in range(NC):
                        for f in range(2):
                            mm = pe.matmul(ps[:, c // 2, (c % 2) * D:(c % 2 + 1) * D], rr[:, f, c * P:(c + 1) * P],
                                           wo[:, f, :], start=(f == 0), stop=(f == 1))
                        if c % 2:
                            mm.then_inc(out_psum, 1)
                    pe.wait_ge(ei_ready, 1)
                    for d in range(DC):
                        for c in range(NC):
                            mm = pe.transpose(two[2 + d][:, c * P:(c + 1) * P], xn[:, c, d * P:(d + 1) * P], g.ident[:])
                    mm.then_inc(eT_psum, 1)
                    pe.wait_ge(eT_ready, 1)
                    for c in range(NC):
                        for d in range(DC):
                            mm = pe.matmul(ps[:, 3, c * NE:(c + 1) * NE], xT[:, d, 1 + c * P:1 + (c + 1) * P], rw[:, d, :],
                                           start=(d == 0), stop=(d == DC - 1))
                    mm.then_inc(lg_psum, 1)

                @block.scalar
                def _(act):
                    act.wait_ge(xT_psum, 1)
                    act.activation(xT[:, 0, cur], two[0][:, 0:SEQ], ACT.Copy)
                    act.activation(xT[:, 1, cur], two[1][:, 0:SEQ], ACT.Copy).then_inc(xT_ready, 1)
                    for i, (w, f) in enumerate(proj):
                        act.wait_ge(p_psum, i + 1)
                        src, dst = two[pair[i]][:, 0:SEQ], (kk, vv, rr)[w][:, f, :]
                        if w < 2:
                            act.activation(dst, src, ACT.Copy).then_inc(p_used, 1)
                        else:
                            act.activation(dst, src, ACT.Sigmoid).then_inc(p_used, 1)
                    for i in range(2):
                        act.wait_ge(exp_arg, i + 1)
                        act.activation(t[:, 2 * i:2 * i + 2], t[:, 2 * i:2 * i + 2], ACT.Exp).then_inc(exp_done, 1)
                    act.wait_ge(eT_psum, 1)
                    act.activation(xT[:, 0, cur], two[2][:, 0:SEQ], ACT.Copy)
                    act.activation(xT[:, 1, cur], two[3][:, 0:SEQ], ACT.Copy).then_inc(eT_ready, 1)

                @block.gpsimd
                def _(pool):
                    pool.wait_ge(x2_ready, 1)
                    pool.tensor_tensor(hb, hb, hn[:], ALU.add).then_inc(pool_ready, 1)

                @block.sync
                def _(sp):
                    sp.wait_ge(ei_ready, 1)
                    dst = g.scr_e[bass.ds(b, 1), 1:SEQ + 1].rearrange("o (c p) n -> p (o c) n", p=P)
                    sp.dma_start(dst, xn[:]).then_inc(e_stored, 16)
                    sp.wait_ge(e_stored, 16)

                @block.vector
                def _(dve):
                    link = chain(dve, vchain)
                    tiles = [hb[:, c, :] for c in range(NC)]
                    hns, xns = [hn[:, c, :] for c in range(NC)], [xn[:, c, :] for c in range(NC)]
                    row = [bc(rows[:, i * D:(i + 1) * D].unsqueeze(1), [P, NC, D]) for i in range(4)]
                    layernorm(dve, link, tiles, hns, stats, mv, rs, ltmp)
                    layernorm(dve, link, hns, xns, stats, mv, rs, ltmp)
                    link(dve.tensor_tensor(xn[:], xn[:], row[0], ALU.mult))
                    dve.tensor_tensor(xn[:], xn[:], row[1], ALU.add).then_inc(xn_ready, 1)
                    dve.wait_ge(xT_ready, 1)
                    link(dve.tensor_tensor(dT[:], xT[:, :, cur], xT[:, :, prev], ALU.subtract))
                    for w in range(3):
                        for d in range(DC):
                            op = dve.scalar_tensor_tensor(mix[:, w, d, :], dT[:, d, :], cols[:, w, d:d + 1], xT[:, d, prev],
                                                          ALU.mult, ALU.add)
                        op.then_inc(mix_ready, 1)
                    dve.wait_ge(p_used, 2)
                    for f in range(2):
                        op = dve.tensor_tensor_scan(pp[:, f, cur], bc(cols[:, 3, f:f + 1], [P, SEQ]), kk[:, f, :], -1e30,
                                                    ALU.add, ALU.max)
                    link(op)
                    for f in range(2):
                        dve.tensor_scalar(t[:, 0, f, :], pp[:, f, prev], cols[:, 3, f:f + 1], None, ALU.add)
                        op = dve.tensor_scalar(t[:, 3, f, :], kk[:, f, :], cols[:, 4, f:f + 1], None, ALU.add)
                    link(op)
                    dve.tensor_tensor(t[:, 0], t[:, 0], pp[:, :, cur], ALU.subtract)
                    dve.tensor_tensor(t[:, 1], kk[:], pp[:, :, cur], ALU.subtract).then_inc(exp_arg, 1)
                    link(dve.tensor_tensor(t[:, 2], t[:, 3], pp[:, :, prev], ALU.max))
                    link(dve.tensor_tensor(t[:, 3], t[:, 3], t[:, 2], ALU.subtract))
                    dve.tensor_tensor(t[:, 2], pp[:, :, prev], t[:, 2], ALU.subtract).then_inc(exp_arg, 1)
                    dve.wait_ge(exp_done, 1)
                    dve.wait_ge(p_used, 4)
                    link(dve.tensor_tensor(kk[:], t[:, 1], vv[:], ALU.mult))
                    for f in range(2):
                        dve.tensor_tensor_scan(aa[:, f, cur], t[:, 0, f, :], kk[:, f, :], 0.0, ALU.mult, ALU.add)
                        op = dve.tensor_tensor_scan(bb[:, f, cur], t[:, 0, f, :], t[:, 1, f, :], 0.0, ALU.mult, ALU.add)
                    link(op)
                    dve.wait_ge(exp_done, 2)
                    dve.wait_ge(p_used, 6)
                    dve.tensor_tensor(t[:, 0], t[:, 2], aa[:, :, prev], ALU.mult)
                    dve.tensor_tensor(vv[:], t[:, 3], vv[:], ALU.mult)
                    link(dve.tensor_tensor(t[:, 1], t[:, 2], bb[:, :, prev], ALU.mult))
                    dve.tensor_tensor(t[:, 0], t[:, 0], vv[:], ALU.add)
                    link(dve.tensor_tensor(t[:, 1], t[:, 1], t[:, 3], ALU.add))
                    dve.tensor_tensor(rr[:], rr[:], t[:, 0], ALU.mult)
                    link(dve.reciprocal(t[:, 1], t[:, 1]))
                    dve.tensor_tensor(rr[:], rr[:], t[:, 1], ALU.mult).then_inc(y_ready, 1)
                    for m in range(NC // 2):
                        dve.wait_ge(out_psum, m + 1)
                        op = dve.tensor_tensor(hn[:, 2 * m:2 * m + 2], hn[:, 2 * m:2 * m + 2],
                                               ps[:, m, :].rearrange("p (c n) -> p c n", c=2), ALU.add)
                    op.then_inc(x2_ready, 1)
                    dve.wait_ge(x2_ready, 1)
                    layernorm(dve, link, hns, xns, stats, mv, rs, ltmp)
                    link(dve.tensor_tensor(xn[:], xn[:], row[2], ALU.mult))
                    dve.tensor_tensor(xn[:], xn[:], row[3], ALU.add).then_inc(ei_ready, 1)
                    dve.wait_ge(lg_psum, 1)
                    dve.tensor_copy(g.gates1[:, :, bass.ds(b, 1), :].rearrange("p c o e -> p c (o e)"),
                                    ps[:, 3, 0:NC * NE].rearrange("p (c e) -> p c e", c=NC))
            s.round_end()


def top2_of_softmax(nc, g):
    NE, NTT = 8, NC * NB
    with Scope(nc) as s:
        pr, eq, cum = (s.sb("to_" + n, [P, NTT, NE]) for n in ("pr", "eq", "cum"))
        v8, cnt, ones = s.sb("to_v8", [P, NTT, 8]), s.sb("to_cnt", [P, NTT]), s.sb("to_ones", [P, 32])
        vchain, shifted, sm_done = s.sem("to_vchain"), s.sem("to_shifted"), s.sem("to_exp")
        lg, sel = g.gates1[:].rearrange("p c b e -> p (c b) e"), g.sel1[:].rearrange("p c b e -> p (c b) e")
        with nc.Block() as block:
            @block.scalar
            def _(act):
                act.wait_ge(shifted, 1)
                act.activation(pr[:], lg, ACT.Exp).then_inc(sm_done, 1)

            @block.vector
            def _(dve):
                link = chain(dve, vchain)

                def normalise(dst, src):
                    link(dve.tensor_reduce(cnt[:], src, AX_X, ALU.add))
                    link(dve.reciprocal(cnt[:], cnt[:]))
                    link(dve.tensor_tensor(dst, src, bc(cnt[:].unsqueeze(2), [P, NTT, NE]), ALU.mult))
                dve.memset(ones[:], 1.0)
                link(dve.tensor_reduce(cnt[:], lg, AX_X, ALU.max))
                dve.tensor_tensor(lg, lg, bc(cnt[:].unsqueeze(2), [P, NTT, NE]), ALU.subtract).then_inc(shifted, 1)
                dve.wait_ge(sm_done, 1)
                normalise(pr[:], pr[:])
                pick_top(dve, link, pr[:], 2, v8[:], sel, eq[:], cum[:], cnt[:], ones[:])
                link(dve.tensor_tensor(lg, pr[:], sel, ALU.mult))
                normalise(lg, lg)
        s.round_end()


def route_groups(nc, g):
    NE, NGR = 32, 8
    with Scope(nc) as s:
        gw, bias = s.sb("rg_gw", [P, DC, NE]), s.sb("rg_bias", [P, NE])
        nx, nT, nTm = s.sb("rg_nx", [P, NB, D]), s.sb("rg_nT", [P, DC, NB * P]), s.sb("rg_nT_cut", [P, DC, NB * P])
        score_all = s.sb("rg_scores", [P, NC, NB, NE])
        stats, mv, rs, ltmp = s.sb("rg_stats", [P, NB, 6]), s.sb("rg_mv", [P, NB, 2]), s.sb("rg_rs", [P, NB]), s.sb("rg_ltmp", [P, 2, NB])
        def norm(dve, link, hc):
            layernorm(dve, link, [hc[:, b, :] for b in range(NB)], [nx[:, b, :] for b in range(NB)], stats, mv, rs, ltmp)

        with Scope(nc) as u:
            loaded, first_chain = u.sem("rg_loaded"), u.sem("rg_first_chain")
            with nc.Block() as block:
                @block.sync
                def _(sp):
                    sp.dma_start(gw[:], g.d["m2_gate"]).then_inc(loaded, 16)
                    sp.dma_start(bias[:], g.d["m2_bias"]).then_inc(loaded, 16)
                    sp.wait_ge(loaded, 32)

                @block.vector
                def _(dve):
                    dve.memset(g.comb[:], 1.0)
                    dve.memset(g.h_spare[:, NC + 1], 0.0)
                    norm(dve, chain(dve, first_chain), g.h[:, 0])
            u.round_end()
        vchain, nT_psum, nT_ready, cut_ready, lg_psum, e_ready, high_ready, low_ready = (s.sem("rg_" + n) for n in (
            "vchain nT_psum nT_ready cut_ready lg_psum e_ready high_ready low_ready").split())
        ps = g.ps
        with nc.Fori(0, NC) as c:
            h_next = g.h_spare[:, bass.ds(c + 2, 1)].rearrange("p o b n -> p (o b) n")
            with nc.Block() as block:
                @block.tensor
                def _(pe):
                    for d in range(DC):
                        for b in range(NB):
                            mm = pe.transpose(ps[:, d, b * P:(b + 1) * P], nx[:, b, d * P:(d + 1) * P], g.ident[:])
                    mm.then_inc(nT_psum, 1)
                    pe.wait_ge(nT_ready, 1)
                    for b in range(NB):
                        for d in range(DC):
                            mm = pe.matmul(ps[:, 2, b * NE:(b + 1) * NE], nT[:, d, b * P:(b + 1) * P], gw[:, d, :],
                                           start=(d == 0), stop=(d == DC - 1))
                    mm.then_inc(lg_psum, 1)

                @block.scalar
                def _(act):
                    act.wait_ge(nT_psum, 1)
                    act.activation(nT[:, 0, :], ps[:, 0, :], ACT.Copy)
                    act.activation(nT[:, 1, :], ps[:, 1, :], ACT.Copy).then_inc(nT_ready, 1)
                    act.wait_ge(lg_psum, 1)
                    act.activation(score_all[:, bass.ds(c, 1)].rearrange("p o b e -> p (o b e)"), ps[:, 2, 0:NB * NE], ACT.Exp,
                                   scale=-1.0).then_inc(e_ready, 1)
                    act.wait_ge(cut_ready, 1)
                    act.activation(g.xh[:, :, bass.ds(c, 1), :].rearrange("p d o n -> p d (o n)"), nTm[:], ACT.Copy
                                   ).then_inc(high_ready, 1)

                @block.gpsimd
                def _(pool):
                    pool.wait_ge(cut_ready, 1)
                    pool.tensor_tensor(g.xl[:, :, bass.ds(c, 1), :].rearrange("p d o n -> p d (o n)"), nT[:], nTm[:],
                                       ALU.subtract).then_inc(low_ready, 1)

                @block.vector
                def _(dve):
                    link = chain(dve, vchain)
                    dve.wait_ge(nT_ready, 1)
                    cut(dve, nTm[:].rearrange("p d n -> p (d n)"), nT[:].rearrange("p d n -> p (d n)")).then_inc(cut_ready, 1)
                    norm(dve, link, h_next)
            s.round_end()
        with Scope(nc) as v:
            NTT = NC * NB
            score = score_all[:].rearrange("p c b e -> p (c b) e")
            sc, sel, eq, cum, comb = (v.sb("rg_" + n, [P, NTT, NE]) for n in ("sc", "sel", "eq", "cum", "comb"))
            pairs = v.sb("rg_pairs", [P, NTT, NGR, 6])
            gs, gsel, geq, gcum = (v.sb("rg_" + n, [P, NTT, NGR]) for n in ("gs", "gsel", "geq", "gcum"))
            v8, cnt, ones = v.sb("rg_v8", [P, NTT, 8]), v.sb("rg_cnt", [P, NTT]), v.sb("rg_ones", [P, 32])
            gchain = v.sem("rg_gchain")
            with nc.Block() as block:
                @block.vector
                def _(dve):
                    link = chain(dve, gchain)
                    dve.memset(ones[:], 1.0)
                    link(dve.tensor_scalar(score, score, 1.0, None, ALU.add))
                    link(dve.reciprocal(score, score))
                    link(dve.tensor_tensor(sc[:], score, bc(bias[:].unsqueeze(1), [P, NTT, NE]), ALU.add))
                    q = sc[:].rearrange("p b (g k) -> p b g k", g=NGR)
                    for b in range(NTT):
                        dve.tensor_tensor(pairs[:, b, :, 0:3], q[:, b, :, 0:3], q[:, b, :, 1:4], ALU.add)
                        dve.tensor_tensor(pairs[:, b, :, 3:5], q[:, b, :, 0:2], q[:, b, :, 2:4], ALU.add)
                    link(dve.tensor_tensor(pairs[:, :, :, 5], q[:, :, :, 0], q[:, :, :, 3], ALU.add))
                    link(dve.tensor_reduce(gs[:], pairs[:], AX_X, ALU.max))
                    pick_top(dve, link, gs[:], 4, v8[:], gsel[:], geq[:], gcum[:], cnt[:], ones[:])
                    link(dve.tensor_tensor(q, q, bc(gsel[:].unsqueeze(3), [P, NTT, NGR, 4]), ALU.mult))
                    pick_top(dve, link, sc[:], 8, v8[:], sel[:], eq[:], cum[:], cnt[:], ones[:])
                    link(dve.tensor_tensor(comb[:], sel[:], score, ALU.mult))
                    link(dve.tensor_reduce(cnt[:], comb[:], AX_X, ALU.add))
                    link(dve.tensor_scalar(cnt[:], cnt[:], 1e-20, None, ALU.add))
                    link(dve.reciprocal(cnt[:], cnt[:]))
                    link(dve.tensor_scalar(cnt[:], cnt[:], 2.5, None, ALU.mult))
                    dve.tensor_tensor(g.comb[:].rearrange("p c b e -> p (c b) e")[:, :, 0:NE], comb[:],
                                      bc(cnt[:].unsqueeze(2), [P, NTT, NE]), ALU.mult)
            v.round_end()


def moe_silu(nc, g, first, count, per):
    with Scope(nc) as s:
        tag = f"ms{first}_"
        W = 3 * 2 * P
        w, wm = s.sb(tag + "w", [P, per, W]), s.sb(tag + "w_cut", [P, W])
        wh, wl = s.sb(tag + "w_high", [P, 2, W], F32R), s.sb(tag + "w_low", [P, 2, W], F32R)
        act_g, hid, hm = s.sb(tag + "silu", [P, 2, 512]), s.sb(tag + "hid", [P, 2, 512]), s.sb(tag + "hid_cut", [P, 2, 512])
        hh, hl = s.sb(tag + "hid_high", [P, 3, 512], F32R), s.sb(tag + "hid_low", [P, 3, 512], F32R)
        cw = s.sb(tag + "comb", [P, per, NC, NB])

        def load(sp, slot, e, sem):
            sp.dma_start(w[:, slot], g.d["m2_w"][bass.ds(e, 1)].rearrange("o p n -> p (o n)")).then_inc(sem, 16)
        with Scope(nc) as u:
            loaded, w_cut, w_high, w_low = (u.sem(tag + "first_" + n) for n in "loaded w_cut w_high w_low".split())
            with nc.Block() as block:
                @block.sync
                def _(sp):
                    for i in range(per):
                        load(sp, i, first + i, loaded)
                    sp.wait_ge(loaded, 16 * per)

                @block.vector
                def _(dve):
                    dve.wait_ge(loaded, 16 * per)
                    cut(dve, wm[:], w[:, 0]).then_inc(w_cut, 1)

                @block.scalar
                def _(act):
                    act.wait_ge(w_cut, 1)
                    act.activation(wh[:, 0], wm[:], ACT.Copy).then_inc(w_high, 1)

                @block.gpsimd
                def _(pool):
                    pool.wait_ge(w_cut, 1)
                    pool.tensor_tensor(wl[:, 0], w[:, 0], wm[:], ALU.subtract).then_inc(w_low, 1)
            u.round_end()
        (loaded, loaded0, cw_ready, w_cut, w_high, w_low, gu_psum, s_ready, hid_ready, cut_ready, high_ready, low_ready, y_psum,
         y_used) = (s.sem(tag + n) for n in ("next_loaded next_loaded0 cw_ready w_cut w_high w_low gu_psum s_ready hid_ready "
                                             "cut_ready high_ready low_ready y_psum y_used").split())
        ps = g.ps
        NR = per * NC
        more = count > per
        LAG = 2

        def split_at(n, c):
            slot = n // NC + 1
            return slot if n % NC == c and (slot < per or more) else None
        with nc.Fori(0, count // per) as r:
            e = r * per + first
            with nc.Block() as block:
                @block.sync
                def _(sp):
                    if more:
                        for i in range(per):
                            if i:
                                sp.wait_ge(w_low, i)
                                sp.wait_ge(w_cut, i)
                            load(sp, i, e + per + i, loaded if i else loaded0)
                        sp.wait_ge(loaded0, 16)
                        sp.wait_ge(loaded, 16 * (per - 1))

                @block.tensor
                def _(pe):
                    def three(out, ah, al, bh, bl, first, last):
                        pe.matmul(out, ah, bh, start=first, stop=False)
                        pe.matmul(out, al, bh, start=False, stop=False)
                        return pe.matmul(out, ah, bl, start=False, stop=last)
                    for n in range(NR + LAG):
                        if n < NR:
                            slot, c = divmod(n, NC)
                            if n >= 2:
                                pe.wait_ge(hid_ready, n - 1)
                            if c == 0 and slot:
                                pe.wait_ge(w_high, slot)
                                pe.wait_ge(w_low, slot)
                            for k in range(2):
                                for d in range(DC):
                                    at = slice((2 * k + d) * P, (2 * k + d + 1) * P)
                                    mm = three(ps[:, 2 * k + n % 2, :], wh[:, slot % 2, at], wl[:, slot % 2, at],
                                               g.xh[:, d, c, :], g.xl[:, d, c, :], d == 0, d == DC - 1)
                                mm.then_inc(gu_psum, 1)
                        if n >= LAG:
                            m = n - LAG
                            slot = m // NC % 2
                            pe.wait_ge(high_ready, m + 1)
                            pe.wait_ge(low_ready, m + 1)
                            at = slice(4 * P, 4 * P + D)
                            for b in range(NB):
                                k = m * NB + b
                                if k >= 4:
                                    pe.wait_ge(y_used, k - 3)
                                t = slice(b * P, (b + 1) * P)
                                three(ps[:, 4 + k % 4, 0:D], hh[:, m % 3, t], hl[:, m % 3, t], wh[:, slot, at], wl[:, slot, at],
                                      True, True).then_inc(y_psum, 1)

                @block.scalar
                def _(act):
                    for n in range(NR):
                        act.wait_ge(gu_psum, 2 * n + 1)
                        if n >= 2:
                            act.wait_ge(hid_ready, n - 1)
                        act.activation(act_g[:, n % 2, :], ps[:, n % 2, :], ACT.Silu).then_inc(s_ready, 1)
                        act.wait_ge(cut_ready, n + 1)
                        if n >= 3:
                            act.wait_ge(y_psum, NB * (n - 2))
                        act.activation(hh[:, n % 3, :], hm[:, n % 2, :], ACT.Copy).then_inc(high_ready, 1)
                        slot = split_at(n, 2)
                        if slot is not None:
                            act.wait_ge(w_cut, slot)
                            if slot >= 2:
                                act.wait_ge(y_psum, NB * NC * (slot - 1))
                            act.activation(wh[:, slot % 2], wm[:], ACT.Copy).then_inc(w_high, 1)

                @block.gpsimd
                def _(pool):
                    for n in range(NR):
                        pool.wait_ge(cut_ready, n + 1)
                        if n >= 3:
                            pool.wait_ge(y_psum, NB * (n - 2))
                        pool.tensor_tensor(hl[:, n % 3, :], hid[:, n % 2, :], hm[:, n % 2, :], ALU.subtract).then_inc(low_ready, 1)
                        slot = split_at(n, 2)
                        if slot is not None:
                            pool.wait_ge(w_cut, slot)
                            if slot >= 2:
                                pool.wait_ge(y_psum, NB * NC * (slot - 1))
                            pool.tensor_tensor(wl[:, slot % 2], w[:, slot % per], wm[:], ALU.subtract).then_inc(w_low, 1)

                @block.vector
                def _(dve):
                    for k in range(per):
                        op = dve.tensor_copy(cw[:, k], g.comb[:, :, :, bass.ds(e + k, 1)].rearrange("p c b o -> p c (b o)"))
                    op.then_inc(cw_ready, 1)
                    dve.wait_ge(cw_ready, 1)
                    for n in range(NR + LAG):
                        if n < NR:
                            dve.wait_ge(s_ready, n + 1)
                            dve.wait_ge(gu_psum, 2 * n + 2)
                            if n >= 2:
                                dve.wait_ge(low_ready, n - 1)
                                dve.wait_ge(high_ready, n - 1)
                            dve.tensor_tensor(hid[:, n % 2, :], act_g[:, n % 2, :], ps[:, 2 + n % 2, :], ALU.mult
                                              ).then_inc(hid_ready, 1)
                            dve.wait_ge(hid_ready, n + 1)
                            cut(dve, hm[:, n % 2, :], hid[:, n % 2, :]).then_inc(cut_ready, 1)
                            slot = split_at(n, 1)
                            if slot is not None:
                                if slot >= 2:
                                    dve.wait_ge(w_high, slot - 1)
                                    dve.wait_ge(w_low, slot - 1)
                                if slot == per:
                                    dve.wait_ge(loaded0, 16)
                                cut(dve, wm[:], w[:, slot % per]).then_inc(w_cut, 1)
                        if n >= LAG:
                            m = n - LAG
                            slot, c = divmod(m, NC)
                            if m >= NC:
                                dve.wait_ge(y_used, NB * (m + 1 - NC))
                            for b in range(NB):
                                k = m * NB + b
                                dve.wait_ge(y_psum, k + 1)
                                dve.scalar_tensor_tensor(g.h[:, c, b, :], ps[:, 4 + k % 4, 0:D], cw[:, slot, c, b:b + 1],
                                                         g.h[:, c, b, :], ALU.mult, ALU.add).then_inc(y_used, 1)
            s.round_end()


def layer1_ffn(nc, g):
    with Scope(nc) as s:
        g.xh, g.xl = s.sb("l1_x_high", [P, DC, NC, NB * P], F32R), s.sb("l1_x_low", [P, DC, NC, NB * P], F32R)
        g.comb = s.sb("l1_comb", [P, NC, NB, 34])
        route_groups(nc, g)
        moe_silu(nc, g, 0, 32, 8)
        moe_silu(nc, g, 32, 2, 2)


NE = 8
TS = 256
NT = NC * NB * P * 2 // TS + NE
TPR, AHEAD = 8, 4


def top2_slots(nc, g, tag, sel, gates, rows, src, width, ld):
    NTT = NC * NB
    with Scope(nc, tag) as s:
        tri = s.sb("ts_tri", [P, 2 * P])
        iota = s.sb("ts_iota", [P, NT // 2 + NT + AHEAD])
        ones = s.sb("ts_ones", [P, NTT])
        rank, m1, m2 = (s.sb("ts_" + n, [P, NTT, NE]) for n in ("rank", "m1", "m2"))
        cnt, incl = s.sb("ts_cnt", [P, NE, NTT]), s.sb("ts_incl", [P, NE, NTT])
        NJ = NTT * P // TS
        cmp_n, cmp_t = s.sb("ts_cmp_n", [P, NE, NJ]), s.sb("ts_cmp_t", [P, NT + AHEAD, NE])
        tiles, cumt, base = (s.sb("ts_" + n, [P, NE]) for n in ("tiles", "cumt", "base"))
        pf, te = s.sb("ts_posf", [P, 2, NTT]), s.sb("ts_tile_e", [P, NT + AHEAD])
        consts_loaded, loaded, counted, vchain, placed, scattered = (
            s.sem("ts_" + n) for n in "consts_loaded loaded counted vchain placed scattered".split())
        ps = g.ps
        sv, gv = (t.rearrange("p c b e -> p (c b) e") for t in (sel, gates))
        with nc.Block() as block:
            @block.sync
            def _(sp):
                sp.dma_start(tri[:], g.d["ts_tri"]).then_inc(consts_loaded, 16)
                sp.dma_start(iota[:], g.d["ts_iota"]).then_inc(consts_loaded, 16)
                for dst, from_dram in src:
                    sp.dma_start(dst, from_dram).then_inc(loaded, 16)
                sp.wait_ge(placed, 1)
                for i in range(AHEAD):
                    ld.weights_of(sp, g.tile_e, i, i)

            @block.tensor
            def _(pe):
                pe.wait_ge(consts_loaded, 32)
                for k in range(2):
                    mm = pe.matmul(ps[:, k, 0:NTT * NE], tri[:, k * P:(k + 1) * P], sv.rearrange("p t e -> p (t e)"),
                                   start=True, stop=True)
                mm.then_inc(counted, 1)

            @block.vector
            def _(dve):
                link = chain(dve, vchain)
                dve.memset(ones[:], 1.0)
                dve.wait_ge(counted, 1)
                dve.tensor_copy(rank[:].rearrange("p t e -> p (t e)"), ps[:, 0, 0:NTT * NE])
                link(dve.tensor_copy(cnt[:], ps[:, 1, 0:NTT * NE].rearrange("p (t e) -> p e t", e=NE)))
                for e in range(NE):
                    op = dve.tensor_tensor_scan(incl[:, e, :], ones[:], cnt[:, e, :], 0.0, ALU.mult, ALU.add)
                link(op)
                dve.tensor_tensor(cnt[:], incl[:], cnt[:], ALU.subtract)
                link(dve.tensor_tensor(cmp_n[:], bc(incl[:, :, NTT - 1:NTT], [P, NE, NJ]),
                                       bc(iota[:, 0:NJ].unsqueeze(1), [P, NE, NJ]), ALU.is_gt))
                link(dve.tensor_reduce(tiles[:], cmp_n[:], AX_X, ALU.add))
                link(dve.tensor_tensor_scan(cumt[:], ones[:, 0:NE], tiles[:], 0.0, ALU.mult, ALU.add))
                dve.tensor_tensor(cmp_t[:], bc(iota[:, NT // 2:].unsqueeze(2), [P, NT + AHEAD, NE]),
                                  bc(cumt[:].unsqueeze(1), [P, NT + AHEAD, NE]), ALU.is_ge)
                link(dve.tensor_tensor(base[:], cumt[:], tiles[:], ALU.subtract))
                dve.tensor_reduce(te[:], cmp_t[:], AX_X, ALU.add)
                link(dve.tensor_scalar(base[:], base[:], float(TS), None, ALU.mult))
                dve.tensor_scalar(te[:], te[:], float(NE - 1), None, ALU.min)
                link(dve.tensor_tensor(cnt[:], cnt[:], bc(base[:].unsqueeze(2), [P, NE, NTT]), ALU.add))
                dve.tensor_copy(g.tile_e[:], te[:])
                link(dve.tensor_tensor(rank[:], rank[:], cnt[:].rearrange("p e t -> p t e"), ALU.add))
                link(dve.tensor_tensor(rank[:], rank[:], sv, ALU.mult))
                dve.tensor_reduce(pf[:, 0], rank[:], AX_X, ALU.add)
                link(dve.tensor_reduce(pf[:, 1], rank[:], AX_X, ALU.max))
                link(dve.tensor_tensor(pf[:, 0], pf[:, 0], pf[:, 1], ALU.subtract))
                dve.tensor_copy(g.pos[:], pf[:]).then_inc(placed, 1)
                link(dve.tensor_tensor(m1[:], rank[:], bc(pf[:, 1].unsqueeze(2), [P, NTT, NE]), ALU.is_equal))
                dve.tensor_tensor(m2[:], sv, m1[:], ALU.subtract)
                link(dve.tensor_tensor(m1[:], m1[:], gv, ALU.mult))
                link(dve.tensor_tensor(m2[:], m2[:], gv, ALU.mult))
                dve.tensor_reduce(g.pw[:, 1], m1[:], AX_X, ALU.add)
                dve.tensor_reduce(g.pw[:, 0], m2[:], AX_X, ALU.add)

            @block.gpsimd
            def _(pool):
                if src:
                    pool.wait_ge(loaded, 16 * len(src))
                pool.wait_ge(placed, 1)
                to = g.slots[0:NT * TS * width].rearrange("(r n) -> r n", n=width)
                for t in range(NTT):
                    for k in range(2):
                        pool.indirect_dma_start(to, bass.IndirectOffsetOnAxis(g.pos[:, k, t:t + 1], axis=0), rows(t), None
                                                ).then_inc(scattered, 16)
                pool.wait_ge(scattered, 16 * 2 * NTT)
        s.round_end(swdge=True)


def top2_combine(nc, g, tag, ld):
    with Scope(nc, tag) as s:
        yg = s.sb("tc_y", [P, NC, NB, 2, D])
        gathered = [s.sem(f"tc_gathered{c}") for c in range(NC)]
        added = s.sem("tc_added")
        with nc.Block() as block:
            @block.sync
            def _(sp):
                ld.finish(sp)

            @block.gpsimd
            def _(pool):
                for c in range(NC):
                    for b in range(NB):
                        for k in range(2):
                            at = g.pos[:, k, c * NB + b:c * NB + b + 1]
                            pool.indirect_dma_start(yg[:, c, b, k], None, g.y_slots, bass.IndirectOffsetOnAxis(at, axis=0)
                                                    ).then_inc(gathered[c], 16)
                for c in range(NC):
                    pool.wait_ge(gathered[c], 16 * 2 * NB)

            @block.vector
            def _(dve):
                for c in range(NC):
                    dve.wait_ge(gathered[c], 16 * 2 * NB)
                    for k in range(2):
                        if k:
                            dve.wait_ge(added, NB * (2 * c + 1))
                        for b in range(NB):
                            t = c * NB + b
                            dve.scalar_tensor_tensor(g.h[:, c, b, :], yg[:, c, b, k], g.pw[:, k, t:t + 1], g.h[:, c, b, :],
                                                     ALU.mult, ALU.add).then_inc(added, 1)
        s.round_end(swdge=True)


class TileLoads:

    def __init__(self, g, s, tag, width, names):
        self.g, self.width, self.names = g, width, names
        self.w = [s.sb(f"{tag}w{k}", [P, AHEAD, g.d[n].shape[2]]) for k, n in enumerate(names)]
        self.x = s.sb(tag + "x", [P, TPR, 2, width])
        self.ids = s.sb(tag + "ids", [1, TPR + AHEAD], I32)
        self.w_loaded = [s.kept_sem(f"{tag}w_loaded{i}") for i in range(AHEAD)]
        self.x_loaded = [s.kept_sem(f"{tag}x_loaded{i}") for i in range(TPR)]

    def wait_cleared(self, eng, i, cleared):
        if i >= AHEAD:
            eng.wait_ge(cleared, i - AHEAD + 1)

    def wait_weights(self, eng, i):
        eng.wait_ge(self.w_loaded[i % AHEAD], 16 * len(self.names))

    def wait_rows(self, eng, i):
        eng.wait_ge(self.x_loaded[i], 16)

    def weights_of(self, sp, ids, at, i, cleared=None):
        sem = self.w_loaded[i % AHEAD]
        e = sp.value_load(ids[0:1, at:at + 1], min_val=0, max_val=NE - 1)
        sp.sem_clear(sem)
        if cleared is not None:
            sp.sem_inc(cleared, 1)
        for w, name in zip(self.w, self.names):
            sp.dma_start(w[:, i % AHEAD], self.g.d[name][bass.ds(e, 1)].rearrange("o p n -> p (o n)")).then_inc(sem, 16)

    def rows_of(self, sp, i, tile):
        src = self.g.slots.rearrange("(t h p n) -> t p h n", h=2, p=P, n=self.width)
        sp.sem_clear(self.x_loaded[i])
        sp.dma_start(self.x[:, i], src[bass.ds(tile, 1)].rearrange("o p h n -> p (o h) n")).then_inc(self.x_loaded[i], 16)

    def finish(self, sp):
        for i in range(AHEAD):
            self.wait_weights(sp, i)
            sp.sem_clear(self.w_loaded[i])
        for i in range(TPR):
            self.wait_rows(sp, i)
            sp.sem_clear(self.x_loaded[i])


def experts_gelu(nc, g, ld):
    F = 1024
    FC = F // P
    with Scope(nc) as s:
        wA, wB, x = ld.w[0], ld.w[1], ld.x
        xT = s.sb("eg_xT", [P, 2, DC, TS])
        hT = s.sb("eg_hT", [P, 2, FC, TS])
        y = s.sb("eg_y", [P, 2, 2, D])
        ids_ready, w_cleared, xT_psum, xT_ready, h_psum, h_ready, y_psum, y_ready = (
            s.sem("eg_" + n) for n in "ids_ready w_cleared xT_psum xT_ready h_psum h_ready y_psum y_ready".split())
        y_stored = [s.sem(f"eg_y_stored{i}") for i in range(2)]
        ps = g.ps
        with nc.Block() as block:
            @block.sync
            def _(sp):
                for i in range(TPR):
                    ld.rows_of(sp, i, i)
        s.round_end()
        with nc.Fori(0, NT // TPR) as r:
            tile0 = r * TPR
            with nc.Block() as block:
                @block.sync
                def _(sp):
                    sp.wait_ge(ids_ready, 1)
                    for i in range(TPR + 1):
                        if i < TPR:
                            sp.wait_ge(xT_psum, i + 1)
                            ld.rows_of(sp, i, tile0 + TPR + i)
                        if i >= 1:
                            sp.wait_ge(y_ready, 2 * i)
                            store_rows(sp, g, y[:, (i - 1) % 2], tile0 + i - 1, y_stored[(i - 1) % 2])
                            ld.weights_of(sp, ld.ids, i - 1 + AHEAD, i - 1, w_cleared)
                    for i in range(2):
                        sp.wait_ge(y_stored[i], 16 * (TPR // 2))

                @block.tensor
                def _(pe):
                    def transposes(i):
                        ld.wait_cleared(pe, i, w_cleared)
                        ld.wait_rows(pe, i)
                        if i >= 1:
                            pe.wait_ge(xT_ready, i)
                        for d in range(DC):
                            for h in range(2):
                                mm = pe.transpose(ps[:, 6, (d * 2 + h) * P:(d * 2 + h + 1) * P], x[:, i, h, d * P:(d + 1) * P],
                                                  g.ident[:])
                        mm.then_inc(xT_psum, 1)
                    transposes(0)
                    for i in range(TPR + 1):
                        if i < TPR:
                            ld.wait_weights(pe, i)
                            pe.wait_ge(xT_ready, i + 1)
                            for f in range(FC):
                                k = i * FC + f
                                if k >= 4:
                                    pe.wait_ge(h_ready, k - 3)
                                for d in range(DC):
                                    mm = pe.matmul(ps[:, k % 4, 0:TS], wA[:, i % AHEAD, d * F + f * P:d * F + (f + 1) * P],
                                                   xT[:, i % 2, d, :], start=(d == 0), stop=(d == DC - 1))
                                mm.then_inc(h_psum, 1)
                        if i + 1 < TPR:
                            transposes(i + 1)
                        if i >= 1:
                            pe.wait_ge(h_ready, FC * i)
                            for h in range(2):
                                k = (i - 1) * 2 + h
                                if k >= 2:
                                    pe.wait_ge(y_ready, k - 1)
                                for f in range(FC):
                                    mm = pe.matmul(ps[:, 4 + h, 0:D], hT[:, (i - 1) % 2, f, h * P:(h + 1) * P],
                                                   wB[:, (i - 1) % AHEAD, f * D:(f + 1) * D], start=(f == 0), stop=(f == FC - 1))
                                mm.then_inc(y_psum, 1)

                @block.scalar
                def _(act):
                    for i in range(TPR):
                        if i >= 2:
                            act.wait_ge(y_psum, 2 * (i - 1))
                        for f in range(FC):
                            act.wait_ge(h_psum, i * FC + f + 1)
                            act.activation(hT[:, i % 2, f, :], ps[:, (i * FC + f) % 4, 0:TS], ACT.Gelu,
                                           bias=wA[:, i % AHEAD, DC * F + f:DC * F + f + 1]).then_inc(h_ready, 1)

                @block.vector
                def _(dve):
                    dve.tensor_copy(ld.ids[:], g.tile_e[0:1, bass.ds(tile0, TPR + AHEAD)]).then_inc(ids_ready, 1)
                    def rows_to_sbuf(i):
                        dve.wait_ge(xT_psum, i + 1)
                        if i >= 2:
                            dve.wait_ge(h_psum, FC * (i - 1))
                        dve.tensor_copy(xT[:, i % 2].rearrange("p d n -> p (d n)"), ps[:, 6, :]).then_inc(xT_ready, 1)
                    rows_to_sbuf(0)
                    for i in range(TPR + 1):
                        if i + 1 < TPR:
                            rows_to_sbuf(i + 1)
                        if i >= 1:
                            if i >= 3:
                                dve.wait_ge(y_stored[(i - 1) % 2], 16 * ((i - 1) // 2))
                            for h in range(2):
                                dve.wait_ge(y_psum, 2 * (i - 1) + h + 1)
                                dve.tensor_copy(y[:, (i - 1) % 2, h], ps[:, 4 + h, 0:D]).then_inc(y_ready, 1)

            s.round_end()


def store_rows(eng, g, y, tile, sem):
    dst = g.y_slots.rearrange("(t h p) n -> t p h n", h=2, p=P)
    eng.dma_start(dst[bass.ds(tile, 1)].rearrange("o p h n -> p (o h) n"), y).then_inc(sem, 16)


def experts_channel_mix(nc, g, ld):
    F = 512
    FC = F // P
    with Scope(nc) as s:
        w, x = ld.w[0], ld.x
        eT, dT = s.sb("ec_eT", [P, DC, TS]), s.sb("ec_dT", [P, DC, TS])
        xk, xr = s.sb("ec_xk", [P, 2, DC, TS]), s.sb("ec_xr", [P, 2, DC, TS])
        rl, kk = s.sb("ec_relu", [P, 2, FC, TS]), s.sb("ec_k", [P, 2, FC, TS])
        sg, y = s.sb("ec_sigmoid", [P, 2, 2, D]), s.sb("ec_y", [P, 2, 2, D])
        at_k, at_v, at_r, at_mu = 0, DC * F, DC * F + FC * D, DC * F + FC * D + DC * D
        (ids_ready, w_cleared, xT_psum, eT_ready, dT_ready, x_ready, k_psum, relu_ready, kk_ready, r_psum, r_ready, kv_psum,
         y_ready) = (s.sem("ec_" + n) for n in ("ids_ready w_cleared xT_psum eT_ready dT_ready x_ready k_psum relu_ready "
                                                "kk_ready r_psum r_ready kv_psum y_ready").split())
        y_stored = [s.sem(f"ec_y_stored{i}") for i in range(2)]
        ps = g.ps
        with nc.Block() as block:
            @block.sync
            def _(sp):
                for i in range(TPR):
                    ld.rows_of(sp, i, i)
        s.round_end()
        with nc.Fori(0, NT // TPR) as r:
            tile0 = r * TPR
            with nc.Block() as block:
                @block.sync
                def _(sp):
                    sp.wait_ge(ids_ready, 1)
                    for i in range(TPR + 1):
                        if i < TPR:
                            sp.wait_ge(xT_psum, i + 1)
                            ld.rows_of(sp, i, tile0 + TPR + i)
                        if i >= 1:
                            sp.wait_ge(y_ready, 2 * i)
                            store_rows(sp, g, y[:, (i - 1) % 2], tile0 + i - 1, y_stored[(i - 1) % 2])
                            ld.weights_of(sp, ld.ids, i - 1 + AHEAD, i - 1, w_cleared)
                    for i in range(2):
                        sp.wait_ge(y_stored[i], 16 * (TPR // 2))

                @block.tensor
                def _(pe):
                    def transposes(i):
                        if i >= 1:
                            pe.wait_ge(eT_ready, i)
                            pe.wait_ge(dT_ready, i)
                        ld.wait_cleared(pe, i, w_cleared)
                        ld.wait_rows(pe, i)
                        for j in range(2):
                            for d in range(DC):
                                for h in range(2):
                                    mm = pe.transpose(ps[:, 6 + j, (d * 2 + h) * P:(d * 2 + h + 1) * P],
                                                      x[:, i, h, (j * DC + d) * P:(j * DC + d + 1) * P], g.ident[:])
                        mm.then_inc(xT_psum, 1)
                    transposes(0)
                    for i in range(TPR + 1):
                        if i < TPR:
                            ld.wait_weights(pe, i)
                            pe.wait_ge(x_ready, i + 1)
                            for f in range(FC):
                                k = i * FC + f
                                if k >= 2:
                                    pe.wait_ge(relu_ready, k - 1)
                                for d in range(DC):
                                    at = at_k + d * F + f * P
                                    mm = pe.matmul(ps[:, k % 2, 0:TS], w[:, i % AHEAD, at:at + P], xk[:, i % 2, d, :],
                                                   start=(d == 0), stop=(d == DC - 1))
                                mm.then_inc(k_psum, 1)
                            for h in range(2):
                                k = i * 2 + h
                                if k >= 2:
                                    pe.wait_ge(r_ready, k - 1)
                                for d in range(DC):
                                    mm = pe.matmul(ps[:, 2 + h, 0:D], xr[:, i % 2, d, h * P:(h + 1) * P],
                                                   w[:, i % AHEAD, at_r + d * D:at_r + (d + 1) * D],
                                                   start=(d == 0), stop=(d == DC - 1))
                                mm.then_inc(r_psum, 1)
                        if i + 1 < TPR:
                            transposes(i + 1)
                        if i >= 1:
                            pe.wait_ge(kk_ready, i)
                            for h in range(2):
                                k = (i - 1) * 2 + h
                                if k >= 2:
                                    pe.wait_ge(y_ready, k - 1)
                                for f in range(FC):
                                    mm = pe.matmul(ps[:, 4 + h, 0:D], kk[:, (i - 1) % 2, f, h * P:(h + 1) * P],
                                                   w[:, (i - 1) % AHEAD, at_v + f * D:at_v + (f + 1) * D],
                                                   start=(f == 0), stop=(f == FC - 1))
                                mm.then_inc(kv_psum, 1)

                @block.scalar
                def _(act):
                    def copy_before(i):
                        act.wait_ge(xT_psum, i + 1)
                        if i >= 1:
                            act.wait_ge(x_ready, i)
                        act.activation(eT[:].rearrange("p d n -> p (d n)"), ps[:, 6, :], ACT.Copy).then_inc(eT_ready, 1)
                    copy_before(0)
                    for i in range(TPR):
                        if i >= 2:
                            act.wait_ge(kk_ready, i - 1)
                        for f in range(FC):
                            k = i * FC + f
                            act.wait_ge(k_psum, k + 1)
                            act.activation(rl[:, i % 2, f, :], ps[:, k % 2, 0:TS], ACT.Relu).then_inc(relu_ready, 1)
                        if i >= 2:
                            act.wait_ge(y_ready, 2 * (i - 1))
                        for h in range(2):
                            act.wait_ge(r_psum, 2 * i + h + 1)
                            act.activation(sg[:, i % 2, h, :], ps[:, 2 + h, 0:D], ACT.Sigmoid).then_inc(r_ready, 1)
                        if i + 1 < TPR:
                            copy_before(i + 1)

                @block.vector
                def _(dve):
                    dve.tensor_copy(ld.ids[:], g.tile_e[0:1, bass.ds(tile0, TPR + AHEAD)]).then_inc(ids_ready, 1)
                    def mixes(i):
                        ld.wait_cleared(dve, i, w_cleared)
                        dve.wait_ge(eT_ready, i + 1)
                        if i >= 1:
                            dve.wait_ge(x_ready, i)
                        dve.tensor_tensor(dT[:].rearrange("p d n -> p (d n)"), ps[:, 7, :],
                                          eT[:].rearrange("p d n -> p (d n)"), ALU.subtract).then_inc(dT_ready, 1)
                        dve.wait_ge(dT_ready, i + 1)
                        if i >= 2:
                            dve.wait_ge(r_psum, 2 * (i - 1))
                        ld.wait_weights(dve, i)
                        for m, dst in ((0, xk), (1, xr)):
                            for d in range(DC):
                                mu = at_mu + m * DC + d
                                op = dve.scalar_tensor_tensor(dst[:, i % 2, d, :], dT[:, d, :], w[:, i % AHEAD, mu:mu + 1],
                                                              eT[:, d, :], ALU.mult, ALU.add)
                        op.then_inc(x_ready, 1)
                    mixes(0)
                    for i in range(TPR + 1):
                        if i + 1 < TPR:
                            mixes(i + 1)
                        if i >= 1:
                            if i >= 3:
                                dve.wait_ge(y_stored[(i - 1) % 2], 16 * ((i - 1) // 2))
                            dve.wait_ge(r_ready, 2 * i)
                            for h in range(2):
                                dve.wait_ge(kv_psum, 2 * (i - 1) + h + 1)
                                dve.tensor_tensor(y[:, (i - 1) % 2, h], sg[:, (i - 1) % 2, h], ps[:, 4 + h, 0:D], ALU.mult
                                                  ).then_inc(y_ready, 1)

                @block.gpsimd
                def _(pool):
                    for i in range(TPR):
                        pool.wait_ge(relu_ready, FC * (i + 1))
                        if i >= 2:
                            pool.wait_ge(kv_psum, 2 * (i - 1))
                        pool.tensor_tensor(kk[:, i % 2], rl[:, i % 2], rl[:, i % 2], ALU.mult).then_inc(kk_ready, 1)
            s.round_end()


def layer0_ffn(nc, g):
    with Scope(nc) as s:
        g.gates0, g.sel0 = s.sb("gates0", [P, NC, NB, NE]), s.sb("sel0", [P, NC, NB, NE])
        slot_tables(g, s, "l0_")
        with Scope(nc) as n:
            g.z = n.sb("l0_z", [P, NC, NB, D])
            with Scope(nc) as t:
                g.aT = t.sb("l0_aT", [P, DC, NB, SEQ])
                with Scope(nc) as v:
                    g.v = v.sb("l0_v", [P, NC, NB, 16, 16])
                    attn_project(nc, g)
                    attn_heads(nc, g)
                attn_finish(nc, g)
            with Scope(nc) as w:
                ld = TileLoads(g, w, "eg_", D, ("m0_w1", "m0_w2"))
                top2_slots(nc, g, "l0_", g.sel0[:], g.gates0[:], lambda t: g.z[:, t // NB, t % NB, :], (), D, ld)
                experts_gelu(nc, g, ld)
                top2_combine(nc, g, "l0_", ld)


def slot_tables(g, s, tag):
    g.pos, g.pw = s.sb(tag + "pos", [P, 2, NC * NB], I32), s.sb(tag + "pos_gates", [P, 2, NC * NB])
    g.tile_e = s.sb(tag + "tile_experts", [P, NT + AHEAD], I32)


def layer1_attn(nc, g):
    with Scope(nc) as s:
        g.gates1, g.sel1 = s.sb("gates1", [P, NC, NB, NE]), s.sb("sel1", [P, NC, NB, NE])
        slot_tables(g, s, "l1_")
        time_mix(nc, g)
        top2_of_softmax(nc, g)
        with Scope(nc) as n:
            e = n.sb("l1_e", [P, NC, NB, 2 * D])
            src = []
            for b in range(NB):
                for j in range(2):
                    src.append((e[:, :, b, j * D:(j + 1) * D], g.scr_e[b, j:j + SEQ].rearrange("(c p) n -> p c n", p=P)))
            ld = TileLoads(g, n, "ec_", 2 * D, ("m1_w",))
            top2_slots(nc, g, "l1_", g.sel1[:], g.gates1[:], lambda t: e[:, t // NB, t % NB, :], src, 2 * D, ld)
            experts_channel_mix(nc, g, ld)
            top2_combine(nc, g, "l1_", ld)


class Shared:
    pass


def program(nc, d, out):
    g = Shared()
    g.d = d
    with ExitStack() as ctx:
        g.ps = ctx.enter_context(nc.psum_tensor("banks", [P, 8, 512], F32))
        g.h_spare = ctx.enter_context(nc.sbuf_tensor("h_res", [P, NC + 2, NB, D], F32))
        g.h = g.h_spare[:, 1:NC + 1]
        g.ident = ctx.enter_context(nc.sbuf_tensor("ident", [P, P], F32))
        g.scr_ssm = nc.dram_tensor("scr_ssm", (NB, 256, 256), F32, kind="Internal").ap()
        g.scr_qk = nc.dram_tensor("scr_qk", (2, 3, D, NB, SEQ), BF16, kind="Internal").ap()
        g.scr_e = nc.dram_tensor("scr_e", (NB, SEQ + 1, D), F32, kind="Internal").ap()
        pad = TPR * TS * 2 * D
        g.slots = nc.dram_tensor("scr_slots", (NT * TS * 2 * D + pad,), F32, kind="Internal").ap()
        g.y_slots = nc.dram_tensor("scr_y_slots", (NT * TS, D), F32, kind="Internal").ap()
        with Scope(nc) as s:
            loaded = s.sem("const_loaded")
            with nc.Block() as block:
                @block.sync
                def _(sp):
                    sp.dma_start(g.ident[:], d["ident"]).then_inc(loaded, 16)
                    sp.wait_ge(loaded, 16)
            s.round_end()
        for stage in STAGES:
            stage(nc, g)
        with Scope(nc) as s:
            stored = s.sem("out_stored")
            with nc.Block() as block:
                @block.sync
                def _(sp):
                    for b in range(NB):
                        sp.dma_start(out[b].rearrange("(c p) n -> p c n", p=P), g.h[:, :, b, :]).then_inc(stored, 16)
                    sp.wait_ge(stored, 16 * NB)
            s.round_end()


def lay_out(**a):
    a = {k: np.ascontiguousarray(v) for k, v in a.items()}
    o = {}

    def dup(x):
        return np.concatenate([x.T, x.T], 0)

    def rep(x):
        return np.broadcast_to(np.asarray(x).reshape(1, -1), (P, np.asarray(x).size))

    def kxn(w):
        return w.reshape(-1, P, w.shape[-1]).transpose(1, 0, 2)

    o["txt"] = a["txt"]
    o["s4_ldt"] = rep(a["L0_tok_log_dt"])
    o["s4_are"], o["s4_aim"] = dup(a["L0_tok_inv_A_real"]), dup(a["L0_tok_A_imag"])
    o["s4_bre"], o["s4_bim"] = dup(a["L0_tok_B_ri"][..., 0]), dup(a["L0_tok_B_ri"][..., 1])
    for k, n in enumerate(("s4_cre", "s4_cim")):
        x = a["x"][..., k].transpose(2, 0, 1)
        o[n] = np.concatenate([x, x], 0)
    o["ident"] = np.eye(P, dtype=np.float32)
    o["identb"] = np.eye(P, dtype=np.float32).astype(mybir.dt.np(BF16))
    order = [(f * 4 + r) * 2 + j for f in range(2) for j in range(2) for r in range(4)]
    o["dn_wqk"] = np.stack([kxn(a["L0_attn_Wq"].T), kxn(a["L0_attn_Wk"].T)], 1)
    o["dn_wv"] = kxn(np.concatenate([a["L0_attn_Wv"], a["L0_attn_Wbeta"][order], a["L0_attn_Wmix"][order],
                                     a["L0_attn_Wgate"]], 0).T)
    o["dn_wout"] = kxn(a["L0_attn_Wout"].T)
    floor = np.array([np.exp(np.float32(-0.5 ** (k // 2 + 1))) for k in order], np.float32)
    o["dn_rows"] = rep(np.concatenate([a["L0_attn_bout"], a["L0_attn_ln_g"], a["L0_attn_ln_b"], a["L0_attn_bbeta"][order],
                                       a["L0_attn_bmix"][order], a["L0_attn_bgate"], floor]))
    i = np.arange(P)
    tri = (i[:, None] <= i[None, :]).astype(np.float32)
    cm = np.where(i[:, None] <= i[None, :], 0.0, -30000.0).astype(np.float32)
    bd = (i[:, None] // 32 == (np.arange(8 * 33) // 33 % 4)[None, :]).astype(np.float32)
    o["dn_masks"] = np.concatenate([tri, np.ones((P, P), np.float32), cm, bd], 1)
    sel = np.zeros((48, 16, P), np.float32)
    for k in range(48):
        sel[k, k % 16] = 1.0
    o["dn_sel"] = sel.astype(mybir.dt.np(BF16))
    extra_layouts(a, o, rep, kxn)
    return {k: np.ascontiguousarray(v) for k, v in o.items()}


def extra_layouts(a, o, rep, kxn):
    w, bias = a["L0_ffn_Wqkv"], a["L0_ffn_bqkv"]
    o["at_wqk"] = np.stack([kxn(w[:, 0:D]), kxn(w[:, D:2 * D])], 1)
    o["at_wv"] = kxn(w[:, 2 * D:])
    o["at_rows"] = rep(np.concatenate([a["L0_ffn_ln1_w"], a["L0_ffn_ln1_b"], bias[2 * D:]]))
    o["at_qkb"] = bias[0:2 * D].reshape(4, P).T
    i = np.arange(P)
    big = np.float32(-1e30)
    qm = np.where(i[None, :] <= i[:, None], np.float32(0), big)
    o["at_consts"] = np.concatenate([np.eye(P, dtype=np.float32), qm, qm.T],
                                    1).astype(mybir.dt.np(BF16))
    o["at_wo"] = kxn(a["L0_ffn_Wo"])
    o["m0_gate"] = kxn(a["L0_ffn_gate_W"])
    o["af_rows"] = rep(np.concatenate([a["L0_ffn_bo"], a["L0_ffn_ln2_w"], a["L0_ffn_ln2_b"]]))
    o["m0_b2"] = a["L0_ffn_fc2_b"]

    def by_expert(x):
        return x.reshape(NE, -1, P, x.shape[-1]).transpose(0, 2, 1, 3).reshape(NE, P, -1)
    b1 = a["L0_ffn_fc1_b"].reshape(NE, 8, P).transpose(0, 2, 1)
    o["m0_w1"] = np.concatenate([by_expert(a["L0_ffn_fc1_w"].transpose(0, 2, 1)), b1], 2)
    o["m0_w2"] = by_expert(a["L0_ffn_fc2_w"].transpose(0, 2, 1))
    o["ts_tri"] = np.concatenate([(i[:, None] < i[None, :]).astype(np.float32), np.ones((P, P), np.float32)], 1)
    o["ts_iota"] = rep(np.concatenate([TS * np.arange(NT // 2), np.arange(NT + AHEAD)]).astype(np.float32))

    o["tm_wkvr"] = np.stack([kxn(a["L1_attn_" + n]) for n in ("Wk", "Wv", "Wr")], 1)
    o["tm_wo"] = kxn(a["L1_attn_Wo"])
    o["m1_router"] = kxn(a["L1_attn_router_w"])
    o["tm_rows"] = rep(np.concatenate([a["L1_attn_" + n] for n in ("ln1_g", "ln1_b", "ln2_g", "ln2_b")]))
    o["tm_cols"] = np.stack([a["L1_attn_" + n].reshape(DC, P).T for n in (
        "tm_mu_k", "tm_mu_v", "tm_mu_r", "time_decay", "time_first")], 1)
    mu = np.stack([a["L1_attn_cm_mu_k"], a["L1_attn_cm_mu_r"]], 1)
    o["m1_w"] = np.concatenate([by_expert(a["L1_attn_eWk"]), by_expert(a["L1_attn_eWv"]), by_expert(a["L1_attn_eWr"]),
                                mu.reshape(NE, 2 * DC, P).transpose(0, 2, 1)], 2)
    o["m2_gate"] = kxn(a["L1_ffn_gate_w"].T)
    o["m2_bias"] = rep(a["L1_ffn_gate_bias"])
    gate = np.concatenate([a["L1_ffn_w_gate"], a["L1_ffn_sh_gate"].reshape(2, P, D)], 0)
    up = np.concatenate([a["L1_ffn_w_up"], a["L1_ffn_sh_up"].reshape(2, P, D)], 0)
    down = np.concatenate([a["L1_ffn_w_down"], a["L1_ffn_sh_down"].reshape(D, 2, P).transpose(1, 0, 2)], 0)

    def by_rows(x):
        return x.transpose(0, 2, 1).reshape(34, DC, P, P).transpose(0, 2, 1, 3).reshape(34, P, 2 * P)
    m2 = np.concatenate([by_rows(gate), by_rows(up), down.transpose(0, 2, 1)], 2)
    o["m2_w"] = np.concatenate([m2, m2[:6]], 0)


STAGES = [ssm_tokens, deltanet, layer0_ffn, layer1_attn, layer1_ffn]


def kernel(**inputs):
    import concourse.bacc as _bacc
    from concourse.bass_utils import run_bass_kernel_spmd as _run

    nc = _bacc.Bacc("TRN2", target_bir_lowering=False, num_devices=1)
    arrays = {"in_" + n: a for n, a in lay_out(**{k: np.asarray(v) for k, v in inputs.items()}).items()}
    d = {n[3:]: nc.dram_tensor(n, a.shape, mybir.dt.from_np(a.dtype), kind="ExternalInput").ap()
         for n, a in arrays.items()}
    out = nc.dram_tensor("out_h", (NB, SEQ, D), F32, kind="ExternalOutput").ap()
    program(nc, d, out)
    r = _run(nc, [arrays], core_ids=[0])
    return r.results[0]["out_h"]
```
